# Optimizing a Trainium2 kernel written in Bass

```python
import numpy as np
import jax
import jax.numpy as jnp

def _softmax(x, axis=-1):
    return jax.nn.softmax(x, axis=axis)

def _gelu(x):
    return jax.nn.gelu(x, approximate=True)

def _silu(x):
    return jax.nn.silu(x)

def _sigmoid(x):
    return jax.nn.sigmoid(x)

def _layernorm(x, axis=-1, eps=1e-05):
    m = jnp.mean(x, axis=axis, keepdims=True)
    v = jnp.var(x, axis=axis, keepdims=True)
    return (x - m) / jnp.sqrt(v + eps)

def _scatter_add(tgt, idx, src, axis=0):
    return tgt.at[idx].add(src)

def _segment_sum(src, seg, n):
    return jax.ops.segment_sum(src, seg, n)
kernel_name = 'mk_gps_d1_gnn_r8_240d61'

def setup_inputs(seed: int=0):
    np.random.seed(seed)
    _w = jnp.asarray

    def _rec_inputs():
        import jax
        import jax.numpy as jnp
        _gk = jax.random.key(seed)
        x = -0.0002117 + 1 * jax.random.normal(jax.random.fold_in(_gk, 1), (12500, 256), jnp.float32)
        _s = jax.random.randint(jax.random.fold_in(_gk, 2), (100000,), 0, 12500, jnp.int32)
        _d = jax.random.randint(jax.random.fold_in(_gk, 3), (100000,), 0, 12500, jnp.int32)
        _loop = jnp.arange(12500, dtype=jnp.int32)
        src = jnp.concatenate([_s, _d, _loop])
        dst = jnp.concatenate([_d, _s, _loop])
        _o = jnp.argsort(dst, stable=True)
        src = src[_o]
        dst = dst[_o]
        edge_weight = jax.random.uniform(jax.random.fold_in(_gk, 12), (212500,), jnp.float32, 0.0, 0.999998)
        return (x, src, dst, edge_weight)
    x, src, dst, edge_weight = _rec_inputs()

    def _L0_gnn_setup():
        import jax, jax.numpy as jnp
        import numpy as np
        N = 12500
        E = 37500
        D = 256

        def _mean_aggregate(x, edge_index, num_nodes):
            src, dst = (edge_index[0], edge_index[1])
            msgs = x[src]
            summed = jax.ops.segment_sum(msgs, dst, num_segments=num_nodes)
            counts = jax.ops.segment_sum(jnp.ones((edge_index.shape[1],), x.dtype), dst, num_segments=num_nodes)
            return summed / jnp.maximum(counts, 1.0)[:, None]
        key = jax.random.key(seed)
        k1, k2, k3, k4, k5, k6 = jax.random.split(key, 6)
        x = jax.random.normal(k1, (N, D), dtype=jnp.float32)
        edge_index = jax.random.randint(k2, (2, E), 0, N, dtype=jnp.int64)
        edge_weight = jax.random.uniform(k3, (E,), dtype=jnp.float32)
        lim = 1.0 / np.sqrt(D)
        W_l = jax.random.uniform(k4, (D, D), dtype=jnp.float32, minval=-lim, maxval=lim)
        b_l = jax.random.uniform(k5, (D,), dtype=jnp.float32, minval=-lim, maxval=lim)
        W_r = jax.random.uniform(k6, (D, D), dtype=jnp.float32, minval=-lim, maxval=lim)
        return {'x': x, 'edge_index': edge_index, 'edge_weight': edge_weight, 'W_l': W_l, 'b_l': b_l, 'W_r': W_r}
    _L0_gnn_all = _L0_gnn_setup()
    _L0_gnn_in = {k: v for k, v in _L0_gnn_all.items() if k in ('W_l', 'b_l', 'W_r')}
    del _L0_gnn_all

    def _L0_mix_setup():
        import jax, jax.numpy as jnp
        import numpy as np
        D_MODEL = 256
        NUM_HEADS = 8
        DEPTH = D_MODEL // NUM_HEADS
        B, L = (32, 512)

        def _feature_map(x):
            return jax.nn.elu(x) + 1.0
        key = jax.random.key(seed)
        ks = jax.random.split(key, 9)
        sc = 1.0 / np.sqrt(D_MODEL)
        return {'x': jax.random.normal(ks[0], (B, L, D_MODEL), dtype=jnp.float32), 'wq': jax.random.normal(ks[1], (D_MODEL, D_MODEL), dtype=jnp.float32) * sc, 'bq': jnp.zeros((D_MODEL,), dtype=jnp.float32), 'wk': jax.random.normal(ks[2], (D_MODEL, D_MODEL), dtype=jnp.float32) * sc, 'bk': jnp.zeros((D_MODEL,), dtype=jnp.float32), 'wv': jax.random.normal(ks[3], (D_MODEL, D_MODEL), dtype=jnp.float32) * sc, 'bv': jnp.zeros((D_MODEL,), dtype=jnp.float32), 'wo': jax.random.normal(ks[4], (D_MODEL, D_MODEL), dtype=jnp.float32) * sc, 'bo': jnp.zeros((D_MODEL,), dtype=jnp.float32)}
    _L0_mix_all = _L0_mix_setup()
    _L0_mix_in = {k: v for k, v in _L0_mix_all.items() if k in ('wq', 'bq', 'wk', 'bk', 'wv', 'bv', 'wo', 'bo')}
    del _L0_mix_all

    def _L0_ffn_setup():
        import math
        import jax, jax.numpy as jnp
        import numpy as np
        CAPACITY_FACTOR = 1.25
        TOP_K = 2
        LN_EPS = 1e-05

        def _layer_norm(x, gamma, beta):
            mu = jnp.mean(x, axis=-1, keepdims=True)
            var = jnp.var(x, axis=-1, keepdims=True)
            return (x - mu) * jax.lax.rsqrt(var + LN_EPS) * gamma + beta
        key = jax.random.key(seed)
        ks = jax.random.split(key, 4)
        B, S, D, F, E = (8, 512, 256, 512, 8)
        x = jax.random.normal(ks[0], (B, S, D), dtype=jnp.float32)
        Wr = jax.random.normal(ks[1], (D, E), dtype=jnp.float32) / np.sqrt(D)
        br = jnp.zeros((E,), jnp.float32)
        W1 = jax.random.normal(ks[2], (E, D, F), dtype=jnp.float32) / np.sqrt(D)
        b1 = jnp.zeros((E, F), jnp.float32)
        W2 = jax.random.normal(ks[3], (E, F, D), dtype=jnp.float32) / np.sqrt(F)
        b2 = jnp.zeros((E, D), jnp.float32)
        gamma = jnp.ones((D,), jnp.float32)
        beta = jnp.zeros((D,), jnp.float32)
        return {'x': x, 'Wr': Wr, 'br': br, 'W1': W1, 'b1': b1, 'W2': W2, 'b2': b2, 'gamma': gamma, 'beta': beta}
    _L0_ffn_all = _L0_ffn_setup()
    _L0_ffn_in = {k: v for k, v in _L0_ffn_all.items() if k in ('Wr', 'br', 'W1', 'b1', 'W2', 'b2', 'gamma', 'beta')}
    del _L0_ffn_all
    return {'x': x, 'src': src, 'dst': dst, 'edge_weight': edge_weight, 'L0_gnn_W_l': _L0_gnn_in['W_l'], 'L0_gnn_b_l': _L0_gnn_in['b_l'], 'L0_gnn_W_r': _L0_gnn_in['W_r'], 'L0_mix_wq': _L0_mix_in['wq'], 'L0_mix_bq': _L0_mix_in['bq'], 'L0_mix_wk': _L0_mix_in['wk'], 'L0_mix_bk': _L0_mix_in['bk'], 'L0_mix_wv': _L0_mix_in['wv'], 'L0_mix_bv': _L0_mix_in['bv'], 'L0_mix_wo': _L0_mix_in['wo'], 'L0_mix_bo': _L0_mix_in['bo'], 'L0_ffn_Wr': _L0_ffn_in['Wr'], 'L0_ffn_br': _L0_ffn_in['br'], 'L0_ffn_W1': _L0_ffn_in['W1'], 'L0_ffn_b1': _L0_ffn_in['b1'], 'L0_ffn_W2': _L0_ffn_in['W2'], 'L0_ffn_b2': _L0_ffn_in['b2'], 'L0_ffn_gamma': _L0_ffn_in['gamma'], 'L0_ffn_beta': _L0_ffn_in['beta']}

def reference(x, src, dst, edge_weight, L0_gnn_W_l, L0_gnn_b_l, L0_gnn_W_r, L0_mix_wq, L0_mix_bq, L0_mix_wk, L0_mix_bk, L0_mix_wv, L0_mix_bv, L0_mix_wo, L0_mix_bo, L0_ffn_Wr, L0_ffn_br, L0_ffn_W1, L0_ffn_b1, L0_ffn_W2, L0_ffn_b2, L0_ffn_gamma, L0_ffn_beta):
    import jax
    import jax.numpy as jnp

    def _L0_gnn_ref(x, edge_index, edge_weight, W_l, b_l, W_r):
        import jax, jax.numpy as jnp
        import numpy as np
        N = 12500
        E = 37500
        D = 256

        def _mean_aggregate(x, edge_index, num_nodes):
            src, dst = (edge_index[0], edge_index[1])
            msgs = x[src]
            summed = jax.ops.segment_sum(msgs, dst, num_segments=num_nodes)
            counts = jax.ops.segment_sum(jnp.ones((edge_index.shape[1],), x.dtype), dst, num_segments=num_nodes)
            return summed / jnp.maximum(counts, 1.0)[:, None]
        h = x
        agg = _mean_aggregate(x, edge_index, x.shape[0])
        out = agg @ W_l.T + b_l
        out = out + x @ W_r.T
        out = jax.nn.relu(out)
        return out + h

    def _L0_mix_ref(x, wq, bq, wk, bk, wv, bv, wo, bo):
        import jax, jax.numpy as jnp
        import numpy as np
        D_MODEL = 256
        NUM_HEADS = 8
        DEPTH = D_MODEL // NUM_HEADS
        B, L = (32, 512)

        def _feature_map(x):
            return jax.nn.elu(x) + 1.0
        b, l, _ = x.shape
        q = (x @ wq + bq).reshape(b, l, NUM_HEADS, DEPTH)
        k = (x @ wk + bk).reshape(b, l, NUM_HEADS, DEPTH)
        v = (x @ wv + bv).reshape(b, l, NUM_HEADS, DEPTH)
        q = _feature_map(q)
        k = _feature_map(k)
        kv = jnp.einsum('blhd,blhe->bhde', k, v)
        k_sum = jnp.sum(k, axis=1)
        qkv = jnp.einsum('blhd,bhde->blhe', q, kv)
        normalizer = jnp.einsum('blhd,bhd->blh', q, k_sum) + 1e-06
        out = qkv / normalizer[..., None]
        out = out.reshape(b, l, D_MODEL)
        return out @ wo + bo

    def _L0_ffn_ref(x, Wr, br, W1, b1, W2, b2, gamma, beta):
        import math
        import jax, jax.numpy as jnp
        import numpy as np
        CAPACITY_FACTOR = 1.25
        TOP_K = 2
        LN_EPS = 1e-05

        def _layer_norm(x, gamma, beta):
            mu = jnp.mean(x, axis=-1, keepdims=True)
            var = jnp.var(x, axis=-1, keepdims=True)
            return (x - mu) * jax.lax.rsqrt(var + LN_EPS) * gamma + beta
        B, S, D = x.shape
        E = Wr.shape[1]
        N = B * S
        K = TOP_K
        logits = jnp.mean(x, axis=1) @ Wr + br
        routing_weights = jax.nn.softmax(logits, axis=-1)
        capacity = float(math.ceil(N * CAPACITY_FACTOR / E))
        expected_loads = routing_weights.sum(axis=0) * (N / B)
        scale = jnp.where(expected_loads > capacity, capacity / expected_loads, 1.0)
        routing_weights = jax.nn.softmax(routing_weights * scale, axis=-1)
        rw_tok = jnp.broadcast_to(routing_weights[:, None, :], (B, S, E)).reshape(N, E)
        top_w, top_i = jax.lax.top_k(rw_tok, K)
        top_w = jax.nn.softmax(top_w, axis=-1)
        xf = x.reshape(N, D)
        h = jax.nn.gelu(jnp.einsum('nd,edf->enf', xf, W1) + b1[:, None, :], approximate=False)
        y = jnp.einsum('enf,efd->end', h, W2) + b2[:, None, :]
        w_dense = jnp.zeros((N, E), x.dtype).at[jnp.arange(N)[:, None], top_i].add(top_w)
        out = jnp.einsum('ne,end->nd', w_dense, y).reshape(B, S, D)
        out = _layer_norm(out + x, gamma, beta)
        return out
    edge_index = jnp.stack([src, dst])
    xn = _layernorm(x, axis=-1)
    x = x + _L0_gnn_ref(xn, edge_index, edge_weight, L0_gnn_W_l, L0_gnn_b_l, L0_gnn_W_r) + _L0_mix_ref(xn[None], L0_mix_wq, L0_mix_bq, L0_mix_wk, L0_mix_bk, L0_mix_wv, L0_mix_bv, L0_mix_wo, L0_mix_bo)[0]
    x = x + _L0_ffn_ref(_layernorm(x, axis=-1)[None], L0_ffn_Wr, L0_ffn_br, L0_ffn_W1, L0_ffn_b1, L0_ffn_W2, L0_ffn_b2, L0_ffn_gamma, L0_ffn_beta)[0]
    return x

_drawn_inputs = setup_inputs


def setup_inputs(seed=0):
    import zlib

    import numpy as np

    out = dict(_drawn_inputs(seed))
    spreads = {'L0_mix_bq': (0.0, 2.0),
     'L0_mix_bk': (0.0, 2.0),
     'L0_mix_bv': (0.0, 0.1),
     'L0_mix_bo': (0.0, 0.1),
     'L0_ffn_br': (0.0, 0.1),
     'L0_ffn_b1': (0.0, 0.564),
     'L0_ffn_b2': (0.0, 0.379),
     'L0_ffn_gamma': (1.0, 0.2),
     'L0_ffn_beta': (0.0, 0.1)}
    factors = {'L0_gnn_b_l': 4.605,
     'L0_mix_wq': 8.0,
     'L0_mix_wk': 8.0,
     'L0_mix_wv': 8.0,
     'L0_ffn_Wr': 8.0}
    for name, (base, spread) in spreads.items():
        noise = np.random.default_rng([zlib.crc32(name.encode()), seed]).standard_normal(out[name].shape)
        drawn = base * np.exp(spread * noise) if base else spread * noise
        out[name] = jnp.asarray(drawn.astype(out[name].dtype))
    for name, factor in factors.items():
        out[name] = (out[name] * factor).astype(out[name].dtype)
    return out
```

```python
import math
from contextlib import ExitStack

import concourse.bass as bass
from concourse import mybir

F32 = mybir.dt.float32
BF16 = mybir.dt.bfloat16
I32 = mybir.dt.int32
ALU = mybir.AluOpType
ACT = mybir.ActivationFunctionType
AX = mybir.AxisListType

P = 128
EPS = 1e-5


def wait(eng, sem, value):
    if not (isinstance(value, int) and value <= 0):
        eng.wait_ge(sem, value)


def build_layer(nc, x, src, dst, W_l, b_l, W_r, wq, bq, wk, bk, wv, bv, wo, bo,
                Wr, br, W1, b1, W2, b2, gamma, beta, out):
    N, D = x.shape
    E = src.shape[0]
    NE, _, F = W1.shape
    C = D // P
    HD = D // 8
    FC = F // P
    NF = 2 * FC
    QT = 4
    QR = QT * P
    NQ = N // QR
    TAIL = N - NQ * QR
    TAILS = [min(P, TAIL - P * s) for s in range(math.ceil(TAIL / P))]
    BN = 2 * P
    NB = math.ceil(N / BN)
    ET = math.ceil(E / P)
    TB = 34
    LAST = ET - (NB - 1) * TB
    NCH = math.ceil(ET / P)
    TCOLS = NB * TB
    BATCH = [(0, 9), (9, 17), (17, 26), (26, 34)]
    OSLOT = [0, 9, 0, 9]
    WIN = P
    LO = [15 * (k // 2) + 7 * (k % 2) - 60 for k in range(TB)]
    CAP = float(math.ceil(N * 1.25 / NE))
    GW = D + 4
    GT = math.ceil(N / P)
    assert TAIL > 0 and len(TAILS) == 2 and NQ % 2 == 0 and NB % 2 == 1 and BN * (NB - 1) == NQ * QR

    xn_table = nc.dram_tensor("xn_table", (N, D), F32).ap()
    y_rows = nc.dram_tensor("y_rows", (N, D), F32).ap()
    x1_rows = nc.dram_tensor("x1_rows", (N, D), F32).ap()
    sum_rows = nc.dram_tensor("sum_rows", ((GT + 1) * P, GW), F32).ap()

    with ExitStack() as ctx:
        def sb(name, shape, dtype=F32):
            return ctx.enter_context(nc.sbuf_tensor(name, shape, dtype))

        def sem(name):
            return ctx.enter_context(nc.semaphore(name))

        yT = sb("yT", [P, NB * C * BN])
        edges = sb("edges", [P, 2 * TCOLS])
        mats = sb("mats", [P, 6 * C * D])
        ring = sb("ring", [P, TB * D])
        ohf = sb("ohf", [P, 17 * WIN])
        ohh = sb("ohh", [P, 17 * WIN], BF16)
        work = sb("work", [P, 9 * 512])
        b1k_b = sb("b1k_b", [P, D])
        bl_b, bo_b, gamma_b, beta_b = sb("bl_b", [P, D]), sb("bo_b", [P, D]), sb("gamma_b", [P, D]), sb("beta_b", [P, D])
        M_s, KS_s = sb("M_s", [P, C, D]), sb("KS_s", [P, C, P])
        Wr_s = sb("Wr_s", [P, C, NE])
        bq_c, bq1_c = sb("bq_c", [P, C]), sb("bq1_c", [P, C])
        bv_r, br_r = sb("bv_r", [1, D]), sb("br_r", [1, NE])
        ident, mask, ones = sb("ident", [P, P]), sb("mask", [P, P]), sb("ones", [P, P])
        ones_h = sb("ones_h", [P, P], BF16)
        iota_i, iota_f, iota_h = sb("iota_i", [P, WIN], I32), sb("iota_f", [P, WIN]), sb("iota_h", [P, WIN], BF16)
        zeros = sb("zeros", [P, GW])
        rstd_a, nmr_a = sb("rstd_a", [P, (NQ + 1) * QT]), sb("nmr_a", [P, (NQ + 1) * QT])
        ysum = sb("ysum", [P, C, NB])
        flag = sb("flag", [1, 1], I32)
        cntp = sb("cntp", [P, 1])
        idxb = sb("idxb", [P, TB], I32)
        mv, bst = sb("mv", [P, QT, 2]), sb("bst", [P, QT, 6])
        rstd2, nmr2 = sb("rstd2", [P, QT]), sb("nmr2", [P, QT])
        rc = sb("rc", [P, BN])
        rt = sb("rt", [1, 16, NE])
        ysr, mean_c = sb("ysr", [P, C]), sb("mean_c", [P, C])
        gates, gate_b, pick = sb("gates", [1, 2]), sb("gate_b", [P, 2]), sb("pick", [1, 2], I32)
        b1_c = sb("b1_c", [P, 2, FC])

        idx = edges[:, 0:TCOLS].bitcast(I32)
        rel = edges[:, TCOLS:2 * TCOLS]

        def mat(n):
            return mats[:, n * C * D:(n + 1) * C * D].rearrange("p (c d) -> p c d", c=C)
        wk_s, wq_s, wv_s, wo_s, wlT, wrT = (mat(n) for n in range(6))
        msgs = ring[:, :].rearrange("p (k d) -> p k d", d=D)
        oh = ohf[:, :].rearrange("p (k w) -> p k w", w=WIN)
        ohc = ohh[:, :].rearrange("p (k w) -> p k w", w=WIN)

        at = {"yT": 8 * C * BN, "ring": 0}

        def early(n, whole="yT"):
            at[whole] += n
            return (yT if whole == "yT" else ring)[:, at[whole] - n:at[whole]]
        KXW = D + 1
        xin = [early(QT * D).rearrange("p (s d) -> p s d", d=D) for _ in range(2)]
        xnb = [early(QT * KXW).rearrange("p (s d) -> p s d", d=KXW) for _ in range(2)]
        xTb = [early(C * QR).rearrange("p (c t) -> p c t", c=C) for _ in range(2)]
        kb1 = [early(2 * D) for _ in range(2)]
        ek = [early(2 * D) for _ in range(2)]
        phi = early(QT * D).rearrange("p (s d) -> p s d", d=D)
        kx_s = early(C * KXW).rearrange("p (c d) -> p c d", c=C)
        kxT = early(C * D).rearrange("p (c d) -> p c d", c=C)
        ks_r = early(D)[0:1, :]
        kvT = early(C * P).rearrange("p (c d) -> p c d", c=C)
        raw = early(NCH * P).bitcast(I32).rearrange("p (c e) -> p c e", e=P)
        rawf = early(NCH * P).rearrange("p (c e) -> p c e", e=P)
        offs = early(TCOLS).bitcast(I32)
        inside = [early(TCOLS) for _ in range(2)]
        wraw = [early(C * D).rearrange("p (c d) -> p c d", c=C) for _ in range(2)]
        g_row = early(GW, "ring")
        g_src = early(1, "ring").bitcast(I32)
        g_dst = early(1, "ring")
        g_dsts = early(P, "ring")
        g_same = early(P, "ring")
        g_before = early(P, "ring")
        g_later = early(P, "ring")
        g_dup, g_pad, g_dup2, g_gap, g_dump = (early(1, "ring") for _ in range(5))
        g_dump_i, g_to = early(1, "ring").bitcast(I32), early(1, "ring").bitcast(I32)
        g_sum = early(GW, "ring")
        g_back = early(GW, "ring")
        g_cnt = early(1, "ring")
        g_mean = early(D, "ring")
        g_node_i, g_node = early(NB, "ring").bitcast(I32), early(NB, "ring")
        g_p, g_ra, g_rb, g_rc = (early(1, "ring") for _ in range(4))
        assert at["yT"] <= NB * C * BN and at["ring"] <= TB * D

        xr, xn2, xT2, pq, qb, aggS, r0, x1, yr = (work[:, n * 512:(n + 1) * 512] for n in range(9))
        hT = [ring[:, u * NF * QR:(u + 1) * NF * QR].rearrange("p (f t) -> p f t", f=NF) for u in range(2)]
        W1_s = mats[:, 0:2 * C * F].rearrange("p (e c f) -> p e c f", e=2, c=C)
        W2_s = ohf[:, 0:NF * D].rearrange("p (f d) -> p f d", d=D)
        W2_r = edges[:, 0:NF * D].rearrange("p (f d) -> p f d", d=D)
        z = [t.rearrange("p (s d) -> p s d", d=D)
             for t in (mats[:, 2 * C * F:2 * C * F + QT * D], edges[:, NF * D:NF * D + QT * D])]
        b2_b = ohh[:, 0:4 * D].bitcast(F32).rearrange("p (e d) -> p e d", e=2)
        b2a = ohh[:, 4 * D:6 * D].bitcast(F32)
        b2m = ohh[:, 6 * D:8 * D].bitcast(F32)
        y_in = [work[:, u * QT * D:(u + 1) * QT * D].rearrange("p (s d) -> p s d", d=D) for u in range(2)]
        x1_in = [work[:, (2 + u) * QT * D:(3 + u) * QT * D].rearrange("p (s d) -> p s d", d=D) for u in range(2)]

        pa = ctx.enter_context(nc.psum_tensor("pa", [P, 2, 512], F32))
        pc = ctx.enter_context(nc.psum_tensor("pc", [P, 2, 512], F32))
        pd = ctx.enter_context(nc.psum_tensor("pd", [P, 4, 512], F32))

        names = """stats_read batch_started iota_set iota_float mask_step wk_loaded consts_set ident_set raw_padded raw_loaded raw_float raw_turned raw_taken
            flag_a flag_b flag_sum flag_added flag_set w_loaded wlr_turned wlr_taken bias1_set
            x_loaded0 x_loaded1 p1_bn p1_mv p1_rstd p1_stats xn_ready xn_stored0 xn_stored1 xt_turned xt_a xt_d
            k_made kb_made ek_made phi_made kx_done kx_taken kxT_made kxT_taken kv_made kv_taken m_made m_taken
            idx_ready gathered0 gathered1 gathered2 gathered3 oh_ready batch_used agg_done agg_taken
            xr_loaded xn2_ready xt2_turned xt2_ready q_made eq_made phq_made nrm_made nrm_eps nrm_rec qhat_made
            cnt_max cnt_rec r0_made r0b_made o_made g1_made x1a_made x1_made d_bn d_mv d_rstd d_stats
            y_made yt_turned yt_ready x1_stored y_stored
            route_step route_exp logits_made ysum_made mean_made picked gates_made gates_spread gates_taken
            experts_loaded w2_scaled b2_step b2_made yin_loaded0 yin_loaded1 yb_made xb_made
            h_made h_act o5_made z_made f_bn f_mv f_rstd f_stats zn_made f_scaled fin_made out_stored0 out_stored1
            g_iota g_zeroed g_src_set g_loaded g_to_made g_taken g_added g_back_loaded g_mean_made g_mean_stored
            g_replaced g_done g_dsts_made g_turned g_same_made g_summed g_consts g_tests g_dup_made g_dup2_made
            g_cnt_made g_rec_made g_index""".split()
        s = {n: sem(n) for n in names}

        def quad_rows(table, q):
            return table[bass.ds(q * QR, QR), :].rearrange("(s p) d -> p s d", p=P)

        def quad_io(eng, table, tile, q, signal, store):
            if isinstance(q, int) and q == NQ:
                pairs = [(tile[0:n, t, 0:D], table[q * QR + t * P:q * QR + t * P + n, :]) for t, n in enumerate(TAILS)]
            else:
                pairs = [(tile[:, :, 0:D], quad_rows(table, q))]
            for a, b in pairs:
                (eng.dma_start(b, a) if store else eng.dma_start(a, b)).then_inc(signal, 16)

        def quad_dmas(q, u):
            if isinstance(q, int) and q == NQ:
                return 16 * (NQ // 2 + len(TAILS))
            return (q - u) * 8 + 16

        def block_io(eng, table, tile, d, signal, store):
            t3 = tile.rearrange("p (s d) -> p s d", d=D)
            if isinstance(d, int) and d == NB - 1:
                pairs = [(t3[0:n, t, :], table[d * BN + t * P:d * BN + t * P + n, :]) for t, n in enumerate(TAILS)]
            else:
                pairs = [(t3, table[bass.ds(d * BN, BN), :].rearrange("(s p) d -> p s d", p=P))]
            for a, b in pairs:
                (eng.dma_start(b, a) if store else eng.dma_start(a, b)).then_inc(signal, 16)

        def block_dmas(d):
            return 16 * (d + len(TAILS)) if isinstance(d, int) and d == NB - 1 else 16 * (d + 1)

        def over_quads(eng, body, between=None):
            body(0, 0)
            body(1, 1)
            if between:
                between()
            with eng.Fori(1, NQ // 2 - 1) as i:
                body(2 * i, 0)
                body(2 * i + 1, 1)
            for q in range(NQ - 2, NQ + 1):
                body(q, q % 2)

        def over_blocks(eng, body):
            body(0, 0)
            with eng.Fori(0, (NB - 3) // 2) as i:
                body(2 * i + 1, 1)
                body(2 * i + 2, 0)
            for b in range(NB - 2, NB + 1):
                body(b, b % 2)

        def batch_tiles(b, q):
            k0, k1 = BATCH[q]
            return range(k0, min(k1, LAST) if isinstance(b, int) and b == NB - 1 else k1)

        def batch_gathers(b, q):
            k0, k1 = BATCH[q]
            if isinstance(b, int) and b == NB - 1:
                return 16 * ((k1 - k0) * b + len(batch_tiles(b, q)))
            return 16 * (k1 - k0) * (b + 1)

        def is_int(v, n):
            return isinstance(v, int) and v == n

        minus1 = sb("minus1", [P, 1])
        nv, nh, ny = sb("nv", [P, QT]), sb("nh", [P, QT]), sb("ny", [P, QT])
        NEWTON = 4
        RSQRT_STEPS = 3 + 3 * NEWTON
        (R_LG, R_E1, R_RW, R_E2, R_W, R_T, R_W2, R_IO, R_MX1, R_S1, R_MX2, R_S2, R_M, R_I, R_G, R_U) = range(16)
        ROUTE_EXP = (3, 7, 21)
        W_LOADS = 16 * 13
        NG = math.ceil(NCH / 4)

        def hbank(f):
            return (pa if f % 4 < 2 else pc)[:, f % 2, :]

        def bc(v, n):
            return v.unsqueeze(1).to_broadcast([P, n, v.shape[1]])

        def pair(v):
            return v.rearrange("p (a d) -> p a d", a=2)

        def if_general(eng, program):
            eng.wait_ge(s["flag_set"], 1)
            bad = eng.value_load(flag[0:1, 0:1], min_val=0, max_val=1)
            with eng.If(bad):
                if program:
                    program(eng)
                eng.wait_ge(s["g_done"], 1)

        TILE_A, TILE_B, TILE_C = LO.index(0), 25, 26
        assert LO[TILE_B] == P - 1 and LO[TILE_C] > P - 1 and TILE_C < min(LAST, TB)

        general_sp = None

        def general_pool(pool):
            pool.iota(g_dump_i, pattern=[[0, 1]], base=GT * P, channel_multiplier=1).then_inc(s["g_iota"], 1)
            pool.iota(g_node_i, pattern=[[BN, NB]], base=0, channel_multiplier=1).then_inc(s["g_iota"], 1)
            pool.affine_select(out=g_later, in_=ones[:, :], compare_op=ALU.is_gt, fill=0.0, base=0,
                               pattern=[[-1, P]], channel_multiplier=1).then_inc(s["g_iota"], 1)
            with pool.Fori(0, GT + 1) as t:
                pool.dma_start(sum_rows[bass.ds(t * P, P), :], zeros[:, :]).then_inc(s["g_zeroed"], 16)
            pool.wait_ge(s["g_zeroed"], 16 * (GT + 1))
            with pool.Fori(0, ET) as t:
                pool.wait_ge(s["g_src_set"], t + 1)
                pool.sem_inc(s["batch_started"], 1)
                pool.indirect_dma_start(out=g_row[:, 0:D], out_offset=None, in_=xn_table[:, :],
                                        in_offset=bass.IndirectOffsetOnAxis(ap=g_src, axis=0))\
                    .then_inc(s["g_loaded"], 16)
                pool.wait_ge(s["g_to_made"], t + 1)
                pool.wait_ge(s["g_taken"], t + 1)
                pool.sem_inc(s["batch_started"], 1)
                pool.indirect_dma_start(out=sum_rows[:, :], out_offset=bass.IndirectOffsetOnAxis(ap=g_to, axis=0),
                                        in_=g_sum, in_offset=None, compute_op=ALU.add).then_inc(s["g_added"], 16)
                pool.wait_ge(s["g_added"], 16 * t + 16)
            with pool.Fori(0, GT - 1) as t:
                pool.dma_start(g_back, sum_rows[bass.ds(t * P, P), :]).then_inc(s["g_back_loaded"], 16)
                pool.wait_ge(s["g_mean_made"], t + 1)
                pool.dma_start(xn_table[bass.ds(t * P, P), :], g_mean).then_inc(s["g_mean_stored"], 16)
                pool.wait_ge(s["g_mean_stored"], 16 * t + 16)
            n = N - (GT - 1) * P
            pool.dma_start(g_back, sum_rows[(GT - 1) * P:GT * P, :]).then_inc(s["g_back_loaded"], 16)
            pool.wait_ge(s["g_mean_made"], GT)
            pool.dma_start(xn_table[(GT - 1) * P:N, :], g_mean[0:n, :]).then_inc(s["g_mean_stored"], 16)
            pool.wait_ge(s["g_mean_stored"], 16 * GT)
            pool.wait_ge(s["g_replaced"], 1)
            pool.sem_inc(s["g_done"], 1)

        def general_pe(pe):
            with pe.Fori(0, ET) as t:
                pe.wait_ge(s["g_dsts_made"], t + 1)
                nc.tensor.transpose(pa[:, 0, 0:P], g_dsts, ident[:, :]).then_inc(s["g_turned"], 1)
                pe.wait_ge(s["g_same_made"], t + 1)
                pe.wait_ge(s["g_loaded"], 16 * t + 16)
                nc.tensor.matmul(pa[:, 1, 0:GW], g_same, g_row, start=True, stop=True).then_inc(s["g_summed"], 1)

        def general_dve(dve):
            V = nc.vector
            dve.wait_ge(s["g_iota"], 3)
            V.tensor_copy(g_dump, g_dump_i)
            V.memset(g_row[:, D:GW], 0.0).then_inc(s["g_consts"], 1)
            dve.wait_ge(s["g_consts"], 1)
            V.memset(g_row[:, D:D + 1], 1.0).then_inc(s["g_consts"], 1)
            dve.wait_ge(s["g_consts"], 2)
            with dve.Fori(0, ET) as t:
                V.tensor_tensor(g_dst, rel[:, bass.ds(t, 1)], offs[:, bass.ds(t, 1)], ALU.add)
                V.tensor_copy(g_src, idx[:, bass.ds(t, 1)]).then_inc(s["g_src_set"], 1)
                dve.wait_ge(s["g_src_set"], t + 1)
                V.tensor_copy(g_dsts, g_dst.to_broadcast([P, P])).then_inc(s["g_dsts_made"], 1)
                dve.wait_ge(s["g_turned"], t + 1)
                V.tensor_scalar(g_same, pa[:, 0, 0:P], g_dst, None, ALU.is_equal).then_inc(s["g_same_made"], 1)
                dve.wait_ge(s["g_same_made"], t + 1)
                V.tensor_tensor(g_before, g_same, g_later, ALU.mult)
                V.tensor_scalar(g_pad, g_dst, 0.0, None, ALU.is_lt)
                V.tensor_tensor(g_gap, g_dump, g_dst, ALU.subtract).then_inc(s["g_tests"], 1)
                dve.wait_ge(s["g_tests"], t + 1)
                V.tensor_reduce(g_dup, g_before, AX.X, ALU.max).then_inc(s["g_dup_made"], 1)
                dve.wait_ge(s["g_dup_made"], t + 1)
                V.tensor_tensor(g_dup2, g_dup, g_pad, ALU.max).then_inc(s["g_dup2_made"], 1)
                dve.wait_ge(s["g_dup2_made"], t + 1)
                V.scalar_tensor_tensor(out=g_to, in0=g_gap, scalar=g_dup2, in1=g_dst, op0=ALU.mult, op1=ALU.add)\
                    .then_inc(s["g_to_made"], 1)
                dve.wait_ge(s["g_summed"], t + 1)
                V.tensor_copy(g_sum, pa[:, 1, 0:GW]).then_inc(s["g_taken"], 1)
                dve.wait_ge(s["g_added"], 16 * t + 16)
            with dve.Fori(0, GT) as t:
                dve.wait_ge(s["g_back_loaded"], 16 * t + 16)
                V.tensor_scalar(g_cnt, g_back[:, D:D + 1], 1.0, None, ALU.max).then_inc(s["g_cnt_made"], 1)
                dve.wait_ge(s["g_cnt_made"], t + 1)
                V.reciprocal(g_cnt, g_cnt).then_inc(s["g_rec_made"], 1)
                dve.wait_ge(s["g_rec_made"], t + 1)
                V.tensor_scalar(g_mean, g_back[:, 0:D], g_cnt, None, ALU.mult).then_inc(s["g_mean_made"], 1)
                dve.wait_ge(s["g_mean_made"], t + 1)
                dve.wait_ge(s["g_mean_stored"], 16 * t + 16)
            idx3, rel3 = (v.rearrange("p (b k) -> p b k", k=TB) for v in (idx, rel))
            V.memset(idx, 0)
            V.memset(rel, -1.0)
            V.tensor_scalar(g_p, g_dump, float(GT * P), None, ALU.subtract)
            V.tensor_copy(g_node, g_node_i).then_inc(s["g_index"], 1)
            dve.wait_ge(s["g_index"], 1)
            V.tensor_scalar(idx3[:, :, TILE_A], g_node, N - 1.0, None, ALU.min)
            V.tensor_scalar(idx3[:, :, TILE_B], g_node, float(P), N - 1.0, ALU.add, ALU.min)
            V.tensor_scalar(idx3[:, :, TILE_C], g_node, float(P), N - 1.0, ALU.add, ALU.min)
            V.tensor_scalar(g_ra, g_p, P - 1.0, None, ALU.is_lt)
            V.tensor_scalar(g_rc, g_p, P - 1.0, BN - LO[TILE_C], ALU.is_equal, ALU.mult)
            V.tensor_scalar(g_rb, g_p, 2.0, None, ALU.add).then_inc(s["g_index"], 1)
            dve.wait_ge(s["g_index"], 2)
            V.tensor_scalar(g_rc, g_rc, -1.0, None, ALU.add)
            V.tensor_tensor(g_rb, g_rb, g_ra, ALU.mult).then_inc(s["g_index"], 1)
            dve.wait_ge(s["g_index"], 3)
            V.tensor_scalar(g_rb, g_rb, -1.0, None, ALU.add).then_inc(s["g_index"], 1)
            dve.wait_ge(s["g_index"], 4)
            for tile, v in ((TILE_A, g_p), (TILE_B, g_rb), (TILE_C, g_rc)):
                ins = V.tensor_copy(rel3[:, :, tile], v.to_broadcast([P, NB]))
            ins.then_inc(s["g_replaced"], 1)
            dve.wait_ge(s["g_replaced"], 1)


        block = ctx.enter_context(nc.Block())

        @block.sync
        def _(sp):
            def edge_list(lst):
                full, rest = (NCH - 1) * P, ET - (NCH - 1) * P
                sp.dma_start(raw[:, 0:NCH - 1, :], lst[0:full * P].rearrange("(c p e) -> p c e", p=P, e=P))\
                    .then_inc(s["raw_loaded"], 16)
                sp.dma_start(raw[0:rest - 1, NCH - 1, :], lst[full * P:(ET - 1) * P].rearrange("(p e) -> p e", e=P))\
                    .then_inc(s["raw_loaded"], 16)
                sp.dma_start(raw[rest - 1:rest, NCH - 1, 0:E - (ET - 1) * P],
                             lst[(ET - 1) * P:E].rearrange("(a e) -> a e", a=1)).then_inc(s["raw_loaded"], 16)

            quad_io(sp, x, xin[0], 0, s["x_loaded0"], False)
            quad_io(sp, x, xin[1], 1, s["x_loaded1"], False)
            sp.wait_ge(s["raw_padded"], 1)
            edge_list(dst)

            def stage1(q, u):
                sp.wait_ge(s["xn_ready"], q + 1)
                quad_io(sp, xn_table, xnb[u], q, s[f"xn_stored{u}"], True)
                if not (isinstance(q, int) and q + 2 > NQ):
                    quad_io(sp, x, xin[u], q + 2, s[f"x_loaded{u}"], False)

            def src_list():
                sp.wait_ge(s["raw_padded"], 2)
                edge_list(src)
            over_quads(sp, stage1, src_list)

            if_general(sp, general_sp)

            def stage3(b, u):
                if is_int(b, 0):
                    block_io(sp, x, xr, 0, s["xr_loaded"], False)
                    return
                d = b - 1
                sp.wait_ge(s["r0_made"], d + 1)
                if not is_int(b, NB):
                    block_io(sp, x, xr, b, s["xr_loaded"], False)
                sp.wait_ge(s["x1_made"], d + 1)
                block_io(sp, x1_rows, x1, d, s["x1_stored"], True)
                sp.wait_ge(s["y_made"], d + 1)
                block_io(sp, y_rows, yr, d, s["y_stored"], True)
            over_blocks(sp, stage3)

            sp.wait_ge(s["picked"], 1)
            for n in range(2):
                e = sp.value_load(pick[0:1, n:n + 1], min_val=0, max_val=NE - 1)
                sp.dma_start(W1_s[:, n, :, :], W1[bass.ds(e, 1), :, :].rearrange("a (c p) f -> p (a c) f", p=P))\
                    .then_inc(s["experts_loaded"], 16)
                sp.dma_start(W2_r[:, n * FC:(n + 1) * FC, :],
                             W2[bass.ds(e, 1), :, :].rearrange("a (c p) d -> p (a c) d", p=P))\
                    .then_inc(s["experts_loaded"], 16)
                sp.dma_start(b1_c[:, n, :], b1[bass.ds(e, 1), :].rearrange("a (c p) -> p (a c)", p=P),
                             allow_slow_non_contiguous=True)\
                    .then_inc(s["experts_loaded"], 16)
                sp.dma_start(b2_b[:, n, :], b2[bass.ds(e, 1), :].rearrange("a d -> (a d)").partition_broadcast(P))\
                    .then_inc(s["experts_loaded"], 16)
            sp.wait_ge(s["x1_stored"], block_dmas(NB - 1))
            sp.wait_ge(s["y_stored"], block_dmas(NB - 1))

            def stage5(q, u):
                if is_int(q, 0):
                    for v in range(2):
                        quad_io(sp, y_rows, y_in[v], v, s[f"yin_loaded{v}"], False)
                        quad_io(sp, x1_rows, x1_in[v], v, s[f"yin_loaded{v}"], False)
                sp.wait_ge(s["fin_made"], q + 1)
                quad_io(sp, out, x1_in[u], q, s[f"out_stored{u}"], True)
                if not (isinstance(q, int) and q + 2 > NQ):
                    quad_io(sp, y_rows, y_in[u], q + 2, s[f"yin_loaded{u}"], False)
                    sp.wait_ge(s[f"out_stored{u}"], quad_dmas(q, u))
                    quad_io(sp, x1_rows, x1_in[u], q + 2, s[f"yin_loaded{u}"], False)
            over_quads(sp, stage5)
            for u in range(2):
                sp.wait_ge(s[f"out_stored{u}"], quad_dmas(NQ - 1 + (u == 0), u))

        @block.gpsimd
        def _(pool):
            pool.iota(iota_i[:, :], pattern=[[1, WIN]], base=0, channel_multiplier=0).then_inc(s["iota_set"], 1)
            pool.iota(offs[:, :], pattern=[[BN, NB], [15, TB // 2], [7, 2]], base=LO[0], channel_multiplier=0)\
                .then_inc(s["iota_set"], 1)
            pool.memset(ident[:, :], 0.0).then_inc(s["ident_set"], 1)
            pool.wait_ge(s["ident_set"], 1)
            pool.affine_select(out=ident[:, :], in_=ident[:, :], compare_op=ALU.not_equal, fill=1.0, base=0,
                               pattern=[[-1, P]], channel_multiplier=1).then_inc(s["ident_set"], 1)
            for t, m in ((wq_s, wq), (wv_s, wv), (wo_s, wo), (wraw[0], W_l), (wraw[1], W_r), (Wr_s, Wr)):
                pool.dma_start(t[:, :, :], m.rearrange("(c p) n -> p c n", p=P)).then_inc(s["w_loaded"], 16)
            for t, v in ((bl_b, b_l), (bo_b, bo), (gamma_b, gamma), (beta_b, beta)):
                pool.dma_start(t[:, :], v.partition_broadcast(P)).then_inc(s["w_loaded"], 16)
            for t, v in ((bv_r, bv), (br_r, br)):
                pool.dma_start(t[:, :], v.rearrange("(a n) -> a n", a=1)).then_inc(s["w_loaded"], 16)
            pool.dma_start(bq_c[:, :], bq.rearrange("(c p) -> p c", p=P), allow_slow_non_contiguous=True)\
                .then_inc(s["w_loaded"], 16)

            pool.wait_ge(s["xn_stored0"], quad_dmas(NQ, 0))
            pool.wait_ge(s["xn_stored1"], quad_dmas(NQ - 1, 1))
            if_general(pool, general_pool)

            def stage3(b, u):
                if is_int(b, NB):
                    return
                for q in range(4):
                    pool.wait_ge(s["idx_ready"], 4 * b + q + 1)
                    wait(pool, s["batch_used"], 4 * b + q - 3)
                    pool.sem_inc(s["batch_started"], 1)
                    for k in batch_tiles(b, q):
                        pool.indirect_dma_start(
                            out=msgs[:, k, :], out_offset=None, in_=xn_table[:, :],
                            in_offset=bass.IndirectOffsetOnAxis(ap=idxb[:, k:k + 1], axis=0))\
                            .then_inc(s[f"gathered{q}"], 16)
            over_blocks(pool, stage3)

            def stage5(q, u):
                tail = is_int(q, NQ)
                n = len(TAILS) if tail else QT
                pool.wait_ge(s[f"yin_loaded{u}"], 2 * quad_dmas(q, u))
                if is_int(q, 0):
                    pool.wait_ge(s["b2_made"], 1)
                pool.tensor_tensor(y_in[u][:, 0:n, :], y_in[u][:, 0:n, :],
                                   b2m[:, :].unsqueeze(1).to_broadcast([P, n, D]), ALU.add).then_inc(s["yb_made"], 1)
                pool.tensor_tensor(x1_in[u][:, 0:n, :], x1_in[u][:, 0:n, :],
                                   beta_b[:, :].unsqueeze(1).to_broadcast([P, n, D]), ALU.add)\
                    .then_inc(s["xb_made"], 1)
            over_quads(pool, stage5)

        @block.scalar
        def _(act):
            def exp_keys(q, u):
                for pr in range(1 if is_int(q, NQ) else 2):
                    act.wait_ge(s["kb_made"], 2 * q + pr + 1)
                    nc.scalar.activation(ek[pr], kb1[pr], ACT.Exp, bias=minus1[:, :]).then_inc(s["ek_made"], 1)

            def stage1(q, u):
                tiles = list(enumerate(TAILS)) if is_int(q, NQ) else [(t, P) for t in range(QT)]
                act.wait_ge(s["p1_stats"], q + 1)
                if not (isinstance(q, int) and q < 2):
                    act.wait_ge(s[f"xn_stored{u}"], quad_dmas(q - 2, u))
                    act.wait_ge(s["kx_done"], q - 1)
                for t, n in tiles:
                    col = q * QT + t
                    ins = nc.scalar.activation(xnb[u][0:n, t, 0:D], xin[u][0:n, t, :], ACT.Identity,
                                               bias=nmr_a[0:n, bass.ds(col, 1)], scale=rstd_a[0:n, bass.ds(col, 1)])
                ins.then_inc(s["xn_ready"], 1)
                if not is_int(q, 0):
                    exp_keys(q - 1, 1 - u)
                act.wait_ge(s["xt_turned"], q + 1)
                w = TAIL if is_int(q, NQ) else QR
                nc.scalar.activation(xTb[u][:, 0, 0:w], pd[:, 0, 0:w], ACT.Copy).then_inc(s["xt_a"], 1)

            act.dma_start(wk_s[:, :, :], wk.rearrange("(c p) n -> p c n", p=P)).then_inc(s["wk_loaded"], 16)
            act.dma_start(b1k_b[:, :], bk.partition_broadcast(P)).then_inc(s["wk_loaded"], 16)
            act.wait_ge(s["consts_set"], 1)
            over_quads(act, stage1)
            exp_keys(NQ, 0)

            def indices(b, q):
                ks = batch_tiles(b, q)
                if not ks:
                    return
                if not is_int(b, 0):
                    act.wait_ge(s[f"gathered{q}"], batch_gathers(b - 1, q))
                nc.scalar.activation(idxb[:, ks[0]:ks[-1] + 1], idx[:, bass.ds(b * TB + ks[0], len(ks))], ACT.Copy)\
                    .then_inc(s["idx_ready"], 1)

            if_general(act, None)
            act.wait_ge(s["raw_taken"], 2 * math.ceil(NCH / 4))
            for q in range(4):
                indices(0, q)

            def stage3(b, u):
                if is_int(b, 0):
                    for q in range(4):
                        indices(1, q)
                    return
                d = b - 1
                tail = is_int(d, NB - 1)
                rows = list(enumerate(TAILS)) if tail else [(0, P), (1, P)]
                more = not (isinstance(b, int) and b + 1 >= NB)
                act.wait_ge(s["xr_loaded"], block_dmas(d))
                wait(act, s["r0_made"], d)
                for t, n in rows:
                    col = d * 2 + t
                    ins = nc.scalar.activation(xn2[0:n, t * D:(t + 1) * D], xr[0:n, t * D:(t + 1) * D], ACT.Identity,
                                               bias=nmr_a[0:n, bass.ds(col, 1)], scale=rstd_a[0:n, bass.ds(col, 1)])
                ins.then_inc(s["xn2_ready"], 1)
                act.wait_ge(s["xt2_turned"], d + 1)
                w = TAIL if tail else BN
                nc.scalar.activation(pair(xT2)[:, :, 0:w], pair(pd[:, 0, :])[:, :, 0:w], ACT.Copy)\
                    .then_inc(s["xt2_ready"], 1)
                if more:
                    indices(b + 1, 0)
                act.wait_ge(s["q_made"], d + 1)
                wait(act, s["qhat_made"], d)
                wait(act, s["o_made"], d)
                for c in range(C):
                    nc.scalar.activation(pq[:, c * BN:(c + 1) * BN], pd[:, 1, c * BN:(c + 1) * BN], ACT.Exp,
                                         bias=bq_c[:, c:c + 1])
                for c in range(C):
                    ins = nc.scalar.activation(qb[:, c * BN:(c + 1) * BN], pd[:, 1, c * BN:(c + 1) * BN],
                                               ACT.Identity, bias=bq1_c[:, c:c + 1])
                ins.then_inc(s["eq_made"], 1)
                if more:
                    indices(b + 1, 1)
                act.wait_ge(s["d_stats"], d + 1)
                wait(act, s["y_stored"], 16 * d)
                wait(act, s["yt_turned"], d)
                for t, n in rows:
                    ins = nc.scalar.activation(yr[0:n, t * D:(t + 1) * D], x1[0:n, t * D:(t + 1) * D], ACT.Identity,
                                               bias=nmr2[0:n, t:t + 1], scale=rstd2[0:n, t:t + 1])
                ins.then_inc(s["y_made"], 1)
                if more:
                    indices(b + 1, 2)
                act.wait_ge(s["yt_turned"], d + 1)
                w = TAIL if tail else BN
                for c in range(C):
                    ins = nc.scalar.activation(yT[:, bass.ds(d * C * BN + c * BN, w)], pd[:, 1, c * BN:c * BN + w],
                                               ACT.Copy, accum_out=ysum[:, c, bass.ds(d, 1)])
                ins.then_inc(s["yt_ready"], 1)
                if more:
                    indices(b + 1, 3)
            over_blocks(act, stage3)

            act.wait_ge(s["route_step"], ROUTE_EXP[0])
            nc.scalar.activation(rt[:, R_E1, :], rt[:, R_LG, :], ACT.Exp, bias=rt[:, R_MX1, 0:1],
                                 accum_out=rt[:, R_S1, 0:1]).then_inc(s["route_exp"], 1)
            act.wait_ge(s["route_step"], ROUTE_EXP[1])
            nc.scalar.activation(rt[:, R_E2, :], rt[:, R_RW, :], ACT.Exp, bias=rt[:, R_MX2, 0:1],
                                 accum_out=rt[:, R_S2, 0:1]).then_inc(s["route_exp"], 1)
            act.wait_ge(s["route_step"], ROUTE_EXP[2])
            nc.scalar.activation(rt[:, R_G, 1:2], rt[:, R_M, 2:3], ACT.Exp).then_inc(s["route_exp"], 1)

            def hidden(q, u):
                w = TAIL if is_int(q, NQ) else QR
                wait(act, s["o5_made"], 2 * q - 2)
                for f in range(NF):
                    act.wait_ge(s["h_made"], NF * q + f + 1)
                    nc.scalar.activation(hT[u][:, f, 0:w], hbank(f)[:, 0:w], ACT.Gelu,
                                         bias=b1_c[:, f // FC, f % FC:f % FC + 1]).then_inc(s["h_act"], 1)

            act.wait_ge(s["experts_loaded"], 16 * 8)
            hidden(0, 0)

            def stage5(q, u):
                if not is_int(q, NQ):
                    hidden(q + 1, 1 - u)
                act.wait_ge(s["f_stats"], q + 1)
                for t, n in (enumerate(TAILS) if is_int(q, NQ) else [(t, P) for t in range(QT)]):
                    ins = nc.scalar.activation(z[u][0:n, t, :], z[u][0:n, t, :], ACT.Identity,
                                               bias=nmr2[0:n, t:t + 1], scale=rstd2[0:n, t:t + 1])
                ins.then_inc(s["zn_made"], 1)
            over_quads(act, stage5)

        @block.tensor
        def _(pe):
            mm = nc.tensor.matmul

            def add_keys(q, u):
                tiles = list(enumerate(TAILS)) if is_int(q, NQ) else [(t, P) for t in range(QT)]
                pe.wait_ge(s["phi_made"], 2 * q + len(tiles) // 2)
                for t, n in tiles:
                    for c in range(C):
                        ins = mm(pc[:, c, 0:KXW], phi[0:n, t, c * P:(c + 1) * P], xnb[u][0:n, t, :],
                                 start=is_int(q, 0) and t == 0, stop=is_int(q, NQ) and t == len(TAILS) - 1)
                ins.then_inc(s["kx_done"], 1)

            def stage1(q, u):
                tiles = list(enumerate(TAILS)) if is_int(q, NQ) else [(t, P) for t in range(QT)]
                pe.wait_ge(s["xn_ready"], q + 1)
                for t, n in tiles:
                    for c in range(C):
                        ins = nc.tensor.transpose(pd[:, c, t * P:t * P + n], xnb[u][0:n, t, c * P:(c + 1) * P],
                                                  ident[0:n, 0:n])
                ins.then_inc(s["xt_turned"], 1)
                if not is_int(q, 0):
                    add_keys(q - 1, 1 - u)
                else:
                    pe.wait_ge(s["wk_loaded"], 32)
                pe.wait_ge(s["xt_a"], q + 1)
                pe.wait_ge(s["xt_d"], q + 1)
                for pr in range(len(tiles) // 2):
                    for t, n in tiles[2 * pr:2 * pr + 2]:
                        for c in range(C):
                            ins = mm(pd[0:n, 2 + pr, (t % 2) * D:(t % 2 + 1) * D], xTb[u][:, c, t * P:t * P + n],
                                     wk_s[:, c, :], start=c == 0, stop=c == C - 1)
                    ins.then_inc(s["k_made"], 1)

            def turn_lists():
                for n in range(2):
                    pe.wait_ge(s["raw_float"], n + 1)
                    for g in range(NG):
                        wait(pe, s["raw_taken"], NG * n + g - 1)
                        for c in range(4 * g, min(4 * g + 4, NCH)):
                            ins = nc.tensor.transpose(pa[:, g % 2, (c % 4) * P:(c % 4 + 1) * P], rawf[:, c, :],
                                                      ident[:, :])
                        ins.then_inc(s["raw_turned"], 1)
                pe.wait_ge(s["raw_taken"], 2 * NG)
                pe.wait_ge(s["w_loaded"], W_LOADS)
                for n in range(2):
                    for o in range(C):
                        for c in range(C):
                            ins = nc.tensor.transpose(pa[:, n, c * D + o * P:c * D + (o + 1) * P],
                                                      wraw[n][:, o, c * P:(c + 1) * P], ident[:, :])
                ins.then_inc(s["wlr_turned"], 1)
                pe.wait_ge(s["flag_sum"], 1)
                pe.wait_ge(s["wlr_taken"], 1)
                mm(pa[0:1, 0, 0:1], cntp[:, 0:1], ones[:, 0:1], start=True, stop=True).then_inc(s["flag_added"], 1)

            pe.wait_ge(s["ident_set"], 2)
            pe.wait_ge(s["consts_set"], 1)
            over_quads(pe, stage1, turn_lists)
            add_keys(NQ, 0)

            pe.wait_ge(s["kx_taken"], 1)
            for c in range(C):
                for fc in range(C):
                    nc.tensor.transpose(pd[:, 0, fc * D + c * P:fc * D + (c + 1) * P],
                                        kx_s[:, c, fc * P:(fc + 1) * P], ident[:, :])
                ins = nc.tensor.transpose(pd[0:1, 1, c * P:(c + 1) * P], kx_s[:, c, D:D + 1], ident[:, :])
            ins.then_inc(s["kxT_made"], 1)
            pe.wait_ge(s["kxT_taken"], 1)
            for c in range(C):
                o = pd[:, 2, c * P:(c + 1) * P]
                for fc in range(C):
                    mm(o, wv_s[:, fc, c * P:(c + 1) * P], kxT[:, fc, c * P:(c + 1) * P], start=fc == 0, stop=False)
                ins = mm(o, bv_r[0:1, c * P:(c + 1) * P], ks_r[0:1, c * P:(c + 1) * P], start=False, stop=True)
            ins.then_inc(s["kv_made"], 1)
            pe.wait_ge(s["kv_taken"], 1)
            for c in range(C):
                ins = mm(pd[:, 3, c * D:(c + 1) * D], kvT[:, c, :], wo_s[:, c, :], start=True, stop=True)
            ins.then_inc(s["m_made"], 1)
            if_general(pe, general_pe)
            pe.wait_ge(s["m_taken"], 1)

            def turn_xn(d):
                pe.wait_ge(s["xn2_ready"], d + 1)
                wait(pe, s["nrm_eps"], d)
                for h in range(2):
                    n = TAILS[h] if is_int(d, NB - 1) else P
                    for c in range(C):
                        ins = nc.tensor.transpose(pd[:, 0, c * BN + h * P:c * BN + h * P + n],
                                                  xn2[0:n, h * D + c * P:h * D + (c + 1) * P], ident[0:n, 0:n])
                ins.then_inc(s["xt2_turned"], 1)

            def queries(d):
                pe.wait_ge(s["xt2_ready"], d + 1)
                wait(pe, s["yt_ready"], d)
                for o in range(C):
                    for c in range(C):
                        ins = mm(pd[:, 1, o * BN:(o + 1) * BN], wq_s[:, c, o * P:(o + 1) * P],
                                 xT2[:, c * BN:(c + 1) * BN], start=c == 0, stop=c == C - 1)
                ins.then_inc(s["q_made"], 1)

            def normalizers(d):
                pe.wait_ge(s["phq_made"], d + 1)
                for c in range(C):
                    ins = mm(pd[:, 0, c * BN:(c + 1) * BN], KS_s[:, c, :], pq[:, c * BN:(c + 1) * BN],
                             start=True, stop=True)
                ins.then_inc(s["nrm_made"], 1)

            def products(d):
                pe.wait_ge(s["agg_taken"], d + 1)
                pe.wait_ge(s["qhat_made"], d + 1)
                wait(pe, s["x1_made"], d)
                for h in range(2):
                    t = [(aggS, wlT), (xT2, wrT)]
                    for n, (a, w) in enumerate(t):
                        for c in range(C):
                            mm(pd[:, 2 + h, 0:D], a[:, c * BN + h * P:c * BN + (h + 1) * P], w[:, c, :],
                               start=n == 0 and c == 0, stop=n == 1 and c == C - 1)
                    for c in range(C):
                        ins = mm(pd[:, 2 + h, D:2 * D], pq[:, c * BN + h * P:c * BN + (h + 1) * P], M_s[:, c, :],
                                 start=c == 0, stop=c == C - 1)
                ins.then_inc(s["o_made"], 1)

            def turn_y(d):
                pe.wait_ge(s["y_made"], d + 1)
                for h in range(2):
                    n = TAILS[h] if is_int(d, NB - 1) else P
                    for c in range(C):
                        ins = nc.tensor.transpose(pd[:, 1, c * BN + h * P:c * BN + h * P + n],
                                                  yr[0:n, h * D + c * P:h * D + (c + 1) * P], ident[0:n, 0:n])
                ins.then_inc(s["yt_turned"], 1)

            HOOKS = {1: turn_xn, 4: queries, 9: normalizers, 17: products, 26: turn_y}

            def stage3(b, u):
                if is_int(b, NB):
                    for k in sorted(HOOKS):
                        HOOKS[k](b - 1)
                    return
                last_block = is_int(b, NB - 1)
                for q in range(4):
                    ks = batch_tiles(b, q)
                    for k in ks:
                        if k in HOOKS and not is_int(b, 0):
                            HOOKS[k](b - 1)
                        if k == ks[0]:
                            pe.wait_ge(s["oh_ready"], 4 * b + q + 1)
                            pe.wait_ge(s[f"gathered{q}"], batch_gathers(b, q))
                        slot = OSLOT[q] + k - BATCH[q][0]
                        parts = []
                        for db in (-1, 0, 1):
                            c0, c1 = max(LO[k], db * BN), min(LO[k] + WIN, (db + 1) * BN)
                            if c0 < c1 and not (db < 0 and is_int(b, 0)) and not (db > 0 and last_block):
                                parts.append((db, c0 - db * BN, c1 - db * BN, c0 - LO[k]))
                        for db, c0, c1, o0 in parts:
                            v = (u + db) % 2
                            first = (db == 1 and LO[k - 1] + WIN <= BN) or (is_int(b, 0) and k == 0)
                            if db == 1 and first:
                                wait(pe, s["agg_taken"], b)
                            closing = (db == -1 and LO[k + 1] >= 0) or (last_block and k == LAST - 1)
                            o1 = o0 + c1 - c0
                            for c in range(C):
                                mm(pa[:, v, c * BN + c0:c * BN + c1], msgs[:, k, c * P:(c + 1) * P],
                                   oh[:, slot, o0:o1], start=first and c == 0, stop=closing, skip_group_check=True)
                            ins = mm(pc[:, v, c0:c1], ones_h[:, :], ohc[:, slot, o0:o1], start=first, stop=closing,
                                     skip_group_check=True)
                            if closing:
                                ins.then_inc(s["agg_done"], 1)
                    if not (last_block and ks[-1] == LAST - 1):
                        ins.then_inc(s["batch_used"], 1)
            over_blocks(pe, stage3)

            pe.wait_ge(s["mean_made"], 1)
            for c in range(C):
                ins = mm(pd[0:1, 0, 0:NE], mean_c[:, c:c + 1], Wr_s[:, c, :], start=c == 0, stop=c == C - 1)
            ins.then_inc(s["logits_made"], 1)
            pe.wait_ge(s["gates_made"], 1)
            mm(pd[:, 1, 0:2], ones[0:1, :], gates[0:1, :], start=True, stop=True).then_inc(s["gates_spread"], 1)

            def hidden(q, u):
                w = TAIL if is_int(q, NQ) else QR
                for f in range(NF):
                    wait(pe, s["h_act"], NF * q + f - 3)
                    e, fc = divmod(f, FC)
                    for c in range(C):
                        if is_int(q, NQ):
                            rhs, o = yT[:, q * 2 * C * BN + c * BN:q * 2 * C * BN + c * BN + w], hbank(f)[:, 0:w]
                        else:
                            rhs = yT[:, bass.ds(q * 2 * C * BN, 2 * C * BN)]\
                                .rearrange("p (b c t) -> p b c t", b=2, c=C)[:, :, c, :]
                            o = pair(hbank(f))
                        ins = mm(o, W1_s[:, e, c, fc * P:(fc + 1) * P], rhs, start=c == 0, stop=c == C - 1)
                    ins.then_inc(s["h_made"], 1)

            pe.wait_ge(s["experts_loaded"], 16 * 8)
            hidden(0, 0)

            def stage5(q, u):
                if not is_int(q, NQ):
                    hidden(q + 1, 1 - u)
                if is_int(q, 0):
                    pe.wait_ge(s["w2_scaled"], 2)
                    pe.wait_ge(s["gates_taken"], 1)
                pe.wait_ge(s["h_act"], NF * (q + 1))
                wait(pe, s["z_made"], 2 * q - 2)
                tiles = list(enumerate(TAILS)) if is_int(q, NQ) else [(t, P) for t in range(QT)]
                for t, n in tiles:
                    for f in range(NF):
                        ins = mm(pd[0:n, 2 * u + t // 2, (t % 2) * D:(t % 2 + 1) * D], hT[u][:, f, t * P:t * P + n],
                                 W2_s[:, f, :], start=f == 0, stop=f == NF - 1)
                    if t % 2:
                        ins.then_inc(s["o5_made"], 1)
            over_quads(pe, stage5)

        @block.vector
        def _(dve):
            V = nc.vector

            V.memset(minus1[:, :], -1.0)
            V.memset(ones_h[:, :], 1.0)
            V.memset(zeros[:, :], 0.0)
            V.memset(mv[:, :, :], 1.0)
            V.memset(mask[:, :], 0.0)
            V.memset(rel[:, NCH * P:TCOLS], -1.0)
            V.memset(idx[:, NCH * P:TCOLS], 0)
            for u in range(2):
                V.memset(xnb[u][:, :, D:KXW], 1.0)
            V.memset(ones[:, :], 1.0).then_inc(s["mask_step"], 1)
            dve.wait_ge(s["mask_step"], 1)
            for h in range(P // HD):
                ins = V.memset(mask[h * HD:(h + 1) * HD, h * HD:(h + 1) * HD], 1.0)
            ins.then_inc(s["consts_set"], 1)
            V.memset(raw[:, NCH - 1, :], -(1 << 20)).then_inc(s["raw_padded"], 1)
            dve.wait_ge(s["iota_set"], 2)
            V.tensor_copy(iota_f[:, :], iota_i[:, :]).then_inc(s["iota_float"], 1)
            dve.wait_ge(s["wk_loaded"], 32)
            V.tensor_scalar(b1k_b[:, :], b1k_b[:, :], 1.0, None, ALU.add).then_inc(s["bias1_set"], 1)

            def row_stats(tiles, bn, m, r, done, value, rs, nm):
                wait(dve, s[done], value - 1)
                for t, (v, n) in enumerate(tiles):
                    ins = V.bn_stats(bst[0:n, t, :], v)
                ins.then_inc(s[bn], 1)
                dve.wait_ge(s[bn], value)
                dve.sem_inc(s["stats_read"], 1)
                for t, (v, n) in enumerate(tiles):
                    ins = V.bn_aggr(mv[0:n, t, :], bst[0:n, t, :])
                ins.then_inc(s[m], 1)
                dve.wait_ge(s[m], value)
                k = len(tiles)
                v, h, ys, yi = nv[:, 0:k], nh[:, 0:k], rs, ny[:, 0:k]
                chain = [RSQRT_STEPS * (value - 1)]

                def then(ins):
                    chain[0] = chain[0] + 1
                    ins.then_inc(s[r], 1)
                    dve.wait_ge(s[r], chain[0])
                then(V.tensor_scalar(v, mv[:, 0:k, 1], EPS, None, ALU.add))
                then(V.tensor_scalar(h.bitcast(I32), v.bitcast(I32), 1, None, ALU.logical_shift_right))
                then(V.tensor_scalar(yi.bitcast(I32), h.bitcast(I32), -1.0, float(0x5F3759DF), ALU.mult, ALU.add))
                for n in range(NEWTON):
                    then(V.tensor_tensor(h, yi, yi, ALU.mult))
                    then(V.scalar_tensor_tensor(out=h, in0=h, scalar=-0.5, in1=v, op0=ALU.mult, op1=ALU.mult))
                    then(V.scalar_tensor_tensor(out=ys if n == NEWTON - 1 else yi, in0=h, scalar=1.5, in1=yi,
                                                op0=ALU.add, op1=ALU.mult))
                V.scalar_tensor_tensor(out=nm, in0=mv[:, 0:k, 0], scalar=-1.0, in1=rs, op0=ALU.mult, op1=ALU.mult)\
                    .then_inc(s[done], 1)

            def keys(q):
                np_ = 1 if is_int(q, NQ) else 2
                wait(dve, s["phi_made"], 2 * q)
                for pr in range(np_):
                    dve.wait_ge(s["k_made"], 2 * q + pr + 1)
                    V.tensor_tensor(pair(kb1[pr]), pair(pd[:, 2 + pr, :]), bc(b1k_b[:, :], 2), ALU.add)\
                        .then_inc(s["kb_made"], 1)
                for pr in range(np_):
                    dve.wait_ge(s["ek_made"], 2 * q + pr + 1)
                    V.scalar_tensor_tensor(out=phi[:, 2 * pr:2 * pr + 2, :], in0=pair(ek[pr]), scalar=1.0,
                                           in1=pair(kb1[pr]), op0=ALU.min, op1=ALU.max).then_inc(s["phi_made"], 1)

            def stage1(q, u):
                tiles = list(enumerate(TAILS)) if is_int(q, NQ) else [(t, P) for t in range(QT)]
                dve.wait_ge(s[f"x_loaded{u}"], quad_dmas(q, u))
                row_stats([(xin[u][0:n, t, :], n) for t, n in tiles], "p1_bn", "p1_mv", "p1_rstd", "p1_stats", q + 1,
                          rstd_a[:, bass.ds(q * QT, len(tiles))], nmr_a[:, bass.ds(q * QT, len(tiles))])
                if is_int(q, 0):
                    dve.wait_ge(s["bias1_set"], 1)
                else:
                    keys(q - 1)
                dve.wait_ge(s["xt_turned"], q + 1)
                w = TAIL if is_int(q, NQ) else QR
                V.tensor_copy(xTb[u][:, 1, 0:w], pd[:, 1, 0:w]).then_inc(s["xt_d"], 1)

            def take_lists():
                for n in range(2):
                    dve.wait_ge(s["raw_loaded"], 48 * (n + 1))
                    V.tensor_copy(rawf, raw).then_inc(s["raw_float"], 1)
                    if n == 0:
                        dve.wait_ge(s["raw_float"], 1)
                        V.memset(raw[:, NCH - 1, :], 0).then_inc(s["raw_padded"], 1)
                    for g in range(NG):
                        w = min(4, NCH - 4 * g) * P
                        cols = slice(4 * g * P, 4 * g * P + w)
                        dve.wait_ge(s["raw_turned"], NG * n + g + 1)
                        if n == 0:
                            ins = V.tensor_tensor(rel[:, cols], pa[:, g % 2, 0:w], offs[:, cols], ALU.subtract)
                        else:
                            ins = V.tensor_copy(idx[:, cols], pa[:, g % 2, 0:w])
                        ins.then_inc(s["raw_taken"], 1)
                dve.wait_ge(s["wlr_turned"], 1)
                V.tensor_copy(wlT[:, :, :], pair(pa[:, 0, :]))
                V.tensor_copy(wrT[:, :, :], pair(pa[:, 1, :])).then_inc(s["wlr_taken"], 1)
                dve.wait_ge(s["raw_taken"], 2 * NG)
                V.tensor_scalar(bq1_c[:, :], bq_c[:, :], 1.0, None, ALU.add)
                V.tensor_scalar(inside[0], rel, 0.0, None, ALU.is_ge).then_inc(s["flag_a"], 1)
                dve.wait_ge(s["flag_a"], 1)
                V.scalar_tensor_tensor(out=inside[1], in0=rel, scalar=WIN - 1.0, in1=inside[0], op0=ALU.is_le,
                                       op1=ALU.mult).then_inc(s["flag_b"], 1)
                dve.wait_ge(s["flag_b"], 1)
                V.tensor_reduce(cntp[:, :], inside[1], AX.X, ALU.add).then_inc(s["flag_sum"], 1)
                dve.wait_ge(s["flag_added"], 1)
                V.tensor_scalar(flag[:, :], pa[0:1, 0, 0:1], float(E), None, ALU.is_lt).then_inc(s["flag_set"], 1)
            over_quads(dve, stage1, take_lists)
            keys(NQ)

            dve.wait_ge(s["kx_done"], NQ + 1)
            V.tensor_copy(kx_s, pc[:, :, 0:KXW]).then_inc(s["kx_taken"], 1)
            dve.wait_ge(s["kx_taken"], 1)
            for c in range(C):
                V.tensor_scalar(KS_s[:, c, :], mask[:, :], kx_s[:, c, D:D + 1], None, ALU.mult)
            dve.wait_ge(s["kxT_made"], 1)
            V.tensor_copy(kxT, pair(pd[:, 0, :]))
            V.tensor_copy(ks_r, pd[0:1, 1, 0:D]).then_inc(s["kxT_taken"], 1)
            dve.wait_ge(s["kv_made"], 1)
            V.tensor_tensor(kvT, pair(pd[:, 2, 0:C * P]), bc(mask[:, :], 2), ALU.mult).then_inc(s["kv_taken"], 1)
            dve.wait_ge(s["m_made"], 1)
            V.tensor_copy(M_s[:, :, :], pair(pd[:, 3, :])).then_inc(s["m_taken"], 1)
            if_general(dve, general_dve)
            dve.wait_ge(s["iota_float"], 1)
            dve.wait_ge(s["raw_taken"], 2 * NG)
            dve.wait_ge(s["p1_stats"], NQ + 1)

            def one_hots(b, q):
                ks = batch_tiles(b, q)
                if not ks:
                    return
                wait(dve, s["batch_used"], 4 * b + q - 1)
                m, slot = len(ks), OSLOT[q]
                number = bc(iota_f[:, :], m)
                where = rel[:, bass.ds(b * TB + ks[0], m)].unsqueeze(2).to_broadcast([P, m, WIN])
                V.tensor_tensor(oh[:, slot:slot + m, :], number, where, ALU.is_equal)
                V.tensor_tensor(ohc[:, slot:slot + m, :], number, where, ALU.is_equal).then_inc(s["oh_ready"], 1)

            def stage3(b, u):
                if is_int(b, 0):
                    for q in range(4):
                        one_hots(b, q)
                    return
                edges_left = not is_int(b, NB)
                d = b - 1
                if edges_left:
                    one_hots(b, 0)
                    one_hots(b, 1)
                dve.wait_ge(s["eq_made"], d + 1)
                V.scalar_tensor_tensor(out=pq, in0=pq, scalar=1.0, in1=qb, op0=ALU.min, op1=ALU.max)\
                    .then_inc(s["phq_made"], 1)
                dve.wait_ge(s["xn2_ready"], d + 1)
                wait(dve, s["x1a_made"], d)
                V.tensor_tensor(r0, xr, xn2, ALU.add).then_inc(s["r0_made"], 1)
                dve.wait_ge(s["r0_made"], d + 1)
                V.tensor_tensor(pair(r0), pair(r0), bc(bo_b[:, :], 2), ALU.add).then_inc(s["r0b_made"], 1)
                dve.wait_ge(s["agg_done"], d + 1)
                wait(dve, s["o_made"], d)
                wait(dve, s["x1_made"], d)
                wait(dve, s["agg_taken"], d)
                V.tensor_scalar(rc[:, :], pc[:, 1 - u, 0:BN], 1.0, None, ALU.max).then_inc(s["cnt_max"], 1)
                dve.wait_ge(s["cnt_max"], d + 1)
                V.reciprocal(rc[:, :], rc[:, :]).then_inc(s["cnt_rec"], 1)
                dve.wait_ge(s["cnt_rec"], d + 1)
                V.tensor_tensor(pair(aggS), pair(pa[:, 1 - u, :]), bc(rc[:, :], 2), ALU.mult)\
                    .then_inc(s["agg_taken"], 1)
                dve.wait_ge(s["nrm_made"], d + 1)
                V.tensor_scalar(qb, pd[:, 0, :], 1e-6, None, ALU.add).then_inc(s["nrm_eps"], 1)
                dve.wait_ge(s["nrm_eps"], d + 1)
                V.reciprocal(qb, qb).then_inc(s["nrm_rec"], 1)
                dve.wait_ge(s["nrm_rec"], d + 1)
                V.tensor_tensor(pq, pq, qb, ALU.mult).then_inc(s["qhat_made"], 1)
                if edges_left:
                    one_hots(b, 2)
                    one_hots(b, 3)
                dve.wait_ge(s["o_made"], d + 1)
                V.tensor_tensor(pair(aggS), pd[:, 2:4, 0:D], bc(bl_b[:, :], 2), ALU.add).then_inc(s["g1_made"], 1)
                dve.wait_ge(s["g1_made"], d + 1)
                dve.wait_ge(s["r0b_made"], d + 1)
                V.scalar_tensor_tensor(out=aggS, in0=aggS, scalar=0.0, in1=r0, op0=ALU.max, op1=ALU.add)\
                    .then_inc(s["x1a_made"], 1)
                dve.wait_ge(s["x1a_made"], d + 1)
                wait(dve, s["x1_stored"], 16 * d)
                wait(dve, s["y_made"], d)
                V.tensor_tensor(pair(x1), pair(aggS), pd[:, 2:4, D:2 * D], ALU.add).then_inc(s["x1_made"], 1)
                dve.wait_ge(s["x1_made"], d + 1)
                rows = TAILS if is_int(d, NB - 1) else [P, P]
                row_stats([(x1[0:n, t * D:(t + 1) * D], n) for t, n in enumerate(rows)],
                          "d_bn", "d_mv", "d_rstd", "d_stats", d + 1, rstd2[:, 0:2], nmr2[:, 0:2])
            over_blocks(dve, stage3)

            dve.wait_ge(s["yt_ready"], NB)
            V.tensor_reduce(ysr[:, :], ysum[:, :, :], AX.X, ALU.add).then_inc(s["ysum_made"], 1)
            dve.wait_ge(s["ysum_made"], 1)
            V.tensor_scalar(mean_c[:, :], ysr[:, :], 1.0 / N, None, ALU.mult).then_inc(s["mean_made"], 1)
            V.tensor_copy(rt[:, R_IO, :], iota_f[0:1, 0:NE])
            steps = [0]

            def step(ins):
                steps[0] += 1
                ins.then_inc(s["route_step"], 1)
                dve.wait_ge(s["route_step"], steps[0])

            def row(n, w=NE, at=0):
                return rt[:, n, at:at + w]
            dve.wait_ge(s["logits_made"], 1)
            step(V.tensor_tensor(row(R_LG), pd[0:1, 0, 0:NE], br_r[:, :], ALU.add))
            step(V.tensor_reduce(row(R_MX1, 1), row(R_LG), AX.X, ALU.max))
            step(V.tensor_scalar(row(R_MX1, 1), row(R_MX1, 1), -1.0, None, ALU.mult))
            assert steps[0] == ROUTE_EXP[0]
            dve.wait_ge(s["route_exp"], 1)
            step(V.reciprocal(row(R_S1, 1), row(R_S1, 1)))
            step(V.tensor_scalar(row(R_RW), row(R_E1), row(R_S1, 1), CAP / N, ALU.mult, ALU.min))
            step(V.tensor_reduce(row(R_MX2, 1), row(R_RW), AX.X, ALU.max))
            step(V.tensor_scalar(row(R_MX2, 1), row(R_MX2, 1), -1.0, None, ALU.mult))
            assert steps[0] == ROUTE_EXP[1]
            dve.wait_ge(s["route_exp"], 2)
            step(V.reciprocal(row(R_S2, 1), row(R_S2, 1)))
            step(V.tensor_scalar(row(R_W), row(R_E2), row(R_S2, 1), None, ALU.mult))
            step(V.tensor_reduce(row(R_M, 1), row(R_W), AX.X, ALU.max))

            def first_at(values, largest, n):
                step(V.tensor_scalar(row(R_T), values, largest, float(NE), ALU.is_lt, ALU.mult))
                step(V.tensor_tensor(row(R_U), row(R_T), row(R_IO), ALU.add))
                step(V.tensor_reduce(row(R_I, 1, n), row(R_U), AX.X, ALU.min))
            first_at(row(R_W), row(R_M, 1), 0)
            step(V.tensor_scalar(row(R_T), row(R_IO), row(R_I, 1), -2.0, ALU.is_equal, ALU.mult))
            step(V.tensor_tensor(row(R_W2), row(R_W), row(R_T), ALU.add))
            step(V.tensor_reduce(row(R_M, 1, 1), row(R_W2), AX.X, ALU.max))
            first_at(row(R_W2), row(R_M, 1, 1), 1)
            step(V.tensor_tensor(row(R_M, 1, 2), row(R_M, 1, 1), row(R_M, 1, 0), ALU.subtract))
            V.tensor_copy(pick[:, :], row(R_I, 2)).then_inc(s["picked"], 1)
            step(V.tensor_scalar(row(R_G, 1, 2), row(R_M, 1, 2), 1.0, None, ALU.mult))
            assert steps[0] == ROUTE_EXP[2]
            dve.wait_ge(s["route_exp"], 3)
            step(V.tensor_scalar(row(R_G, 1), row(R_G, 1, 1), 1.0, None, ALU.add))
            step(V.reciprocal(gates[:, 0:1], row(R_G, 1)))
            V.tensor_tensor(gates[:, 1:2], gates[:, 0:1], row(R_G, 1, 1), ALU.mult).then_inc(s["gates_made"], 1)
            dve.wait_ge(s["gates_spread"], 1)
            V.tensor_copy(gate_b[:, :], pd[:, 1, 0:2]).then_inc(s["gates_taken"], 1)
            dve.wait_ge(s["gates_taken"], 1)
            dve.wait_ge(s["experts_loaded"], 16 * 8)
            for e in range(2):
                V.tensor_scalar(W2_s[:, e * FC:(e + 1) * FC, :], W2_r[:, e * FC:(e + 1) * FC, :], gate_b[:, e:e + 1],
                                None, ALU.mult).then_inc(s["w2_scaled"], 1)
            V.tensor_scalar(b2a, b2_b[:, 0, :], gate_b[:, 0:1], None, ALU.mult).then_inc(s["b2_step"], 1)
            dve.wait_ge(s["b2_step"], 1)
            V.scalar_tensor_tensor(out=b2m, in0=b2_b[:, 1, :], scalar=gate_b[:, 1:2], in1=b2a, op0=ALU.mult,
                                   op1=ALU.add).then_inc(s["b2_made"], 1)
            dve.wait_ge(s["w2_scaled"], 2)

            def finish(q, u):
                n = len(TAILS) if is_int(q, NQ) else QT
                dve.wait_ge(s["zn_made"], q + 1)
                V.tensor_tensor(z[u][:, 0:n, :], z[u][:, 0:n, :], bc(gamma_b[:, :], n), ALU.mult)\
                    .then_inc(s["f_scaled"], 1)
                dve.wait_ge(s["f_scaled"], q + 1)
                dve.wait_ge(s["xb_made"], q + 1)
                V.tensor_tensor(x1_in[u][:, 0:n, :], x1_in[u][:, 0:n, :], z[u][:, 0:n, :], ALU.add)\
                    .then_inc(s["fin_made"], 1)

            def stage5(q, u):
                tiles = list(enumerate(TAILS)) if is_int(q, NQ) else [(t, P) for t in range(QT)]
                dve.wait_ge(s["yb_made"], q + 1)
                wait(dve, s["fin_made"], q - 1)
                for pr in range(len(tiles) // 2):
                    dve.wait_ge(s["o5_made"], 2 * q + pr + 1)
                    V.tensor_tensor(z[u][:, 2 * pr:2 * pr + 2, :], pair(pd[:, 2 * u + pr, :]),
                                    y_in[u][:, 2 * pr:2 * pr + 2, :], ALU.add).then_inc(s["z_made"], 1)
                dve.wait_ge(s["z_made"], 2 * q + len(tiles) // 2)
                if not is_int(q, 0):
                    wait(dve, s["zn_made"], q)
                row_stats([(z[u][0:n, t, :], n) for t, n in tiles], "f_bn", "f_mv", "f_rstd", "f_stats", q + 1,
                          rstd2[:, 0:len(tiles)], nmr2[:, 0:len(tiles)])
                if not is_int(q, 0):
                    finish(q - 1, 1 - u)
            over_quads(dve, stage5)
            finish(NQ, 0)


_INS = ["x", "src", "dst", "L0_gnn_W_l", "L0_gnn_b_l", "L0_gnn_W_r", "L0_mix_wq", "L0_mix_bq", "L0_mix_wk", "L0_mix_bk",
        "L0_mix_wv", "L0_mix_bv", "L0_mix_wo", "L0_mix_bo", "L0_ffn_Wr", "L0_ffn_br", "L0_ffn_W1", "L0_ffn_b1",
        "L0_ffn_W2", "L0_ffn_b2", "L0_ffn_gamma", "L0_ffn_beta"]


def kernel(**inputs):
    import numpy as np
    import concourse.bacc as bacc
    from concourse.bass_utils import run_bass_kernel_spmd

    nc = bacc.Bacc("TRN2", target_bir_lowering=False, num_devices=1)
    arrays, args = {}, []
    for name in _INS:
        a = np.ascontiguousarray(inputs[name])
        arrays[f"in_{name}"] = a
        args.append(nc.dram_tensor(f"in_{name}", a.shape, mybir.dt.from_np(a.dtype), kind="ExternalInput").ap())
    out = nc.dram_tensor("out", inputs["x"].shape, F32, kind="ExternalOutput").ap()
    build_layer(nc, *args, out)
    r = run_bass_kernel_spmd(nc, [arrays], core_ids=[0])
    return r.results[0]["out"]
```

```python
import math
from contextlib import ExitStack

import concourse.bass as bass
from concourse import mybir

F32 = mybir.dt.float32
F16 = mybir.dt.float16
I32 = mybir.dt.int32
ALU = mybir.AluOpType
ACT = mybir.ActivationFunctionType
AX = mybir.AxisListType

P = 128
EPS = 1e-5


def wait(eng, sem, value):
    if not (isinstance(value, int) and value <= 0):
        eng.wait_ge(sem, value)


def build_layer(nc, x, src, dst, W_l, b_l, W_r, wq, bq, wk, bk, wv, bv, wo, bo,
                Wr, br, W1, b1, W2, b2, gamma, beta, out):
    N, D = x.shape
    E = src.shape[0]
    NE, _, F = W1.shape
    C = D // P
    HD = D // 8
    FC = F // P
    NF = 2 * FC
    QT = 4
    QR = QT * P
    NQ = N // QR
    TAIL = N - NQ * QR
    TAILS = [min(P, TAIL - P * s) for s in range(math.ceil(TAIL / P))]
    BN = 2 * P
    NB = math.ceil(N / BN)
    ET = math.ceil(E / P)
    TB = 34
    LAST = ET - (NB - 1) * TB
    NCH = math.ceil(ET / P)
    TCOLS = NB * TB
    BATCH = [(0, 4), (4, 8), (8, 12), (12, 17), (17, 21), (21, 25), (25, 29), (29, 34)]
    NBT = len(BATCH)
    SLOTS = TB // 2
    PARTS = 2
    XS = 2048.0
    RING = 12800
    WIN = P
    LO = [15 * (k // 2) + 7 * (k % 2) - 60 for k in range(TB)]
    CAP = float(math.ceil(N * 1.25 / NE))
    GW = D + 4
    GT = math.ceil(N / P)
    assert TAIL > 0 and len(TAILS) == 2 and NQ % 2 == 0 and NB % 2 == 1 and BN * (NB - 1) == NQ * QR

    xn_table = nc.dram_tensor("xn_table", (N, PARTS * D), F16).ap()
    y_rows = nc.dram_tensor("y_rows", (N, D), F32).ap()
    x1_rows = nc.dram_tensor("x1_rows", (N, D), F32).ap()
    sum_rows = nc.dram_tensor("sum_rows", ((GT + 1) * P, GW), F32).ap()

    with ExitStack() as ctx:
        def sb(name, shape, dtype=F32):
            return ctx.enter_context(nc.sbuf_tensor(name, shape, dtype))

        def sem(name):
            return ctx.enter_context(nc.semaphore(name))

        YT = NB * C * BN - (BN - TAIL)
        yT = sb("yT", [P, YT])
        edges = sb("edges", [P, 2 * TCOLS])
        mats = sb("mats", [P, 6 * C * D])
        ring = sb("ring", [P, RING])
        ohh = sb("ohh", [P, SLOTS * WIN], F16)
        work = sb("work", [P, 9 * 512])
        bl_b, bo_b, gamma_b, beta_b = sb("bl_b", [P, D]), sb("bo_b", [P, D]), sb("gamma_b", [P, D]), sb("beta_b", [P, D])
        M_s, KS_s = sb("M_s", [P, C, D]), sb("KS_s", [P, C, P])
        Wr_s = sb("Wr_s", [P, C, NE])
        bq_c, bq1_c = sb("bq_c", [P, C]), sb("bq1_c", [P, C])
        br_r = sb("br_r", [1, NE])
        ident, ones = sb("ident", [P, P]), sb("ones", [P, P])
        ones_h = sb("ones_h", [P, P], F16)
        iota_f = sb("iota_f", [P, WIN])
        rstd_a, nmr_a = sb("rstd_a", [P, (NQ + 1) * QT]), sb("nmr_a", [P, (NQ + 1) * QT])
        ysum = sb("ysum", [P, C, NB])
        flag = sb("flag", [1, 1], I32)
        cntp = sb("cntp", [P, 1])
        idxb = sb("idxb", [P, TB], I32)
        mv, bst = sb("mv", [P, QT, 2]), sb("bst", [P, QT, 6])
        rstd2, nmr2 = sb("rstd2", [P, QT]), sb("nmr2", [P, QT])
        rc = sb("rc", [P, BN])

        idx = edges[:, 0:TCOLS].bitcast(I32)
        rel = edges[:, TCOLS:2 * TCOLS]

        def mat(n):
            return mats[:, n * C * D:(n + 1) * C * D].rearrange("p (c d) -> p c d", c=C)
        wk_s, wq_s, wv_s, wo_s, wlT, wrT = (mat(n) for n in range(6))
        msgs = ring[:, 0:TB * PARTS * D // 2].bitcast(F16).rearrange("p (k s d) -> p k s d", s=PARTS, d=D)
        oh = ohh[:, :].rearrange("p (k w) -> p k w", w=WIN)

        at = {"yT": 8 * C * BN, "ring": 0}

        def early(n, whole="yT"):
            at[whole] += n
            return (yT if whole == "yT" else ring)[:, at[whole] - n:at[whole]]
        KXW = D + 1
        xin = [early(QT * D).rearrange("p (s d) -> p s d", d=D) for _ in range(2)]
        xnb = [early(QT * KXW).rearrange("p (s d) -> p s d", d=KXW) for _ in range(2)]
        xTb = [early(C * QR).rearrange("p (c t) -> p c t", c=C) for _ in range(2)]
        xp = [early(QT * PARTS * D // 2, "ring").bitcast(F16).rearrange("p (s d) -> p s d", d=PARTS * D) for _ in range(2)]
        xs = early(QT * D, "ring").rearrange("p (s d) -> p s d", d=D)
        kb1 = [early(2 * D) for _ in range(2)]
        ek = [early(2 * D) for _ in range(2)]
        phi = early(QT * D).rearrange("p (s d) -> p s d", d=D)
        kx_s = early(C * KXW).rearrange("p (c d) -> p c d", c=C)
        kxT = early(C * D).rearrange("p (c d) -> p c d", c=C)
        ks_r = early(D)[0:1, :]
        kvT = early(C * P).rearrange("p (c d) -> p c d", c=C)
        inside = [early(TCOLS) for _ in range(2)]
        raw = inside[0][:, 0:NCH * P].bitcast(I32).rearrange("p (c e) -> p c e", e=P)
        rawf = inside[1][:, 0:NCH * P].rearrange("p (c e) -> p c e", e=P)
        offs = early(TCOLS, "ring").bitcast(I32)
        b1k_b = early(D)
        bv_r = early(D)[0:1, :]
        mask = early(P)
        iota_i = early(WIN).bitcast(I32)
        zeros = early(GW, "ring")
        wraw = [early(C * D).rearrange("p (c d) -> p c d", c=C) for _ in range(2)]
        g_parts = early(PARTS * D // 2, "ring").bitcast(F16)
        g_row = early(GW, "ring")
        g_src = early(1, "ring").bitcast(I32)
        g_dst = early(1, "ring")
        g_dsts = early(P, "ring")
        g_same = early(P, "ring")
        g_before = early(P, "ring")
        g_later = early(P, "ring")
        g_dup, g_pad, g_dup2, g_gap, g_dump = (early(1, "ring") for _ in range(5))
        g_dump_i, g_to = early(1, "ring").bitcast(I32), early(1, "ring").bitcast(I32)
        g_sum = early(GW, "ring")
        g_back = early(GW, "ring")
        g_cnt = early(1, "ring")
        g_mean = early(D, "ring")
        g_out = early(PARTS * D // 2, "ring").bitcast(F16)
        g_node_i, g_node = early(NB, "ring").bitcast(I32), early(NB, "ring")
        g_p, g_ra, g_rb, g_rc = (early(1, "ring") for _ in range(4))
        assert at["yT"] <= YT and at["ring"] <= RING

        xr, xn2, xT2, pq, qb, aggS, r0, x1, yr = (work[:, n * 512:(n + 1) * 512] for n in range(9))
        hT = [ring[:, u * NF * QR:(u + 1) * NF * QR].rearrange("p (f t) -> p f t", f=NF) for u in range(2)]
        W1_s = mats[:, 0:2 * C * F].rearrange("p (e c f) -> p e c f", e=2, c=C)
        late_at = [2 * NF * QR]

        def late(n):
            late_at[0] += n
            return ring[:, late_at[0] - n:late_at[0]]
        W2_s = late(NF * D).rearrange("p (f d) -> p f d", d=D)
        W2_r = edges[:, 0:NF * D].rearrange("p (f d) -> p f d", d=D)
        rt = late(16 * NE)[0:1, :].rearrange("a (r n) -> a r n", n=NE)
        ysr, mean_c, gate_b = (late(C) for _ in range(3))
        gates, pick = late(2)[0:1, :], late(2)[0:1, :].bitcast(I32)
        b1_c = late(2 * FC).rearrange("p (e f) -> p e f", e=2)
        assert late_at[0] <= RING
        z = [t.rearrange("p (s d) -> p s d", d=D)
             for t in (mats[:, 2 * C * F:2 * C * F + QT * D], edges[:, NF * D:NF * D + QT * D])]
        b2_b = ohh[:, 0:4 * D].bitcast(F32).rearrange("p (e d) -> p e d", e=2)
        b2a = ohh[:, 4 * D:6 * D].bitcast(F32)
        b2m = ohh[:, 6 * D:8 * D].bitcast(F32)
        y_in = [work[:, u * QT * D:(u + 1) * QT * D].rearrange("p (s d) -> p s d", d=D) for u in range(2)]
        x1_in = [work[:, (2 + u) * QT * D:(3 + u) * QT * D].rearrange("p (s d) -> p s d", d=D) for u in range(2)]

        pa = ctx.enter_context(nc.psum_tensor("pa", [P, 2, 512], F32))
        pc = ctx.enter_context(nc.psum_tensor("pc", [P, 2, 512], F32))
        pd = ctx.enter_context(nc.psum_tensor("pd", [P, 4, 512], F32))

        names = """stats_read batch_started iota_set iota_float mask_step wk_loaded consts_set ident_set raw_padded raw_loaded raw_float raw_turned raw_taken
            flag_a flag_b flag_sum flag_added flag_set w_loaded wlr_turned wlr_taken bias1_set
            x_loaded0 x_loaded1 p1_bn p1_mv p1_rstd p1_stats quad_started xs_made hi_made lo_made xn_ready xn_stored0 xn_stored1 xt_turned xt_made
            k_made kb_made ek_made phi_made kx_done kx_taken kxT_made kxT_taken kv_made kv_taken m_made m_taken
            idx_ready gathered0 gathered1 gathered2 gathered3 gathered4 gathered5
            gathered6 gathered7 oh_ready batch_used agg_done agg_taken
            xr_loaded xn2_ready xt2_turned xt2_ready q_made eq_made phq_made nrm_made nrm_eps nrm_rec qhat_made
            cnt_max cnt_rec r0_made r0b_made o_made g1_made x1a_made x1_made d_bn d_mv d_rstd d_stats
            y_made yt_turned yt_ready x1_stored y_stored
            route_step route_exp logits_made ysum_made mean_made picked gates_made gates_spread gates_taken
            experts_loaded w2_scaled b2_step b2_made yin_loaded0 yin_loaded1 yb_made xb_made
            h_made h_act o5_made z_made f_bn f_mv f_rstd f_stats zn_made f_scaled fin_made out_stored0 out_stored1
            g_iota g_zeroed g_src_set g_loaded g_row_made g_split g_to_made g_taken g_added g_back_loaded g_mean_made g_mean_stored
            g_replaced g_done g_dsts_made g_turned g_same_made g_summed g_consts g_tests g_dup_made g_dup2_made
            g_cnt_made g_rec_made g_index""".split()
        s = {n: sem(n) for n in names}

        def quad_rows(table, q):
            return table[bass.ds(q * QR, QR), :].rearrange("(s p) d -> p s d", p=P)

        def quad_io(eng, table, tile, q, signal, store):
            if isinstance(q, int) and q == NQ:
                pairs = [(tile[0:n, t, :], table[q * QR + t * P:q * QR + t * P + n, :]) for t, n in enumerate(TAILS)]
            else:
                pairs = [(tile[:, :, :], quad_rows(table, q))]
            for a, b in pairs:
                (eng.dma_start(b, a) if store else eng.dma_start(a, b)).then_inc(signal, 16)

        def quad_dmas(q, u):
            if isinstance(q, int) and q == NQ:
                return 16 * (NQ // 2 + len(TAILS))
            return (q - u) * 8 + 16

        def block_io(eng, table, tile, d, signal, store):
            t3 = tile.rearrange("p (s d) -> p s d", d=D)
            if isinstance(d, int) and d == NB - 1:
                pairs = [(t3[0:n, t, :], table[d * BN + t * P:d * BN + t * P + n, :]) for t, n in enumerate(TAILS)]
            else:
                pairs = [(t3, table[bass.ds(d * BN, BN), :].rearrange("(s p) d -> p s d", p=P))]
            for a, b in pairs:
                (eng.dma_start(b, a) if store else eng.dma_start(a, b)).then_inc(signal, 16)

        def block_dmas(d):
            return 16 * (d + len(TAILS)) if isinstance(d, int) and d == NB - 1 else 16 * (d + 1)

        def over_quads(eng, body, between=None):
            body(0, 0)
            body(1, 1)
            if between:
                between()
            with eng.Fori(1, NQ // 2 - 1) as i:
                body(2 * i, 0)
                body(2 * i + 1, 1)
            for q in range(NQ - 2, NQ + 1):
                body(q, q % 2)

        def over_blocks(eng, body):
            for b in range(3):
                body(b, b % 2)
            with eng.Fori(1, (NB - 3) // 2) as i:
                body(2 * i + 1, 1)
                body(2 * i + 2, 0)
            for b in range(NB - 2, NB + 1):
                body(b, b % 2)

        def batch_tiles(b, q):
            k0, k1 = BATCH[q]
            return range(k0, min(k1, LAST) if isinstance(b, int) and b == NB - 1 else k1)

        def batch_gathers(b, q):
            k0, k1 = BATCH[q]
            if isinstance(b, int) and b == NB - 1:
                return 16 * ((k1 - k0) * b + len(batch_tiles(b, q)))
            return 16 * (k1 - k0) * (b + 1)

        def is_int(v, n):
            return isinstance(v, int) and v == n

        def whole(q):
            return [(slice(t, t + 1), n) for t, n in enumerate(TAILS)] if is_int(q, NQ) else [(slice(0, QT), P)]

        minus1 = sb("minus1", [P, 1])
        nv, nh, ny = sb("nv", [P, QT]), sb("nh", [P, QT]), sb("ny", [P, QT])
        NEWTON = 3
        RSQRT_STEPS = 3 + 3 * NEWTON
        (R_LG, R_E1, R_RW, R_E2, R_W, R_T, R_W2, R_IO, R_MX1, R_S1, R_MX2, R_S2, R_M, R_I, R_G, R_U) = range(16)
        ROUTE_EXP = (3, 7, 21)
        W_LOADS = 16 * 13
        NG = math.ceil(NCH / 4)

        def hbank(f):
            return (pa if f % 4 < 2 else pc)[:, f % 2, :]

        def bc(v, n):
            return v.unsqueeze(1).to_broadcast([P, n, v.shape[1]])

        def pair(v):
            return v.rearrange("p (a d) -> p a d", a=2)

        def if_general(eng, program):
            eng.wait_ge(s["flag_set"], 1)
            bad = eng.value_load(flag[0:1, 0:1], min_val=0, max_val=1)
            with eng.If(bad):
                if program:
                    program(eng)
                eng.wait_ge(s["g_done"], 1)

        TILE_A, TILE_B, TILE_C = LO.index(0), 25, 26
        assert LO[TILE_B] == P - 1 and LO[TILE_C] > P - 1 and TILE_C < min(LAST, TB)

        SPLITS = 2 * PARTS - 1

        general_sp = None

        def general_pool(pool):
            pool.iota(g_dump_i, pattern=[[0, 1]], base=GT * P, channel_multiplier=1).then_inc(s["g_iota"], 1)
            pool.iota(g_node_i, pattern=[[BN, NB]], base=0, channel_multiplier=1).then_inc(s["g_iota"], 1)
            pool.affine_select(out=g_later, in_=ones[:, :], compare_op=ALU.is_gt, fill=0.0, base=0,
                               pattern=[[-1, P]], channel_multiplier=1).then_inc(s["g_iota"], 1)
            with pool.Fori(0, GT + 1) as t:
                pool.dma_start(sum_rows[bass.ds(t * P, P), :], zeros[:, :]).then_inc(s["g_zeroed"], 16)
            pool.wait_ge(s["g_zeroed"], 16 * (GT + 1))
            with pool.Fori(0, ET) as t:
                pool.wait_ge(s["g_src_set"], t + 1)
                pool.sem_inc(s["batch_started"], 1)
                pool.indirect_dma_start(out=g_parts, out_offset=None, in_=xn_table[:, :],
                                        in_offset=bass.IndirectOffsetOnAxis(ap=g_src, axis=0))\
                    .then_inc(s["g_loaded"], 16)
                pool.wait_ge(s["g_to_made"], t + 1)
                pool.wait_ge(s["g_taken"], t + 1)
                pool.sem_inc(s["batch_started"], 1)
                pool.indirect_dma_start(out=sum_rows[:, :], out_offset=bass.IndirectOffsetOnAxis(ap=g_to, axis=0),
                                        in_=g_sum, in_offset=None, compute_op=ALU.add).then_inc(s["g_added"], 16)
                pool.wait_ge(s["g_added"], 16 * t + 16)
            with pool.Fori(0, GT - 1) as t:
                pool.dma_start(g_back, sum_rows[bass.ds(t * P, P), :]).then_inc(s["g_back_loaded"], 16)
                pool.wait_ge(s["g_split"], SPLITS * (t + 1))
                pool.dma_start(xn_table[bass.ds(t * P, P), :], g_out).then_inc(s["g_mean_stored"], 16)
                pool.wait_ge(s["g_mean_stored"], 16 * t + 16)
            n = N - (GT - 1) * P
            pool.dma_start(g_back, sum_rows[(GT - 1) * P:GT * P, :]).then_inc(s["g_back_loaded"], 16)
            pool.wait_ge(s["g_split"], SPLITS * GT)
            pool.dma_start(xn_table[(GT - 1) * P:N, :], g_out[0:n, :]).then_inc(s["g_mean_stored"], 16)
            pool.wait_ge(s["g_mean_stored"], 16 * GT)
            pool.wait_ge(s["g_replaced"], 1)
            pool.sem_inc(s["g_done"], 1)

        def general_pe(pe):
            with pe.Fori(0, ET) as t:
                pe.wait_ge(s["g_dsts_made"], t + 1)
                nc.tensor.transpose(pa[:, 0, 0:P], g_dsts, ident[:, :]).then_inc(s["g_turned"], 1)
                pe.wait_ge(s["g_same_made"], t + 1)
                pe.wait_ge(s["g_row_made"], t + 1)
                nc.tensor.matmul(pa[:, 1, 0:GW], g_same, g_row, start=True, stop=True).then_inc(s["g_summed"], 1)

        def general_dve(dve):
            V = nc.vector
            dve.wait_ge(s["g_iota"], 3)
            V.tensor_copy(g_dump, g_dump_i)
            V.memset(g_row[:, D:GW], 0.0).then_inc(s["g_consts"], 1)
            dve.wait_ge(s["g_consts"], 1)
            V.memset(g_row[:, D:D + 1], 1.0).then_inc(s["g_consts"], 1)
            dve.wait_ge(s["g_consts"], 2)
            with dve.Fori(0, ET) as t:
                V.tensor_tensor(g_dst, rel[:, bass.ds(t, 1)], offs[:, bass.ds(t, 1)], ALU.add)
                V.tensor_copy(g_src, idx[:, bass.ds(t, 1)]).then_inc(s["g_src_set"], 1)
                dve.wait_ge(s["g_src_set"], t + 1)
                V.tensor_copy(g_dsts, g_dst.to_broadcast([P, P])).then_inc(s["g_dsts_made"], 1)
                dve.wait_ge(s["g_turned"], t + 1)
                V.tensor_scalar(g_same, pa[:, 0, 0:P], g_dst, None, ALU.is_equal).then_inc(s["g_same_made"], 1)
                dve.wait_ge(s["g_same_made"], t + 1)
                dve.wait_ge(s["g_loaded"], 16 * t + 16)
                V.tensor_tensor(g_row[:, 0:D], g_parts[:, 0:D], g_parts[:, D:2 * D], ALU.add)\
                    .then_inc(s["g_row_made"], 1)
                V.tensor_tensor(g_before, g_same, g_later, ALU.mult)
                V.tensor_scalar(g_pad, g_dst, 0.0, None, ALU.is_lt)
                V.tensor_tensor(g_gap, g_dump, g_dst, ALU.subtract).then_inc(s["g_tests"], 1)
                dve.wait_ge(s["g_tests"], t + 1)
                V.tensor_reduce(g_dup, g_before, AX.X, ALU.max).then_inc(s["g_dup_made"], 1)
                dve.wait_ge(s["g_dup_made"], t + 1)
                V.tensor_tensor(g_dup2, g_dup, g_pad, ALU.max).then_inc(s["g_dup2_made"], 1)
                dve.wait_ge(s["g_dup2_made"], t + 1)
                V.scalar_tensor_tensor(out=g_to, in0=g_gap, scalar=g_dup2, in1=g_dst, op0=ALU.mult, op1=ALU.add)\
                    .then_inc(s["g_to_made"], 1)
                dve.wait_ge(s["g_summed"], t + 1)
                V.tensor_copy(g_sum, pa[:, 1, 0:GW]).then_inc(s["g_taken"], 1)
                dve.wait_ge(s["g_added"], 16 * t + 16)
            with dve.Fori(0, GT) as t:
                dve.wait_ge(s["g_back_loaded"], 16 * t + 16)
                V.tensor_scalar(g_cnt, g_back[:, D:D + 1], 1.0, None, ALU.max).then_inc(s["g_cnt_made"], 1)
                dve.wait_ge(s["g_cnt_made"], t + 1)
                V.reciprocal(g_cnt, g_cnt).then_inc(s["g_rec_made"], 1)
                dve.wait_ge(s["g_rec_made"], t + 1)
                V.tensor_scalar(g_mean, g_back[:, 0:D], g_cnt, None, ALU.mult).then_inc(s["g_mean_made"], 1)
                dve.wait_ge(s["g_mean_made"], t + 1)
                for n in range(PARTS):
                    part = g_out[:, n * D:(n + 1) * D]
                    V.tensor_copy(part, g_mean).then_inc(s["g_split"], 1)
                    dve.wait_ge(s["g_split"], SPLITS * t + 2 * n + 1)
                    if n < PARTS - 1:
                        V.tensor_tensor(g_mean, g_mean, part, ALU.subtract).then_inc(s["g_split"], 1)
                        dve.wait_ge(s["g_split"], SPLITS * t + 2 * n + 2)
                dve.wait_ge(s["g_mean_stored"], 16 * t + 16)
            idx3, rel3 = (v.rearrange("p (b k) -> p b k", k=TB) for v in (idx, rel))
            V.memset(idx, 0)
            V.memset(rel, -1.0)
            V.tensor_scalar(g_p, g_dump, float(GT * P), None, ALU.subtract)
            V.tensor_copy(g_node, g_node_i).then_inc(s["g_index"], 1)
            dve.wait_ge(s["g_index"], 1)
            V.tensor_scalar(idx3[:, :, TILE_A], g_node, N - 1.0, None, ALU.min)
            V.tensor_scalar(idx3[:, :, TILE_B], g_node, float(P), N - 1.0, ALU.add, ALU.min)
            V.tensor_scalar(idx3[:, :, TILE_C], g_node, float(P), N - 1.0, ALU.add, ALU.min)
            V.tensor_scalar(g_ra, g_p, P - 1.0, None, ALU.is_lt)
            V.tensor_scalar(g_rc, g_p, P - 1.0, BN - LO[TILE_C], ALU.is_equal, ALU.mult)
            V.tensor_scalar(g_rb, g_p, 2.0, None, ALU.add).then_inc(s["g_index"], 1)
            dve.wait_ge(s["g_index"], 2)
            V.tensor_scalar(g_rc, g_rc, -1.0, None, ALU.add)
            V.tensor_tensor(g_rb, g_rb, g_ra, ALU.mult).then_inc(s["g_index"], 1)
            dve.wait_ge(s["g_index"], 3)
            V.tensor_scalar(g_rb, g_rb, -1.0, None, ALU.add).then_inc(s["g_index"], 1)
            dve.wait_ge(s["g_index"], 4)
            for tile, v in ((TILE_A, g_p), (TILE_B, g_rb), (TILE_C, g_rc)):
                ins = V.tensor_copy(rel3[:, :, tile], v.to_broadcast([P, NB]))
            ins.then_inc(s["g_replaced"], 1)
            dve.wait_ge(s["g_replaced"], 1)


        block = ctx.enter_context(nc.Block())

        @block.sync
        def _(sp):
            def edge_list(lst):
                full, rest = (NCH - 1) * P, ET - (NCH - 1) * P
                sp.dma_start(raw[:, 0:NCH - 1, :], lst[0:full * P].rearrange("(c p e) -> p c e", p=P, e=P))\
                    .then_inc(s["raw_loaded"], 16)
                sp.dma_start(raw[0:rest - 1, NCH - 1, :], lst[full * P:(ET - 1) * P].rearrange("(p e) -> p e", e=P))\
                    .then_inc(s["raw_loaded"], 16)
                sp.dma_start(raw[rest - 1:rest, NCH - 1, 0:E - (ET - 1) * P],
                             lst[(ET - 1) * P:E].rearrange("(a e) -> a e", a=1)).then_inc(s["raw_loaded"], 16)

            quad_io(sp, x, xin[0], 0, s["x_loaded0"], False)
            quad_io(sp, x, xin[1], 1, s["x_loaded1"], False)
            sp.wait_ge(s["raw_padded"], 1)
            edge_list(dst)

            def stage1(q, u):
                sp.wait_ge(s["xn_ready"], q + 1)
                if not (isinstance(q, int) and q + 2 > NQ):
                    quad_io(sp, x, xin[u], q + 2, s[f"x_loaded{u}"], False)
                sp.wait_ge(s["lo_made"], q + 1)
                quad_io(sp, xn_table, xp[u], q, s[f"xn_stored{u}"], True)

            def src_list():
                sp.wait_ge(s["raw_padded"], 2)
                edge_list(src)
            over_quads(sp, stage1, src_list)

            if_general(sp, general_sp)

            def stage3(b, u):
                if is_int(b, 0):
                    block_io(sp, x, xr, 0, s["xr_loaded"], False)
                    return
                d = b - 1
                sp.wait_ge(s["r0_made"], d + 1)
                if not is_int(b, NB):
                    block_io(sp, x, xr, b, s["xr_loaded"], False)
                sp.wait_ge(s["x1_made"], d + 1)
                block_io(sp, x1_rows, x1, d, s["x1_stored"], True)
                sp.wait_ge(s["y_made"], d + 1)
                block_io(sp, y_rows, yr, d, s["y_stored"], True)
            over_blocks(sp, stage3)

            sp.wait_ge(s["picked"], 1)
            for n in range(2):
                e = sp.value_load(pick[0:1, n:n + 1], min_val=0, max_val=NE - 1)
                sp.dma_start(W1_s[:, n, :, :], W1[bass.ds(e, 1), :, :].rearrange("a (c p) f -> p (a c) f", p=P))\
                    .then_inc(s["experts_loaded"], 16)
                sp.dma_start(W2_r[:, n * FC:(n + 1) * FC, :],
                             W2[bass.ds(e, 1), :, :].rearrange("a (c p) d -> p (a c) d", p=P))\
                    .then_inc(s["experts_loaded"], 16)
                sp.dma_start(b1_c[:, n, :], b1[bass.ds(e, 1), :].rearrange("a (c p) -> p (a c)", p=P),
                             allow_slow_non_contiguous=True)\
                    .then_inc(s["experts_loaded"], 16)
                sp.dma_start(b2_b[:, n, :], b2[bass.ds(e, 1), :].rearrange("a d -> (a d)").partition_broadcast(P))\
                    .then_inc(s["experts_loaded"], 16)
            sp.wait_ge(s["x1_stored"], block_dmas(NB - 1))
            sp.wait_ge(s["y_stored"], block_dmas(NB - 1))

            def stage5(q, u):
                if is_int(q, 0):
                    for v in range(2):
                        quad_io(sp, y_rows, y_in[v], v, s[f"yin_loaded{v}"], False)
                        quad_io(sp, x1_rows, x1_in[v], v, s[f"yin_loaded{v}"], False)
                sp.wait_ge(s["fin_made"], q + 1)
                quad_io(sp, out, x1_in[u], q, s[f"out_stored{u}"], True)
                if not (isinstance(q, int) and q + 2 > NQ):
                    quad_io(sp, y_rows, y_in[u], q + 2, s[f"yin_loaded{u}"], False)
                    sp.wait_ge(s[f"out_stored{u}"], quad_dmas(q, u))
                    quad_io(sp, x1_rows, x1_in[u], q + 2, s[f"yin_loaded{u}"], False)
            over_quads(sp, stage5)
            for u in range(2):
                sp.wait_ge(s[f"out_stored{u}"], quad_dmas(NQ - 1 + (u == 0), u))

        @block.gpsimd
        def _(pool):
            pool.iota(iota_i, pattern=[[1, WIN]], base=0, channel_multiplier=0).then_inc(s["iota_set"], 1)
            pool.iota(offs[:, :], pattern=[[BN, NB], [15, TB // 2], [7, 2]], base=LO[0], channel_multiplier=0)\
                .then_inc(s["iota_set"], 1)
            pool.memset(ident[:, :], 0.0).then_inc(s["ident_set"], 1)
            pool.wait_ge(s["ident_set"], 1)
            pool.affine_select(out=ident[:, :], in_=ident[:, :], compare_op=ALU.not_equal, fill=1.0, base=0,
                               pattern=[[-1, P]], channel_multiplier=1).then_inc(s["ident_set"], 1)
            for t, m in ((wq_s, wq), (wv_s, wv), (wo_s, wo), (wraw[0], W_l), (wraw[1], W_r), (Wr_s, Wr)):
                pool.dma_start(t[:, :, :], m.rearrange("(c p) n -> p c n", p=P)).then_inc(s["w_loaded"], 16)
            for t, v in ((bl_b, b_l), (bo_b, bo), (gamma_b, gamma), (beta_b, beta)):
                pool.dma_start(t[:, :], v.partition_broadcast(P)).then_inc(s["w_loaded"], 16)
            for t, v in ((bv_r, bv), (br_r, br)):
                pool.dma_start(t[:, :], v.rearrange("(a n) -> a n", a=1)).then_inc(s["w_loaded"], 16)
            pool.dma_start(bq_c[:, :], bq.rearrange("(c p) -> p c", p=P), allow_slow_non_contiguous=True)\
                .then_inc(s["w_loaded"], 16)

            def stage1(q, u):
                pool.wait_ge(s["xn_ready"], q + 1)
                wait(pool, s["lo_made"], q)
                pool.sem_inc(s["quad_started"], 1)
                for v, n in whole(q):
                    ins = pool.tensor_scalar(xs[0:n, v, :], xnb[u][0:n, v, 0:D], XS, None, ALU.mult)
                ins.then_inc(s["xs_made"], 1)
                pool.wait_ge(s["xs_made"], q + 1)
                pool.wait_ge(s["hi_made"], q + 1)
                for v, n in whole(q):
                    ins = pool.tensor_tensor(xp[u][0:n, v, D:2 * D], xs[0:n, v, :], xp[u][0:n, v, 0:D], ALU.subtract)
                ins.then_inc(s["lo_made"], 1)
            over_quads(pool, stage1)

            pool.wait_ge(s["xn_stored0"], quad_dmas(NQ, 0))
            pool.wait_ge(s["xn_stored1"], quad_dmas(NQ - 1, 1))
            if_general(pool, general_pool)

            def stage3(b, u):
                if is_int(b, NB):
                    return
                for q in range(NBT):
                    if not batch_tiles(b, q):
                        continue
                    pool.wait_ge(s["idx_ready"], NBT * b + q + 1)
                    wait(pool, s["batch_used"], NBT * (b - 1) + q + 1)
                    pool.sem_inc(s["batch_started"], 1)
                    for k in batch_tiles(b, q):
                        pool.indirect_dma_start(
                            out=msgs[:, k, :, :].rearrange("p s d -> p (s d)"), out_offset=None, in_=xn_table[:, :],
                            in_offset=bass.IndirectOffsetOnAxis(ap=idxb[:, k:k + 1], axis=0))\
                            .then_inc(s[f"gathered{q}"], 16)
            over_blocks(pool, stage3)

            def stage5(q, u):
                tail = is_int(q, NQ)
                n = len(TAILS) if tail else QT
                pool.wait_ge(s[f"yin_loaded{u}"], 2 * quad_dmas(q, u))
                if is_int(q, 0):
                    pool.wait_ge(s["b2_made"], 1)
                pool.tensor_tensor(y_in[u][:, 0:n, :], y_in[u][:, 0:n, :],
                                   b2m[:, :].unsqueeze(1).to_broadcast([P, n, D]), ALU.add).then_inc(s["yb_made"], 1)
                pool.tensor_tensor(x1_in[u][:, 0:n, :], x1_in[u][:, 0:n, :],
                                   beta_b[:, :].unsqueeze(1).to_broadcast([P, n, D]), ALU.add)\
                    .then_inc(s["xb_made"], 1)
            over_quads(pool, stage5)

        @block.scalar
        def _(act):
            def exp_keys(q, u):
                for pr in range(1 if is_int(q, NQ) else 2):
                    act.wait_ge(s["kb_made"], 2 * q + pr + 1)
                    nc.scalar.activation(ek[pr], kb1[pr], ACT.Exp, bias=minus1[:, :]).then_inc(s["ek_made"], 1)

            def normalise(q, u):
                tiles = list(enumerate(TAILS)) if is_int(q, NQ) else [(t, P) for t in range(QT)]
                act.wait_ge(s["p1_stats"], q + 1)
                if not (isinstance(q, int) and q < 2):
                    act.wait_ge(s["lo_made"], q - 1)
                    act.wait_ge(s["kx_done"], q - 1)
                for t, n in tiles:
                    col = q * QT + t
                    ins = nc.scalar.activation(xnb[u][0:n, t, 0:D], xin[u][0:n, t, :], ACT.Identity,
                                               bias=nmr_a[0:n, bass.ds(col, 1)], scale=rstd_a[0:n, bass.ds(col, 1)])
                ins.then_inc(s["xn_ready"], 1)
                act.wait_ge(s["xn_ready"], q + 1)
                if not (isinstance(q, int) and q < 2):
                    act.wait_ge(s[f"xn_stored{u}"], quad_dmas(q - 2, u))
                for v, n in whole(q):
                    ins = nc.scalar.activation(xp[u][0:n, v, 0:D], xnb[u][0:n, v, 0:D], ACT.Copy, scale=XS)
                ins.then_inc(s["hi_made"], 1)

            def take_turned(q, u):
                act.wait_ge(s["xt_turned"], q + 1)
                w = TAIL if is_int(q, NQ) else QR
                nc.scalar.activation(xTb[u][:, :, 0:w], pd[:, 0:2, 0:w], ACT.Copy).then_inc(s["xt_made"], 1)

            def stage1(q, u):
                exp_keys(q, u)
                if not is_int(q, NQ):
                    take_turned(q + 1, 1 - u)
                if not (isinstance(q, int) and q + 2 > NQ):
                    normalise(q + 2, u)

            act.dma_start(wk_s[:, :, :], wk.rearrange("(c p) n -> p c n", p=P)).then_inc(s["wk_loaded"], 16)
            act.dma_start(b1k_b[:, :], bk.partition_broadcast(P)).then_inc(s["wk_loaded"], 16)
            act.wait_ge(s["consts_set"], 1)
            normalise(0, 0)
            normalise(1, 1)
            take_turned(0, 0)
            over_quads(act, stage1)

            def indices(b, q):
                ks = batch_tiles(b, q)
                if not ks:
                    return
                if not is_int(b, 0):
                    act.wait_ge(s[f"gathered{q}"], batch_gathers(b - 1, q))
                nc.scalar.activation(idxb[:, ks[0]:ks[-1] + 1], idx[:, bass.ds(b * TB + ks[0], len(ks))], ACT.Copy)\
                    .then_inc(s["idx_ready"], 1)

            if_general(act, None)
            act.wait_ge(s["raw_taken"], 2 * math.ceil(NCH / 4))
            for q in range(NBT):
                indices(0, q)

            def stage3(b, u):
                if is_int(b, 0):
                    for q in range(NBT):
                        indices(1, q)
                    return
                d = b - 1
                tail = is_int(d, NB - 1)
                rows = list(enumerate(TAILS)) if tail else [(0, P), (1, P)]
                more = not (isinstance(b, int) and b + 1 >= NB)
                act.wait_ge(s["xr_loaded"], block_dmas(d))
                wait(act, s["r0_made"], d)
                for t, n in rows:
                    col = d * 2 + t
                    ins = nc.scalar.activation(xn2[0:n, t * D:(t + 1) * D], xr[0:n, t * D:(t + 1) * D], ACT.Identity,
                                               bias=nmr_a[0:n, bass.ds(col, 1)], scale=rstd_a[0:n, bass.ds(col, 1)])
                ins.then_inc(s["xn2_ready"], 1)
                act.wait_ge(s["xt2_turned"], d + 1)
                w = TAIL if tail else BN
                nc.scalar.activation(pair(xT2)[:, :, 0:w], pair(pd[:, 0, :])[:, :, 0:w], ACT.Copy)\
                    .then_inc(s["xt2_ready"], 1)
                if more:
                    indices(b + 1, 0)
                    indices(b + 1, 1)
                act.wait_ge(s["q_made"], d + 1)
                wait(act, s["qhat_made"], d)
                wait(act, s["o_made"], d)
                for c in range(C):
                    nc.scalar.activation(pq[:, c * BN:(c + 1) * BN], pd[:, 1, c * BN:(c + 1) * BN], ACT.Exp,
                                         bias=bq_c[:, c:c + 1])
                for c in range(C):
                    ins = nc.scalar.activation(qb[:, c * BN:(c + 1) * BN], pd[:, 1, c * BN:(c + 1) * BN],
                                               ACT.Identity, bias=bq1_c[:, c:c + 1])
                ins.then_inc(s["eq_made"], 1)
                if more:
                    indices(b + 1, 2)
                    indices(b + 1, 3)
                act.wait_ge(s["d_stats"], d + 1)
                wait(act, s["y_stored"], 16 * d)
                wait(act, s["yt_turned"], d)
                for t, n in rows:
                    ins = nc.scalar.activation(yr[0:n, t * D:(t + 1) * D], x1[0:n, t * D:(t + 1) * D], ACT.Identity,
                                               bias=nmr2[0:n, t:t + 1], scale=rstd2[0:n, t:t + 1])
                ins.then_inc(s["y_made"], 1)
                if more:
                    indices(b + 1, 4)
                    indices(b + 1, 5)
                act.wait_ge(s["yt_turned"], d + 1)
                w = TAIL if tail else BN
                for c in range(C):
                    ins = nc.scalar.activation(yT[:, bass.ds(d * C * BN + c * BN, w)], pd[:, 1, c * BN:c * BN + w],
                                               ACT.Copy, accum_out=ysum[:, c, bass.ds(d, 1)])
                ins.then_inc(s["yt_ready"], 1)
                if more:
                    indices(b + 1, 6)
                    indices(b + 1, 7)
            over_blocks(act, stage3)

            act.wait_ge(s["route_step"], ROUTE_EXP[0])
            nc.scalar.activation(rt[:, R_E1, :], rt[:, R_LG, :], ACT.Exp, bias=rt[:, R_MX1, 0:1],
                                 accum_out=rt[:, R_S1, 0:1]).then_inc(s["route_exp"], 1)
            act.wait_ge(s["route_step"], ROUTE_EXP[1])
            nc.scalar.activation(rt[:, R_E2, :], rt[:, R_RW, :], ACT.Exp, bias=rt[:, R_MX2, 0:1],
                                 accum_out=rt[:, R_S2, 0:1]).then_inc(s["route_exp"], 1)
            act.wait_ge(s["route_step"], ROUTE_EXP[2])
            nc.scalar.activation(rt[:, R_G, 1:2], rt[:, R_M, 2:3], ACT.Exp).then_inc(s["route_exp"], 1)

            def hidden(q, u):
                w = TAIL if is_int(q, NQ) else QR
                wait(act, s["o5_made"], 2 * q - 2)
                for f in range(NF):
                    act.wait_ge(s["h_made"], NF * q + f + 1)
                    nc.scalar.activation(hT[u][:, f, 0:w], hbank(f)[:, 0:w], ACT.Gelu,
                                         bias=b1_c[:, f // FC, f % FC:f % FC + 1]).then_inc(s["h_act"], 1)

            act.wait_ge(s["experts_loaded"], 16 * 8)
            hidden(0, 0)

            def stage5(q, u):
                if not is_int(q, NQ):
                    hidden(q + 1, 1 - u)
                act.wait_ge(s["f_stats"], q + 1)
                for t, n in (enumerate(TAILS) if is_int(q, NQ) else [(t, P) for t in range(QT)]):
                    ins = nc.scalar.activation(z[u][0:n, t, :], z[u][0:n, t, :], ACT.Identity,
                                               bias=nmr2[0:n, t:t + 1], scale=rstd2[0:n, t:t + 1])
                ins.then_inc(s["zn_made"], 1)
            over_quads(act, stage5)

        @block.tensor
        def _(pe):
            mm = nc.tensor.matmul

            def add_keys(q, u):
                tiles = list(enumerate(TAILS)) if is_int(q, NQ) else [(t, P) for t in range(QT)]
                for t, n in tiles:
                    if t % 2 == 0:
                        pe.wait_ge(s["phi_made"], 2 * q + t // 2 + 1)
                    for c in range(C):
                        ins = mm(pc[:, c, 0:KXW], phi[0:n, t, c * P:(c + 1) * P], xnb[u][0:n, t, :],
                                 start=is_int(q, 0) and t == 0, stop=is_int(q, NQ) and t == len(TAILS) - 1)
                ins.then_inc(s["kx_done"], 1)

            def stage1(q, u):
                tiles = list(enumerate(TAILS)) if is_int(q, NQ) else [(t, P) for t in range(QT)]
                pe.wait_ge(s["xn_ready"], q + 1)
                for t, n in tiles:
                    for c in range(C):
                        ins = nc.tensor.transpose(pd[:, c, t * P:t * P + n], xnb[u][0:n, t, c * P:(c + 1) * P],
                                                  ident[0:n, 0:n])
                ins.then_inc(s["xt_turned"], 1)
                if not is_int(q, 0):
                    add_keys(q - 1, 1 - u)
                else:
                    pe.wait_ge(s["wk_loaded"], 32)
                pe.wait_ge(s["xt_made"], q + 1)
                for pr in range(len(tiles) // 2):
                    for t, n in tiles[2 * pr:2 * pr + 2]:
                        for c in range(C):
                            ins = mm(pd[0:n, 2 + pr, (t % 2) * D:(t % 2 + 1) * D], xTb[u][:, c, t * P:t * P + n],
                                     wk_s[:, c, :], start=c == 0, stop=c == C - 1)
                    ins.then_inc(s["k_made"], 1)

            def turn_lists():
                for n in range(2):
                    pe.wait_ge(s["raw_float"], n + 1)
                    for g in range(NG):
                        wait(pe, s["raw_taken"], NG * n + g - 1)
                        for c in range(4 * g, min(4 * g + 4, NCH)):
                            ins = nc.tensor.transpose(pa[:, g % 2, (c % 4) * P:(c % 4 + 1) * P], rawf[:, c, :],
                                                      ident[:, :])
                        ins.then_inc(s["raw_turned"], 1)
                pe.wait_ge(s["raw_taken"], 2 * NG)
                pe.wait_ge(s["w_loaded"], W_LOADS)
                for n in range(2):
                    for o in range(C):
                        for c in range(C):
                            ins = nc.tensor.transpose(pa[:, n, c * D + o * P:c * D + (o + 1) * P],
                                                      wraw[n][:, o, c * P:(c + 1) * P], ident[:, :])
                ins.then_inc(s["wlr_turned"], 1)
                pe.wait_ge(s["flag_sum"], 1)
                pe.wait_ge(s["wlr_taken"], 1)
                mm(pa[0:1, 0, 0:1], cntp[:, 0:1], ones[:, 0:1], start=True, stop=True).then_inc(s["flag_added"], 1)

            pe.wait_ge(s["ident_set"], 2)
            pe.wait_ge(s["consts_set"], 1)
            over_quads(pe, stage1, turn_lists)
            add_keys(NQ, 0)

            pe.wait_ge(s["kx_taken"], 1)
            for c in range(C):
                for fc in range(C):
                    nc.tensor.transpose(pd[:, 0, fc * D + c * P:fc * D + (c + 1) * P],
                                        kx_s[:, c, fc * P:(fc + 1) * P], ident[:, :])
                ins = nc.tensor.transpose(pd[0:1, 1, c * P:(c + 1) * P], kx_s[:, c, D:D + 1], ident[:, :])
            ins.then_inc(s["kxT_made"], 1)
            pe.wait_ge(s["kxT_taken"], 1)
            for c in range(C):
                o = pd[:, 2, c * P:(c + 1) * P]
                for fc in range(C):
                    mm(o, wv_s[:, fc, c * P:(c + 1) * P], kxT[:, fc, c * P:(c + 1) * P], start=fc == 0, stop=False)
                ins = mm(o, bv_r[0:1, c * P:(c + 1) * P], ks_r[0:1, c * P:(c + 1) * P], start=False, stop=True)
            ins.then_inc(s["kv_made"], 1)
            pe.wait_ge(s["kv_taken"], 1)
            for c in range(C):
                ins = mm(pd[:, 3, c * D:(c + 1) * D], kvT[:, c, :], wo_s[:, c, :], start=True, stop=True)
            ins.then_inc(s["m_made"], 1)
            if_general(pe, general_pe)
            pe.wait_ge(s["m_taken"], 1)

            def turn_xn(d):
                pe.wait_ge(s["xn2_ready"], d + 1)
                wait(pe, s["nrm_eps"], d)
                for h in range(2):
                    n = TAILS[h] if is_int(d, NB - 1) else P
                    for c in range(C):
                        ins = nc.tensor.transpose(pd[:, 0, c * BN + h * P:c * BN + h * P + n],
                                                  xn2[0:n, h * D + c * P:h * D + (c + 1) * P], ident[0:n, 0:n])
                ins.then_inc(s["xt2_turned"], 1)

            def queries(d):
                pe.wait_ge(s["xt2_ready"], d + 1)
                wait(pe, s["yt_ready"], d)
                for o in range(C):
                    for c in range(C):
                        ins = mm(pd[:, 1, o * BN:(o + 1) * BN], wq_s[:, c, o * P:(o + 1) * P],
                                 xT2[:, c * BN:(c + 1) * BN], start=c == 0, stop=c == C - 1)
                ins.then_inc(s["q_made"], 1)

            def normalizers(d):
                pe.wait_ge(s["phq_made"], d + 1)
                for c in range(C):
                    ins = mm(pd[:, 0, c * BN:(c + 1) * BN], KS_s[:, c, :], pq[:, c * BN:(c + 1) * BN],
                             start=True, stop=True)
                ins.then_inc(s["nrm_made"], 1)

            def products(d):
                pe.wait_ge(s["agg_taken"], d + 1)
                pe.wait_ge(s["qhat_made"], d + 1)
                wait(pe, s["x1_made"], d)
                for h in range(2):
                    t = [(aggS, wlT), (xT2, wrT)]
                    for n, (a, w) in enumerate(t):
                        for c in range(C):
                            mm(pd[:, 2 + h, 0:D], a[:, c * BN + h * P:c * BN + (h + 1) * P], w[:, c, :],
                               start=n == 0 and c == 0, stop=n == 1 and c == C - 1)
                    for c in range(C):
                        ins = mm(pd[:, 2 + h, D:2 * D], pq[:, c * BN + h * P:c * BN + (h + 1) * P], M_s[:, c, :],
                                 start=c == 0, stop=c == C - 1)
                ins.then_inc(s["o_made"], 1)

            def turn_y(d):
                pe.wait_ge(s["y_made"], d + 1)
                for h in range(2):
                    n = TAILS[h] if is_int(d, NB - 1) else P
                    for c in range(C):
                        ins = nc.tensor.transpose(pd[:, 1, c * BN + h * P:c * BN + h * P + n],
                                                  yr[0:n, h * D + c * P:h * D + (c + 1) * P], ident[0:n, 0:n])
                ins.then_inc(s["yt_turned"], 1)

            HOOKS = {1: turn_xn, 5: queries, 10: normalizers, 18: products, 28: turn_y}

            def stage3(b, u):
                if is_int(b, NB):
                    for k in sorted(HOOKS):
                        HOOKS[k](b - 1)
                    return
                last_block = is_int(b, NB - 1)
                for q in range(NBT):
                    ks = batch_tiles(b, q)
                    for k in ks:
                        if k in HOOKS and not is_int(b, 0):
                            HOOKS[k](b - 1)
                        if k == ks[0]:
                            pe.wait_ge(s["oh_ready"], NBT * b + q + 1)
                            pe.wait_ge(s[f"gathered{q}"], batch_gathers(b, q))
                        slot = k % SLOTS
                        parts = []
                        for db in (-1, 0, 1):
                            c0, c1 = max(LO[k], db * BN), min(LO[k] + WIN, (db + 1) * BN)
                            if c0 < c1 and not (db < 0 and is_int(b, 0)) and not (db > 0 and last_block):
                                parts.append((db, c0 - db * BN, c1 - db * BN, c0 - LO[k]))
                        for db, c0, c1, o0 in parts:
                            v = (u + db) % 2
                            first = (db == 1 and LO[k - 1] + WIN <= BN) or (is_int(b, 0) and k == 0)
                            if db == 1 and first:
                                wait(pe, s["agg_taken"], b)
                            closing = (db == -1 and LO[k + 1] >= 0) or (last_block and k == LAST - 1)
                            o1 = o0 + c1 - c0
                            for c in range(C):
                                for part in range(PARTS):
                                    mm(pa[:, v, c * BN + c0:c * BN + c1], msgs[:, k, part, c * P:(c + 1) * P],
                                       oh[:, slot, o0:o1], start=first and c == 0 and part == 0, stop=closing,
                                       skip_group_check=True)
                            ins = mm(pc[:, v, c0:c1], ones_h[:, :], oh[:, slot, o0:o1], start=first, stop=closing,
                                     skip_group_check=True)
                            if closing:
                                ins.then_inc(s["agg_done"], 1)
                    if ks and not (last_block and ks[-1] == LAST - 1):
                        ins.then_inc(s["batch_used"], 1)
            over_blocks(pe, stage3)

            pe.wait_ge(s["mean_made"], 1)
            for c in range(C):
                ins = mm(pd[0:1, 0, 0:NE], mean_c[:, c:c + 1], Wr_s[:, c, :], start=c == 0, stop=c == C - 1)
            ins.then_inc(s["logits_made"], 1)
            pe.wait_ge(s["gates_made"], 1)
            mm(pd[:, 1, 0:2], ones[0:1, :], gates[0:1, :], start=True, stop=True).then_inc(s["gates_spread"], 1)

            def hidden(q, u):
                w = TAIL if is_int(q, NQ) else QR
                for f in range(NF):
                    wait(pe, s["h_act"], NF * q + f - 3)
                    e, fc = divmod(f, FC)
                    for c in range(C):
                        if is_int(q, NQ):
                            rhs, o = yT[:, q * 2 * C * BN + c * BN:q * 2 * C * BN + c * BN + w], hbank(f)[:, 0:w]
                        else:
                            rhs = yT[:, bass.ds(q * 2 * C * BN, 2 * C * BN)]\
                                .rearrange("p (b c t) -> p b c t", b=2, c=C)[:, :, c, :]
                            o = pair(hbank(f))
                        ins = mm(o, W1_s[:, e, c, fc * P:(fc + 1) * P], rhs, start=c == 0, stop=c == C - 1)
                    ins.then_inc(s["h_made"], 1)

            pe.wait_ge(s["experts_loaded"], 16 * 8)
            hidden(0, 0)

            def stage5(q, u):
                if not is_int(q, NQ):
                    hidden(q + 1, 1 - u)
                if is_int(q, 0):
                    pe.wait_ge(s["w2_scaled"], 2)
                    pe.wait_ge(s["gates_taken"], 1)
                pe.wait_ge(s["h_act"], NF * (q + 1))
                wait(pe, s["z_made"], 2 * q - 2)
                tiles = list(enumerate(TAILS)) if is_int(q, NQ) else [(t, P) for t in range(QT)]
                for t, n in tiles:
                    for f in range(NF):
                        ins = mm(pd[0:n, 2 * u + t // 2, (t % 2) * D:(t % 2 + 1) * D], hT[u][:, f, t * P:t * P + n],
                                 W2_s[:, f, :], start=f == 0, stop=f == NF - 1)
                    if t % 2:
                        ins.then_inc(s["o5_made"], 1)
            over_quads(pe, stage5)

        @block.vector
        def _(dve):
            V = nc.vector

            V.memset(minus1[:, :], -1.0)
            V.memset(ones_h[:, :], 1.0)
            V.memset(zeros[:, :], 0.0)
            V.memset(mv[:, :, :], 1.0)
            V.memset(mask, 0.0)
            V.memset(rel[:, NCH * P:TCOLS], -1.0)
            V.memset(idx[:, NCH * P:TCOLS], 0)
            for u in range(2):
                V.memset(xnb[u][:, :, D:KXW], 1.0)
            V.memset(ones[:, :], 1.0).then_inc(s["mask_step"], 1)
            dve.wait_ge(s["mask_step"], 1)
            for h in range(P // HD):
                ins = V.memset(mask[h * HD:(h + 1) * HD, h * HD:(h + 1) * HD], 1.0)
            ins.then_inc(s["consts_set"], 1)
            V.memset(raw[:, NCH - 1, :], -(1 << 20)).then_inc(s["raw_padded"], 1)
            dve.wait_ge(s["iota_set"], 2)
            V.tensor_copy(iota_f[:, :], iota_i).then_inc(s["iota_float"], 1)
            dve.wait_ge(s["wk_loaded"], 32)
            V.tensor_scalar(b1k_b[:, :], b1k_b[:, :], 1.0, None, ALU.add).then_inc(s["bias1_set"], 1)

            def row_stats(tiles, bn, m, r, done, value, rs, nm):
                wait(dve, s[done], value - 1)
                for t, (v, n) in enumerate(tiles):
                    ins = V.bn_stats(bst[0:n, t, :], v)
                ins.then_inc(s[bn], 1)
                dve.wait_ge(s[bn], value)
                dve.sem_inc(s["stats_read"], 1)
                for t, (v, n) in enumerate(tiles):
                    ins = V.bn_aggr(mv[0:n, t, :], bst[0:n, t, :])
                ins.then_inc(s[m], 1)
                dve.wait_ge(s[m], value)
                k = len(tiles)
                v, h, ys, yi = nv[:, 0:k], nh[:, 0:k], rs, ny[:, 0:k]
                chain = [RSQRT_STEPS * (value - 1)]

                def then(ins):
                    chain[0] = chain[0] + 1
                    ins.then_inc(s[r], 1)
                    dve.wait_ge(s[r], chain[0])
                then(V.tensor_scalar(v, mv[:, 0:k, 1], EPS, None, ALU.add))
                then(V.tensor_scalar(h.bitcast(I32), v.bitcast(I32), 1, None, ALU.logical_shift_right))
                then(V.tensor_scalar(yi.bitcast(I32), h.bitcast(I32), -1.0, float(0x5F3759DF), ALU.mult, ALU.add))
                for n in range(NEWTON):
                    then(V.tensor_tensor(h, yi, yi, ALU.mult))
                    then(V.scalar_tensor_tensor(out=h, in0=h, scalar=-0.5, in1=v, op0=ALU.mult, op1=ALU.mult))
                    then(V.scalar_tensor_tensor(out=ys if n == NEWTON - 1 else yi, in0=h, scalar=1.5, in1=yi,
                                                op0=ALU.add, op1=ALU.mult))
                V.scalar_tensor_tensor(out=nm, in0=mv[:, 0:k, 0], scalar=-1.0, in1=rs, op0=ALU.mult, op1=ALU.mult)\
                    .then_inc(s[done], 1)

            def keys(q):
                np_ = 1 if is_int(q, NQ) else 2
                wait(dve, s["phi_made"], 2 * q)
                for pr in range(np_):
                    dve.wait_ge(s["k_made"], 2 * q + pr + 1)
                    V.tensor_tensor(pair(kb1[pr]), pair(pd[:, 2 + pr, :]), bc(b1k_b[:, :], 2), ALU.add)\
                        .then_inc(s["kb_made"], 1)
                    dve.wait_ge(s["ek_made"], 2 * q + pr + 1)
                    V.scalar_tensor_tensor(out=phi[:, 2 * pr:2 * pr + 2, :], in0=pair(ek[pr]), scalar=1.0,
                                           in1=pair(kb1[pr]), op0=ALU.min, op1=ALU.max).then_inc(s["phi_made"], 1)

            def quad_stats(q, u):
                tiles = list(enumerate(TAILS)) if is_int(q, NQ) else [(t, P) for t in range(QT)]
                dve.wait_ge(s[f"x_loaded{u}"], quad_dmas(q, u))
                row_stats([(xin[u][0:n, t, :], n) for t, n in tiles], "p1_bn", "p1_mv", "p1_rstd", "p1_stats", q + 1,
                          rstd_a[:, bass.ds(q * QT, len(tiles))], nmr_a[:, bass.ds(q * QT, len(tiles))])

            def stage1(q, u):
                keys(q)
                if not (isinstance(q, int) and q + 2 > NQ):
                    quad_stats(q + 2, u)

            def take_lists():
                for n in range(2):
                    dve.wait_ge(s["raw_loaded"], 48 * (n + 1))
                    V.tensor_copy(rawf, raw).then_inc(s["raw_float"], 1)
                    if n == 0:
                        dve.wait_ge(s["raw_float"], 1)
                        V.memset(raw[:, NCH - 1, :], 0).then_inc(s["raw_padded"], 1)
                    for g in range(NG):
                        w = min(4, NCH - 4 * g) * P
                        cols = slice(4 * g * P, 4 * g * P + w)
                        dve.wait_ge(s["raw_turned"], NG * n + g + 1)
                        if n == 0:
                            ins = V.tensor_tensor(rel[:, cols], pa[:, g % 2, 0:w], offs[:, cols], ALU.subtract)
                        else:
                            ins = V.tensor_copy(idx[:, cols], pa[:, g % 2, 0:w])
                        ins.then_inc(s["raw_taken"], 1)
                dve.wait_ge(s["wlr_turned"], 1)
                V.tensor_copy(wlT[:, :, :], pair(pa[:, 0, :]))
                V.tensor_copy(wrT[:, :, :], pair(pa[:, 1, :])).then_inc(s["wlr_taken"], 1)
                dve.wait_ge(s["raw_taken"], 2 * NG)
                V.tensor_scalar(bq1_c[:, :], bq_c[:, :], 1.0, None, ALU.add)
                dve.wait_ge(s["raw_float"], 2)
                V.tensor_scalar(inside[0], rel, 0.0, None, ALU.is_ge).then_inc(s["flag_a"], 1)
                dve.wait_ge(s["flag_a"], 1)
                V.scalar_tensor_tensor(out=inside[1], in0=rel, scalar=WIN - 1.0, in1=inside[0], op0=ALU.is_le,
                                       op1=ALU.mult).then_inc(s["flag_b"], 1)
                dve.wait_ge(s["flag_b"], 1)
                V.tensor_reduce(cntp[:, :], inside[1], AX.X, ALU.add).then_inc(s["flag_sum"], 1)
                dve.wait_ge(s["flag_added"], 1)
                V.tensor_scalar(flag[:, :], pa[0:1, 0, 0:1], float(E), None, ALU.is_lt).then_inc(s["flag_set"], 1)
            quad_stats(0, 0)
            quad_stats(1, 1)
            dve.wait_ge(s["bias1_set"], 1)
            over_quads(dve, stage1, take_lists)

            dve.wait_ge(s["kx_done"], NQ + 1)
            V.tensor_copy(kx_s, pc[:, :, 0:KXW]).then_inc(s["kx_taken"], 1)
            dve.wait_ge(s["kx_taken"], 1)
            for c in range(C):
                V.tensor_scalar(KS_s[:, c, :], mask, kx_s[:, c, D:D + 1], None, ALU.mult)
            dve.wait_ge(s["kxT_made"], 1)
            V.tensor_copy(kxT, pair(pd[:, 0, :]))
            V.tensor_copy(ks_r, pd[0:1, 1, 0:D]).then_inc(s["kxT_taken"], 1)
            dve.wait_ge(s["kv_made"], 1)
            V.tensor_tensor(kvT, pair(pd[:, 2, 0:C * P]), bc(mask, 2), ALU.mult).then_inc(s["kv_taken"], 1)
            dve.wait_ge(s["m_made"], 1)
            V.tensor_copy(M_s[:, :, :], pair(pd[:, 3, :])).then_inc(s["m_taken"], 1)
            if_general(dve, general_dve)
            dve.wait_ge(s["iota_float"], 1)
            dve.wait_ge(s["raw_taken"], 2 * NG)
            dve.wait_ge(s["p1_stats"], NQ + 1)

            def one_hots(b, q):
                ks = batch_tiles(b, q)
                if not ks:
                    return
                wait(dve, s["batch_used"], NBT * b + q - NBT // 2 + 1)
                m, slot = len(ks), ks[0] % SLOTS
                where = rel[:, bass.ds(b * TB + ks[0], m)].unsqueeze(2).to_broadcast([P, m, WIN])
                V.tensor_tensor(oh[:, slot:slot + m, :], bc(iota_f[:, :], m), where, ALU.is_equal)\
                    .then_inc(s["oh_ready"], 1)

            def stage3(b, u):
                if is_int(b, 0):
                    for q in range(NBT):
                        one_hots(b, q)
                    return
                edges_left = not is_int(b, NB)
                d = b - 1
                if edges_left:
                    for q in range(NBT // 2):
                        one_hots(b, q)
                dve.wait_ge(s["eq_made"], d + 1)
                V.scalar_tensor_tensor(out=pq, in0=pq, scalar=1.0, in1=qb, op0=ALU.min, op1=ALU.max)\
                    .then_inc(s["phq_made"], 1)
                dve.wait_ge(s["xn2_ready"], d + 1)
                wait(dve, s["x1a_made"], d)
                V.tensor_tensor(r0, xr, xn2, ALU.add).then_inc(s["r0_made"], 1)
                dve.wait_ge(s["r0_made"], d + 1)
                V.tensor_tensor(pair(r0), pair(r0), bc(bo_b[:, :], 2), ALU.add).then_inc(s["r0b_made"], 1)
                dve.wait_ge(s["agg_done"], d + 1)
                wait(dve, s["o_made"], d)
                wait(dve, s["x1_made"], d)
                wait(dve, s["agg_taken"], d)
                V.tensor_scalar(rc[:, :], pc[:, 1 - u, 0:BN], 1.0, XS, ALU.max, ALU.mult).then_inc(s["cnt_max"], 1)
                dve.wait_ge(s["cnt_max"], d + 1)
                V.reciprocal(rc[:, :], rc[:, :]).then_inc(s["cnt_rec"], 1)
                dve.wait_ge(s["cnt_rec"], d + 1)
                V.tensor_tensor(pair(aggS), pair(pa[:, 1 - u, :]), bc(rc[:, :], 2), ALU.mult)\
                    .then_inc(s["agg_taken"], 1)
                dve.wait_ge(s["nrm_made"], d + 1)
                V.tensor_scalar(qb, pd[:, 0, :], 1e-6, None, ALU.add).then_inc(s["nrm_eps"], 1)
                dve.wait_ge(s["nrm_eps"], d + 1)
                V.reciprocal(qb, qb).then_inc(s["nrm_rec"], 1)
                dve.wait_ge(s["nrm_rec"], d + 1)
                V.tensor_tensor(pq, pq, qb, ALU.mult).then_inc(s["qhat_made"], 1)
                if edges_left:
                    for q in range(NBT // 2, NBT):
                        one_hots(b, q)
                dve.wait_ge(s["o_made"], d + 1)
                V.tensor_tensor(pair(aggS), pd[:, 2:4, 0:D], bc(bl_b[:, :], 2), ALU.add).then_inc(s["g1_made"], 1)
                dve.wait_ge(s["g1_made"], d + 1)
                dve.wait_ge(s["r0b_made"], d + 1)
                V.scalar_tensor_tensor(out=aggS, in0=aggS, scalar=0.0, in1=r0, op0=ALU.max, op1=ALU.add)\
                    .then_inc(s["x1a_made"], 1)
                dve.wait_ge(s["x1a_made"], d + 1)
                wait(dve, s["x1_stored"], 16 * d)
                wait(dve, s["y_made"], d)
                V.tensor_tensor(pair(x1), pair(aggS), pd[:, 2:4, D:2 * D], ALU.add).then_inc(s["x1_made"], 1)
                dve.wait_ge(s["x1_made"], d + 1)
                rows = TAILS if is_int(d, NB - 1) else [P, P]
                row_stats([(x1[0:n, t * D:(t + 1) * D], n) for t, n in enumerate(rows)],
                          "d_bn", "d_mv", "d_rstd", "d_stats", d + 1, rstd2[:, 0:2], nmr2[:, 0:2])
            over_blocks(dve, stage3)

            dve.wait_ge(s["yt_ready"], NB)
            V.tensor_reduce(ysr[:, :], ysum[:, :, :], AX.X, ALU.add).then_inc(s["ysum_made"], 1)
            dve.wait_ge(s["ysum_made"], 1)
            V.tensor_scalar(mean_c[:, :], ysr[:, :], 1.0 / N, None, ALU.mult).then_inc(s["mean_made"], 1)
            V.tensor_copy(rt[:, R_IO, :], iota_f[0:1, 0:NE])
            steps = [0]

            def step(ins):
                steps[0] += 1
                ins.then_inc(s["route_step"], 1)
                dve.wait_ge(s["route_step"], steps[0])

            def row(n, w=NE, at=0):
                return rt[:, n, at:at + w]
            dve.wait_ge(s["logits_made"], 1)
            step(V.tensor_tensor(row(R_LG), pd[0:1, 0, 0:NE], br_r[:, :], ALU.add))
            step(V.tensor_reduce(row(R_MX1, 1), row(R_LG), AX.X, ALU.max))
            step(V.tensor_scalar(row(R_MX1, 1), row(R_MX1, 1), -1.0, None, ALU.mult))
            assert steps[0] == ROUTE_EXP[0]
            dve.wait_ge(s["route_exp"], 1)
            step(V.reciprocal(row(R_S1, 1), row(R_S1, 1)))
            step(V.tensor_scalar(row(R_RW), row(R_E1), row(R_S1, 1), CAP / N, ALU.mult, ALU.min))
            step(V.tensor_reduce(row(R_MX2, 1), row(R_RW), AX.X, ALU.max))
            step(V.tensor_scalar(row(R_MX2, 1), row(R_MX2, 1), -1.0, None, ALU.mult))
            assert steps[0] == ROUTE_EXP[1]
            dve.wait_ge(s["route_exp"], 2)
            step(V.reciprocal(row(R_S2, 1), row(R_S2, 1)))
            step(V.tensor_scalar(row(R_W), row(R_E2), row(R_S2, 1), None, ALU.mult))
            step(V.tensor_reduce(row(R_M, 1), row(R_W), AX.X, ALU.max))

            def first_at(values, largest, n):
                step(V.tensor_scalar(row(R_T), values, largest, float(NE), ALU.is_lt, ALU.mult))
                step(V.tensor_tensor(row(R_U), row(R_T), row(R_IO), ALU.add))
                step(V.tensor_reduce(row(R_I, 1, n), row(R_U), AX.X, ALU.min))
            first_at(row(R_W), row(R_M, 1), 0)
            step(V.tensor_scalar(row(R_T), row(R_IO), row(R_I, 1), -2.0, ALU.is_equal, ALU.mult))
            step(V.tensor_tensor(row(R_W2), row(R_W), row(R_T), ALU.add))
            step(V.tensor_reduce(row(R_M, 1, 1), row(R_W2), AX.X, ALU.max))
            first_at(row(R_W2), row(R_M, 1, 1), 1)
            step(V.tensor_tensor(row(R_M, 1, 2), row(R_M, 1, 1), row(R_M, 1, 0), ALU.subtract))
            V.tensor_copy(pick[:, :], row(R_I, 2)).then_inc(s["picked"], 1)
            step(V.tensor_scalar(row(R_G, 1, 2), row(R_M, 1, 2), 1.0, None, ALU.mult))
            assert steps[0] == ROUTE_EXP[2]
            dve.wait_ge(s["route_exp"], 3)
            step(V.tensor_scalar(row(R_G, 1), row(R_G, 1, 1), 1.0, None, ALU.add))
            step(V.reciprocal(gates[:, 0:1], row(R_G, 1)))
            V.tensor_tensor(gates[:, 1:2], gates[:, 0:1], row(R_G, 1, 1), ALU.mult).then_inc(s["gates_made"], 1)
            dve.wait_ge(s["gates_spread"], 1)
            V.tensor_copy(gate_b[:, :], pd[:, 1, 0:2]).then_inc(s["gates_taken"], 1)
            dve.wait_ge(s["gates_taken"], 1)
            dve.wait_ge(s["experts_loaded"], 16 * 8)
            for e in range(2):
                V.tensor_scalar(W2_s[:, e * FC:(e + 1) * FC, :], W2_r[:, e * FC:(e + 1) * FC, :], gate_b[:, e:e + 1],
                                None, ALU.mult).then_inc(s["w2_scaled"], 1)
            V.tensor_scalar(b2a, b2_b[:, 0, :], gate_b[:, 0:1], None, ALU.mult).then_inc(s["b2_step"], 1)
            dve.wait_ge(s["b2_step"], 1)
            V.scalar_tensor_tensor(out=b2m, in0=b2_b[:, 1, :], scalar=gate_b[:, 1:2], in1=b2a, op0=ALU.mult,
                                   op1=ALU.add).then_inc(s["b2_made"], 1)
            dve.wait_ge(s["w2_scaled"], 2)

            def finish(q, u):
                n = len(TAILS) if is_int(q, NQ) else QT
                dve.wait_ge(s["zn_made"], q + 1)
                V.tensor_tensor(z[u][:, 0:n, :], z[u][:, 0:n, :], bc(gamma_b[:, :], n), ALU.mult)\
                    .then_inc(s["f_scaled"], 1)
                dve.wait_ge(s["f_scaled"], q + 1)
                dve.wait_ge(s["xb_made"], q + 1)
                V.tensor_tensor(x1_in[u][:, 0:n, :], x1_in[u][:, 0:n, :], z[u][:, 0:n, :], ALU.add)\
                    .then_inc(s["fin_made"], 1)

            def stage5(q, u):
                tiles = list(enumerate(TAILS)) if is_int(q, NQ) else [(t, P) for t in range(QT)]
                dve.wait_ge(s["yb_made"], q + 1)
                wait(dve, s["fin_made"], q - 1)
                for pr in range(len(tiles) // 2):
                    dve.wait_ge(s["o5_made"], 2 * q + pr + 1)
                    V.tensor_tensor(z[u][:, 2 * pr:2 * pr + 2, :], pair(pd[:, 2 * u + pr, :]),
                                    y_in[u][:, 2 * pr:2 * pr + 2, :], ALU.add).then_inc(s["z_made"], 1)
                dve.wait_ge(s["z_made"], 2 * q + len(tiles) // 2)
                if not is_int(q, 0):
                    wait(dve, s["zn_made"], q)
                row_stats([(z[u][0:n, t, :], n) for t, n in tiles], "f_bn", "f_mv", "f_rstd", "f_stats", q + 1,
                          rstd2[:, 0:len(tiles)], nmr2[:, 0:len(tiles)])
                if not is_int(q, 0):
                    finish(q - 1, 1 - u)
            over_quads(dve, stage5)
            finish(NQ, 0)


_INS = ["x", "src", "dst", "L0_gnn_W_l", "L0_gnn_b_l", "L0_gnn_W_r", "L0_mix_wq", "L0_mix_bq", "L0_mix_wk", "L0_mix_bk",
        "L0_mix_wv", "L0_mix_bv", "L0_mix_wo", "L0_mix_bo", "L0_ffn_Wr", "L0_ffn_br", "L0_ffn_W1", "L0_ffn_b1",
        "L0_ffn_W2", "L0_ffn_b2", "L0_ffn_gamma", "L0_ffn_beta"]


def kernel(**inputs):
    import numpy as np
    import concourse.bacc as bacc
    from concourse.bass_utils import run_bass_kernel_spmd

    nc = bacc.Bacc("TRN2", target_bir_lowering=False, num_devices=1)
    arrays, args = {}, []
    for name in _INS:
        a = np.ascontiguousarray(inputs[name])
        arrays[f"in_{name}"] = a
        args.append(nc.dram_tensor(f"in_{name}", a.shape, mybir.dt.from_np(a.dtype), kind="ExternalInput").ap())
    out = nc.dram_tensor("out", inputs["x"].shape, F32, kind="ExternalOutput").ap()
    build_layer(nc, *args, out)
    r = run_bass_kernel_spmd(nc, [arrays], core_ids=[0])
    return r.results[0]["out"]
```

```python
import math
from contextlib import ExitStack

import concourse.bass as bass
from concourse import mybir

F32 = mybir.dt.float32
F16 = mybir.dt.float16
F32R = mybir.dt.float32r
I32 = mybir.dt.int32
ALU = mybir.AluOpType
ACT = mybir.ActivationFunctionType
AX = mybir.AxisListType

P = 128
EPS = 1e-5


def wait(eng, sem, value):
    if not (isinstance(value, int) and value <= 0):
        eng.wait_ge(sem, value)


def build_layer(nc, x, src, dst, W_l, b_l, W_r, wq, bq, wk, bk, wv, bv, wo, bo,
                Wr, br, W1, b1, W2, b2, gamma, beta, out):
    N, D = x.shape
    E = src.shape[0]
    NE, _, F = W1.shape
    C = D // P
    HD = D // 8
    FC = F // P
    NF = 2 * FC
    QT = 4
    QR = QT * P
    NQ = N // QR
    TAIL = N - NQ * QR
    TAILS = [min(P, TAIL - P * s) for s in range(math.ceil(TAIL / P))]
    BN = 2 * P
    NB = math.ceil(N / BN)
    ET = math.ceil(E / P)
    TB = 34
    LAST = ET - (NB - 1) * TB
    NCH = math.ceil(ET / P)
    TCOLS = NB * TB
    BATCH = [(0, 4), (4, 8), (8, 12), (12, 17), (17, 21), (21, 25), (25, 29), (29, 34)]
    NBT = len(BATCH)
    SLOTS = TB // 2
    PARTS = 2
    XS = 2048.0
    RING = 12992
    WIN = P
    LO = [15 * (k // 2) + 7 * (k % 2) - 60 for k in range(TB)]
    CAP = float(math.ceil(N * 1.25 / NE))
    GW = D + 4
    GT = math.ceil(N / P)
    assert TAIL > 0 and len(TAILS) == 2 and NQ % 2 == 0 and NB % 2 == 1 and BN * (NB - 1) == NQ * QR

    xn_table = nc.dram_tensor("xn_table", (N, PARTS * D), F16).ap()
    y_rows = nc.dram_tensor("y_rows", (N, D), F32).ap()
    x1_rows = nc.dram_tensor("x1_rows", (N, D), F32).ap()
    sum_rows = nc.dram_tensor("sum_rows", ((GT + 1) * P, GW), F32).ap()

    with ExitStack() as ctx:
        def sb(name, shape, dtype=F32):
            return ctx.enter_context(nc.sbuf_tensor(name, shape, dtype))

        def sem(name):
            return ctx.enter_context(nc.semaphore(name))

        YT = NB * C * BN - (BN - TAIL)
        yT = sb("yT", [P, YT])
        with nc.sbuf_tensor("mats", [P, 6 * C * D], F32) as mats, nc.sbuf_tensor("edges", [P, 2 * TCOLS], F32) as edges, \
                nc.sbuf_tensor("ring", [P, RING], F32) as ring:
            pass
        W1_lo_t = sb("W1_lo_t", [P, 2 * C * F], F32R)
        sb("rest_of_mats", [P, 6 * C * D - 2 * C * F])
        W2_lo_t = sb("W2_lo_t", [P, NF * D], F32R)
        sb("rest_of_edges", [P, 2 * TCOLS - NF * D])
        HS = 4
        PART_WORDS = 2 * C * F + NF * D + 4 * C * QR + 2 * HS * QR
        parts = sb("parts", [P, PART_WORDS], F32R)
        sb("rest_of_ring", [P, RING - PART_WORDS])
        ohh = sb("ohh", [P, SLOTS * WIN], F16)
        work = sb("work", [P, 9 * 512])
        bl_b, bo_b, gamma_b, beta_b = sb("bl_b", [P, D]), sb("bo_b", [P, D]), sb("gamma_b", [P, D]), sb("beta_b", [P, D])
        M_s, KS_s = sb("M_s", [P, C, D]), sb("KS_s", [P, C, P])
        Wr_s = sb("Wr_s", [P, C, NE])
        bq_c, bq1_c = sb("bq_c", [P, C]), sb("bq1_c", [P, C])
        br_r = sb("br_r", [1, NE])
        ident, ones = sb("ident", [P, P]), sb("ones", [P, P])
        ones_h = sb("ones_h", [P, P], F16)
        iota_f = sb("iota_f", [P, WIN])
        rstd_a, nmr_a = sb("rstd_a", [P, (NQ + 1) * QT]), sb("nmr_a", [P, (NQ + 1) * QT])
        ysum = sb("ysum", [P, C, NB])
        flag = sb("flag", [1, 1], I32)
        cntp = sb("cntp", [P, 1])
        idxb = sb("idxb", [P, TB], I32)
        mv, bst = sb("mv", [P, QT, 2]), sb("bst", [P, QT, 6])
        rstd2, nmr2 = sb("rstd2", [P, QT]), sb("nmr2", [P, QT])
        rc = sb("rc", [P, BN])

        idx = edges[:, 0:TCOLS].bitcast(I32)
        rel = edges[:, TCOLS:2 * TCOLS]

        def mat(n):
            return mats[:, n * C * D:(n + 1) * C * D].rearrange("p (c d) -> p c d", c=C)
        wk_s, wq_s, wv_s, wo_s, wlT, wrT = (mat(n) for n in range(6))
        msgs = ring[:, 0:TB * PARTS * D // 2].bitcast(F16).rearrange("p (k s d) -> p k s d", s=PARTS, d=D)
        oh = ohh[:, :].rearrange("p (k w) -> p k w", w=WIN)

        at = {"yT": 8 * C * BN, "ring": 0}

        def early(n, whole="yT"):
            at[whole] += n
            return (yT if whole == "yT" else ring)[:, at[whole] - n:at[whole]]
        KXW = D + 1
        xin = [early(QT * D).rearrange("p (s d) -> p s d", d=D) for _ in range(2)]
        xnb = [early(QT * KXW).rearrange("p (s d) -> p s d", d=KXW) for _ in range(2)]
        xTb = [early(C * QR).rearrange("p (c t) -> p c t", c=C) for _ in range(2)]
        xp = [early(QT * PARTS * D // 2, "ring").bitcast(F16).rearrange("p (s d) -> p s d", d=PARTS * D) for _ in range(2)]
        xs = early(QT * D, "ring").rearrange("p (s d) -> p s d", d=D)
        kb1 = [early(2 * D) for _ in range(2)]
        ek = [early(2 * D) for _ in range(2)]
        phi = early(QT * D).rearrange("p (s d) -> p s d", d=D)
        kx_s = early(C * KXW).rearrange("p (c d) -> p c d", c=C)
        kxT = early(C * D).rearrange("p (c d) -> p c d", c=C)
        ks_r = early(D)[0:1, :]
        kvT = early(C * P).rearrange("p (c d) -> p c d", c=C)
        inside = [early(TCOLS) for _ in range(2)]
        raw = inside[0][:, 0:NCH * P].bitcast(I32).rearrange("p (c e) -> p c e", e=P)
        rawf = inside[1][:, 0:NCH * P].rearrange("p (c e) -> p c e", e=P)
        offs = early(TCOLS, "ring").bitcast(I32)
        b1k_b = early(D)
        bv_r = early(D)[0:1, :]
        mask = early(P)
        warm = early(1)
        iota_i = early(WIN).bitcast(I32)
        zeros = early(GW, "ring")
        wraw = [early(C * D).rearrange("p (c d) -> p c d", c=C) for _ in range(2)]
        g_parts = early(PARTS * D // 2, "ring").bitcast(F16)
        g_row = early(GW, "ring")
        g_src = early(1, "ring").bitcast(I32)
        g_dst = early(1, "ring")
        g_dsts = early(P, "ring")
        g_same = early(P, "ring")
        g_before = early(P, "ring")
        g_later = early(P, "ring")
        g_dup, g_pad, g_dup2, g_gap, g_dump = (early(1, "ring") for _ in range(5))
        g_dump_i, g_to = early(1, "ring").bitcast(I32), early(1, "ring").bitcast(I32)
        g_sum = early(GW, "ring")
        g_back = early(GW, "ring")
        g_cnt = early(1, "ring")
        g_mean = early(D, "ring")
        g_out = early(PARTS * D // 2, "ring").bitcast(F16)
        g_node_i, g_node = early(NB, "ring").bitcast(I32), early(NB, "ring")
        g_p, g_ra, g_rb, g_rc = (early(1, "ring") for _ in range(4))
        assert at["yT"] <= YT and at["ring"] <= RING

        xr, xn2, xT2, pq, qb, aggS, r0, x1, yr = (work[:, n * 512:(n + 1) * 512] for n in range(9))
        late_at = [0, PART_WORDS]

        def late(n, dtype=F32):
            k = 0 if dtype == F32R else 1
            late_at[k] += n
            return (parts, ring)[k][:, late_at[k] - n:late_at[k]]

        def w1(v):
            return v.rearrange("p (e c f) -> p e c f", e=2, c=C)

        def w2(v):
            return v.rearrange("p (f d) -> p f d", d=D)
        W1_s, W2_s = w1(mats[:, 0:2 * C * F]), w2(edges[:, 0:NF * D])
        W1_lo, W2_lo = w1(W1_lo_t[:, :]), w2(W2_lo_t[:, :])
        W1_hi, W2_hi = w1(late(2 * C * F, F32R)), w2(late(NF * D, F32R))
        y_hi, y_lo = ([late(C * QR, F32R).rearrange("p (c t) -> p c t", c=C) for _ in range(2)] for _ in range(2))
        h_hi, h_lo = ([late(QR, F32R) for _ in range(HS)] for _ in range(2))
        h_full = [late(QR), M_s[:, :, :].rearrange("p c d -> p (c d)")]
        rt = late(16 * NE)[0:1, :].rearrange("a (r n) -> a r n", n=NE)
        ysr, mean_c, gate_b = (late(C) for _ in range(3))
        gates, pick = late(2)[0:1, :], late(2)[0:1, :].bitcast(I32)
        b1_c = late(2 * FC).rearrange("p (e f) -> p e f", e=2)
        assert late_at[0] == PART_WORDS and late_at[1] <= RING
        z = [t.rearrange("p (s d) -> p s d", d=D)
             for t in (mats[:, 2 * C * F:2 * C * F + QT * D], edges[:, NF * D:NF * D + QT * D])]
        b2_b = ohh[:, 0:4 * D].bitcast(F32).rearrange("p (e d) -> p e d", e=2)
        b2a = ohh[:, 4 * D:6 * D].bitcast(F32)
        b2m = ohh[:, 6 * D:8 * D].bitcast(F32)
        y_in = [work[:, u * QT * D:(u + 1) * QT * D].rearrange("p (s d) -> p s d", d=D) for u in range(2)]
        x1_in = [work[:, (2 + u) * QT * D:(3 + u) * QT * D].rearrange("p (s d) -> p s d", d=D) for u in range(2)]

        pa = ctx.enter_context(nc.psum_tensor("pa", [P, 2, 512], F32))
        pc = ctx.enter_context(nc.psum_tensor("pc", [P, 2, 512], F32))
        pd = ctx.enter_context(nc.psum_tensor("pd", [P, 4, 512], F32))

        names = """waits_taken iota_set iota_float mask_step wk_loaded consts_set ident_set raw_padded raw_loaded raw_float raw_turned raw_taken
            flag_a flag_b flag_sum flag_added flag_set w_loaded biases_loaded wlr_turned wlr_taken bias1_set
            x_loaded0 x_loaded1 p1_bn p1_mv p1_rstd p1_stats xs_made hi_made lo_made xn_ready xn_stored0 xn_stored1 xt_turned xt_made
            k_made kb_made ek_made phi_made kx_done kx_taken kxT_made kxT_taken kv_made kv_taken m_made m_taken
            idx_ready gathered0 gathered1 gathered2 gathered3 gathered4 gathered5
            gathered6 gathered7 oh_ready batch_used agg_done agg_taken
            xr_loaded xn2_ready xt2_turned xt2_ready q_made eq_made phq_made nrm_made nrm_eps nrm_rec qhat_made
            cnt_max cnt_rec r0_made r0b_made o_made g1_made x1a_made x1_made d_bn d_mv d_rstd d_stats
            y_made yt_turned yt_ready x1_stored y_stored
            route_step route_exp logits_made ysum_made mean_made picked gates_made gates_spread gates_taken
            w1_loaded0 w1_loaded1 w2_loaded0 w2_loaded1 b2_loaded w1_hi_made w1_split w2_hi_made w2_split yh_made yl_made hh_made hl_made
            l2_done b2_step b2_made yin_loaded0 yin_loaded1 yb_made xb_made
            h_made h_act o5_made z_made f_bn f_mv f_rstd f_stats zn_made f_scaled fin_made out_stored0 out_stored1
            g_iota g_zeroed g_src_set g_loaded g_row_made g_split g_to_made g_taken g_added g_back_loaded g_mean_made g_mean_stored
            g_replaced g_done g_dsts_made g_turned g_same_made g_summed g_consts g_tests g_dup_made g_dup2_made
            g_cnt_made g_rec_made g_index""".split()
        s = {n: sem(n) for n in names}

        def quad_rows(table, q):
            return table[bass.ds(q * QR, QR), :].rearrange("(s p) d -> p s d", p=P)

        def quad_io(eng, table, tile, q, signal, store):
            if isinstance(q, int) and q == NQ:
                pairs = [(tile[0:n, t, :], table[q * QR + t * P:q * QR + t * P + n, :]) for t, n in enumerate(TAILS)]
            else:
                pairs = [(tile[:, :, :], quad_rows(table, q))]
            for a, b in pairs:
                (eng.dma_start(b, a) if store else eng.dma_start(a, b)).then_inc(signal, 16)

        def quad_dmas(q, u):
            if isinstance(q, int) and q == NQ:
                return 16 * (NQ // 2 + len(TAILS))
            return (q - u) * 8 + 16

        def block_io(eng, table, tile, d, signal, store):
            t3 = tile.rearrange("p (s d) -> p s d", d=D)
            if isinstance(d, int) and d == NB - 1:
                pairs = [(t3[0:n, t, :], table[d * BN + t * P:d * BN + t * P + n, :]) for t, n in enumerate(TAILS)]
            else:
                pairs = [(t3, table[bass.ds(d * BN, BN), :].rearrange("(s p) d -> p s d", p=P))]
            for a, b in pairs:
                (eng.dma_start(b, a) if store else eng.dma_start(a, b)).then_inc(signal, 16)

        def block_dmas(d):
            return 16 * (d + len(TAILS)) if isinstance(d, int) and d == NB - 1 else 16 * (d + 1)

        def over_quads(eng, body, peeled=2, after=None):
            def single(q):
                body(q, q % 2)
                if after:
                    after(q)
            for q in range(peeled):
                single(q)
            with eng.Fori(peeled // 2, NQ // 2 - 1) as i:
                body(2 * i, 0)
                body(2 * i + 1, 1)
            for q in range(NQ - 2, NQ + 1):
                single(q)

        LISTS = 6

        def over_blocks(eng, body):
            for b in range(3):
                body(b, b % 2)
            with eng.Fori(1, (NB - 3) // 2) as i:
                body(2 * i + 1, 1)
                body(2 * i + 2, 0)
            for b in range(NB - 2, NB + 1):
                body(b, b % 2)

        def batch_tiles(b, q):
            k0, k1 = BATCH[q]
            return range(k0, min(k1, LAST) if isinstance(b, int) and b == NB - 1 else k1)

        def batch_gathers(b, q):
            k0, k1 = BATCH[q]
            if isinstance(b, int) and b == NB - 1:
                return 16 * ((k1 - k0) * b + len(batch_tiles(b, q)))
            return 16 * (k1 - k0) * (b + 1)

        def is_int(v, n):
            return isinstance(v, int) and v == n

        def whole(q):
            return [(slice(t, t + 1), n) for t, n in enumerate(TAILS)] if is_int(q, NQ) else [(slice(0, QT), P)]

        minus1 = sb("minus1", [P, 1])
        nv, nh, ny = sb("nv", [P, QT]), sb("nh", [P, QT]), sb("ny", [P, QT])
        NEWTON = 3
        RSQRT_STEPS = 3 + 3 * NEWTON
        (R_LG, R_E1, R_RW, R_E2, R_W, R_T, R_W2, R_IO, R_MX1, R_S1, R_MX2, R_S2, R_M, R_I, R_G, R_U) = range(16)
        ROUTE_EXP = (3, 7, 21)
        W_LOADS, B_LOADS = 16 * 6, 16 * 7
        NG = math.ceil(NCH / 4)

        def hbank(f):
            return (pa if f % 4 < 2 else pc)[:, f % 2, :]

        def y_quad(part, q):
            at = q * 2 * C * BN
            if is_int(q, NQ):
                return [(part[:, c, 0:TAIL], yT[:, at + c * BN:at + c * BN + TAIL]) for c in range(C)]
            return [(part.rearrange("p c (b t) -> p b c t", b=2),
                     yT[:, bass.ds(at, 2 * C * BN)].rearrange("p (b c t) -> p b c t", b=2, c=C))]

        def l2_chunks(q, f):
            return (NF - 1) * q + f + 1 if f >= 0 else (NF - 1) * (q - 1) + NF + f + 1

        def bc(v, n):
            return v.unsqueeze(1).to_broadcast([P, n, v.shape[1]])

        def pair(v):
            return v.rearrange("p (a d) -> p a d", a=2)

        def if_general(eng, program):
            eng.wait_ge(s["flag_set"], 1)
            bad = eng.value_load(flag[0:1, 0:1], min_val=0, max_val=1)
            with eng.If(bad):
                if program:
                    program(eng)
                eng.wait_ge(s["g_done"], 1)

        TILE_A, TILE_B, TILE_C = LO.index(0), 25, 26
        assert LO[TILE_B] == P - 1 and LO[TILE_C] > P - 1 and TILE_C < min(LAST, TB)

        SPLITS = 2 * PARTS - 1

        general_sp = None

        def general_pool(pool):
            pool.iota(g_dump_i, pattern=[[0, 1]], base=GT * P, channel_multiplier=1).then_inc(s["g_iota"], 1)
            pool.iota(g_node_i, pattern=[[BN, NB]], base=0, channel_multiplier=1).then_inc(s["g_iota"], 1)
            pool.affine_select(out=g_later, in_=ones[:, :], compare_op=ALU.is_gt, fill=0.0, base=0,
                               pattern=[[-1, P]], channel_multiplier=1).then_inc(s["g_iota"], 1)
            with pool.Fori(0, GT + 1) as t:
                pool.dma_start(sum_rows[bass.ds(t * P, P), :], zeros[:, :]).then_inc(s["g_zeroed"], 16)
            pool.wait_ge(s["g_zeroed"], 16 * (GT + 1))
            with pool.Fori(0, ET) as t:
                pool.wait_ge(s["g_src_set"], t + 1)
                pool.sem_inc(s["waits_taken"], 1)
                pool.indirect_dma_start(out=g_parts, out_offset=None, in_=xn_table[:, :],
                                        in_offset=bass.IndirectOffsetOnAxis(ap=g_src, axis=0))\
                    .then_inc(s["g_loaded"], 16)
                pool.wait_ge(s["g_to_made"], t + 1)
                pool.wait_ge(s["g_taken"], t + 1)
                pool.sem_inc(s["waits_taken"], 1)
                pool.indirect_dma_start(out=sum_rows[:, :], out_offset=bass.IndirectOffsetOnAxis(ap=g_to, axis=0),
                                        in_=g_sum, in_offset=None, compute_op=ALU.add).then_inc(s["g_added"], 16)
                pool.wait_ge(s["g_added"], 16 * t + 16)
            with pool.Fori(0, GT - 1) as t:
                pool.dma_start(g_back, sum_rows[bass.ds(t * P, P), :]).then_inc(s["g_back_loaded"], 16)
                pool.wait_ge(s["g_split"], SPLITS * (t + 1))
                pool.dma_start(xn_table[bass.ds(t * P, P), :], g_out).then_inc(s["g_mean_stored"], 16)
                pool.wait_ge(s["g_mean_stored"], 16 * t + 16)
            n = N - (GT - 1) * P
            pool.dma_start(g_back, sum_rows[(GT - 1) * P:GT * P, :]).then_inc(s["g_back_loaded"], 16)
            pool.wait_ge(s["g_split"], SPLITS * GT)
            pool.dma_start(xn_table[(GT - 1) * P:N, :], g_out[0:n, :]).then_inc(s["g_mean_stored"], 16)
            pool.wait_ge(s["g_mean_stored"], 16 * GT)
            pool.wait_ge(s["g_replaced"], 1)
            pool.sem_inc(s["g_done"], 1)

        def general_pe(pe):
            with pe.Fori(0, ET) as t:
                pe.wait_ge(s["g_dsts_made"], t + 1)
                nc.tensor.transpose(pa[:, 0, 0:P], g_dsts, ident[:, :]).then_inc(s["g_turned"], 1)
                pe.wait_ge(s["g_same_made"], t + 1)
                pe.wait_ge(s["g_row_made"], t + 1)
                nc.tensor.matmul(pa[:, 1, 0:GW], g_same, g_row, start=True, stop=True).then_inc(s["g_summed"], 1)

        def general_dve(dve):
            V = nc.vector
            dve.wait_ge(s["g_iota"], 3)
            V.tensor_copy(g_dump, g_dump_i)
            V.memset(g_row[:, D:GW], 0.0).then_inc(s["g_consts"], 1)
            dve.wait_ge(s["g_consts"], 1)
            V.memset(g_row[:, D:D + 1], 1.0).then_inc(s["g_consts"], 1)
            dve.wait_ge(s["g_consts"], 2)
            with dve.Fori(0, ET) as t:
                V.tensor_tensor(g_dst, rel[:, bass.ds(t, 1)], offs[:, bass.ds(t, 1)], ALU.add)
                V.tensor_copy(g_src, idx[:, bass.ds(t, 1)]).then_inc(s["g_src_set"], 1)
                dve.wait_ge(s["g_src_set"], t + 1)
                V.tensor_copy(g_dsts, g_dst.to_broadcast([P, P])).then_inc(s["g_dsts_made"], 1)
                dve.wait_ge(s["g_turned"], t + 1)
                V.tensor_scalar(g_same, pa[:, 0, 0:P], g_dst, None, ALU.is_equal).then_inc(s["g_same_made"], 1)
                dve.wait_ge(s["g_same_made"], t + 1)
                dve.wait_ge(s["g_loaded"], 16 * t + 16)
                V.tensor_tensor(g_row[:, 0:D], g_parts[:, 0:D], g_parts[:, D:2 * D], ALU.add)\
                    .then_inc(s["g_row_made"], 1)
                V.tensor_tensor(g_before, g_same, g_later, ALU.mult)
                V.tensor_scalar(g_pad, g_dst, 0.0, None, ALU.is_lt)
                V.tensor_tensor(g_gap, g_dump, g_dst, ALU.subtract).then_inc(s["g_tests"], 1)
                dve.wait_ge(s["g_tests"], t + 1)
                V.tensor_reduce(g_dup, g_before, AX.X, ALU.max).then_inc(s["g_dup_made"], 1)
                dve.wait_ge(s["g_dup_made"], t + 1)
                V.tensor_tensor(g_dup2, g_dup, g_pad, ALU.max).then_inc(s["g_dup2_made"], 1)
                dve.wait_ge(s["g_dup2_made"], t + 1)
                V.scalar_tensor_tensor(out=g_to, in0=g_gap, scalar=g_dup2, in1=g_dst, op0=ALU.mult, op1=ALU.add)\
                    .then_inc(s["g_to_made"], 1)
                dve.wait_ge(s["g_summed"], t + 1)
                V.tensor_copy(g_sum, pa[:, 1, 0:GW]).then_inc(s["g_taken"], 1)
                dve.wait_ge(s["g_added"], 16 * t + 16)
            with dve.Fori(0, GT) as t:
                dve.wait_ge(s["g_back_loaded"], 16 * t + 16)
                V.tensor_scalar(g_cnt, g_back[:, D:D + 1], 1.0, None, ALU.max).then_inc(s["g_cnt_made"], 1)
                dve.wait_ge(s["g_cnt_made"], t + 1)
                V.reciprocal(g_cnt, g_cnt).then_inc(s["g_rec_made"], 1)
                dve.wait_ge(s["g_rec_made"], t + 1)
                V.tensor_scalar(g_mean, g_back[:, 0:D], g_cnt, None, ALU.mult).then_inc(s["g_mean_made"], 1)
                dve.wait_ge(s["g_mean_made"], t + 1)
                for n in range(PARTS):
                    part = g_out[:, n * D:(n + 1) * D]
                    V.tensor_copy(part, g_mean).then_inc(s["g_split"], 1)
                    dve.wait_ge(s["g_split"], SPLITS * t + 2 * n + 1)
                    if n < PARTS - 1:
                        V.tensor_tensor(g_mean, g_mean, part, ALU.subtract).then_inc(s["g_split"], 1)
                        dve.wait_ge(s["g_split"], SPLITS * t + 2 * n + 2)
                dve.wait_ge(s["g_mean_stored"], 16 * t + 16)
            idx3, rel3 = (v.rearrange("p (b k) -> p b k", k=TB) for v in (idx, rel))
            V.memset(idx, 0)
            V.memset(rel, -1.0)
            V.tensor_scalar(g_p, g_dump, float(GT * P), None, ALU.subtract)
            V.tensor_copy(g_node, g_node_i).then_inc(s["g_index"], 1)
            dve.wait_ge(s["g_index"], 1)
            V.tensor_scalar(idx3[:, :, TILE_A], g_node, N - 1.0, None, ALU.min)
            V.tensor_scalar(idx3[:, :, TILE_B], g_node, float(P), N - 1.0, ALU.add, ALU.min)
            V.tensor_scalar(idx3[:, :, TILE_C], g_node, float(P), N - 1.0, ALU.add, ALU.min)
            V.tensor_scalar(g_ra, g_p, P - 1.0, None, ALU.is_lt)
            V.tensor_scalar(g_rc, g_p, P - 1.0, BN - LO[TILE_C], ALU.is_equal, ALU.mult)
            V.tensor_scalar(g_rb, g_p, 2.0, None, ALU.add).then_inc(s["g_index"], 1)
            dve.wait_ge(s["g_index"], 2)
            V.tensor_scalar(g_rc, g_rc, -1.0, None, ALU.add)
            V.tensor_tensor(g_rb, g_rb, g_ra, ALU.mult).then_inc(s["g_index"], 1)
            dve.wait_ge(s["g_index"], 3)
            V.tensor_scalar(g_rb, g_rb, -1.0, None, ALU.add).then_inc(s["g_index"], 1)
            dve.wait_ge(s["g_index"], 4)
            for tile, v in ((TILE_A, g_p), (TILE_B, g_rb), (TILE_C, g_rc)):
                V.tensor_copy(rel3[:, :, tile], v.to_broadcast([P, NB]))
            V.tensor_copy(idxb[:, :], idx[:, 0:TB]).then_inc(s["g_replaced"], 1)
            dve.wait_ge(s["g_replaced"], 1)


        block = ctx.enter_context(nc.Block())

        @block.sync
        def _(sp):
            def edge_list(lst):
                full, rest = (NCH - 1) * P, ET - (NCH - 1) * P
                sp.dma_start(raw[:, 0:NCH - 1, :], lst[0:full * P].rearrange("(c p e) -> p c e", p=P, e=P))\
                    .then_inc(s["raw_loaded"], 16)
                sp.dma_start(raw[0:rest - 1, NCH - 1, :], lst[full * P:(ET - 1) * P].rearrange("(p e) -> p e", e=P))\
                    .then_inc(s["raw_loaded"], 16)
                sp.dma_start(raw[rest - 1:rest, NCH - 1, 0:E - (ET - 1) * P],
                             lst[(ET - 1) * P:E].rearrange("(a e) -> a e", a=1)).then_inc(s["raw_loaded"], 16)

            quad_io(sp, x, xin[0], 0, s["x_loaded0"], False)
            quad_io(sp, x, xin[1], 1, s["x_loaded1"], False)
            sp.wait_ge(s["raw_padded"], 1)
            edge_list(dst)
            for t, v in ((bl_b, b_l), (bo_b, bo), (gamma_b, gamma), (beta_b, beta)):
                sp.dma_start(t[:, :], v.partition_broadcast(P)).then_inc(s["biases_loaded"], 16)
            for t, v in ((bv_r, bv), (br_r, br)):
                sp.dma_start(t[:, :], v.rearrange("(a n) -> a n", a=1)).then_inc(s["biases_loaded"], 16)
            sp.dma_start(bq_c[:, :], bq.rearrange("(c p) -> p c", p=P), allow_slow_non_contiguous=True)\
                .then_inc(s["biases_loaded"], 16)

            def stage1(q, u):
                sp.wait_ge(s["xn_ready"], q + 1)
                if not (isinstance(q, int) and q + 2 > NQ):
                    quad_io(sp, x, xin[u], q + 2, s[f"x_loaded{u}"], False)
                if not is_int(q, 0):
                    store_parts(q - 1, 1 - u)

            def store_parts(q, u):
                sp.wait_ge(s["lo_made"], q + 1)
                quad_io(sp, xn_table, xp[u], q, s[f"xn_stored{u}"], True)

            def lists(q):
                if q == 1:
                    sp.wait_ge(s["raw_padded"], 2)
                    edge_list(src)
            over_quads(sp, stage1, LISTS, lists)
            store_parts(NQ, 0)

            if_general(sp, general_sp)

            block_io(sp, x, xr, 0, s["xr_loaded"], False)

            def stage3(b, u):
                d = b - 1
                if not is_int(b, 0):
                    sp.wait_ge(s["x1_made"], d + 1)
                    block_io(sp, x1_rows, x1, d, s["x1_stored"], True)
                if not (isinstance(b, int) and b >= NB - 1):
                    sp.wait_ge(s["r0_made"], b + 1)
                    block_io(sp, x, xr, b + 1, s["xr_loaded"], False)
                if not is_int(b, 0):
                    sp.wait_ge(s["y_made"], d + 1)
                    block_io(sp, y_rows, yr, d, s["y_stored"], True)
            over_blocks(sp, stage3)

            sp.wait_ge(s["picked"], 1)
            chosen = [sp.value_load(pick[0:1, n:n + 1], min_val=0, max_val=NE - 1) for n in range(2)]
            for n, e in enumerate(chosen):
                sp.dma_start(W1_s[:, n, :, :], W1[bass.ds(e, 1), :, :].rearrange("a (c p) f -> p (a c) f", p=P))\
                    .then_inc(s[f"w1_loaded{n}"], 16)
                sp.dma_start(b1_c[:, n, :], b1[bass.ds(e, 1), :].rearrange("a (c p) -> p (a c)", p=P),
                             allow_slow_non_contiguous=True)\
                    .then_inc(s[f"w1_loaded{n}"], 16)
                sp.dma_start(W2_s[:, n * FC:(n + 1) * FC, :],
                             W2[bass.ds(e, 1), :, :].rearrange("a (c p) d -> p (a c) d", p=P))\
                    .then_inc(s[f"w2_loaded{n}"], 16)
            for n, e in enumerate(chosen):
                sp.dma_start(b2_b[:, n, :], b2[bass.ds(e, 1), :].rearrange("a d -> (a d)").partition_broadcast(P))\
                    .then_inc(s["b2_loaded"], 16)
            sp.wait_ge(s["x1_stored"], block_dmas(NB - 1))
            sp.wait_ge(s["y_stored"], block_dmas(NB - 1))

            def stage5(q, u):
                if is_int(q, 0):
                    for v in range(2):
                        quad_io(sp, y_rows, y_in[v], v, s[f"yin_loaded{v}"], False)
                        quad_io(sp, x1_rows, x1_in[v], v, s[f"yin_loaded{v}"], False)
                sp.wait_ge(s["fin_made"], q + 1)
                quad_io(sp, out, x1_in[u], q, s[f"out_stored{u}"], True)
                if not (isinstance(q, int) and q + 2 > NQ):
                    quad_io(sp, y_rows, y_in[u], q + 2, s[f"yin_loaded{u}"], False)
                    sp.wait_ge(s[f"out_stored{u}"], quad_dmas(q, u))
                    quad_io(sp, x1_rows, x1_in[u], q + 2, s[f"yin_loaded{u}"], False)
            over_quads(sp, stage5)
            for u in range(2):
                sp.wait_ge(s[f"out_stored{u}"], quad_dmas(NQ - 1 + (u == 0), u))

        @block.gpsimd
        def _(pool):
            pool.iota(iota_i, pattern=[[1, WIN]], base=0, channel_multiplier=0).then_inc(s["iota_set"], 1)
            pool.memset(ident[:, :], 0.0).then_inc(s["ident_set"], 1)
            pool.wait_ge(s["ident_set"], 1)
            pool.affine_select(out=ident[:, :], in_=ident[:, :], compare_op=ALU.not_equal, fill=1.0, base=0,
                               pattern=[[-1, P]], channel_multiplier=1).then_inc(s["ident_set"], 1)
            for t, m in ((wq_s, wq), (wv_s, wv), (wo_s, wo), (wraw[0], W_l), (wraw[1], W_r), (Wr_s, Wr)):
                pool.dma_start(t[:, :, :], m.rearrange("(c p) n -> p c n", p=P)).then_inc(s["w_loaded"], 16)

            pool.iota(offs[:, :], pattern=[[BN, NB], [15, TB // 2], [7, 2]], base=LO[0], channel_multiplier=0)\
                .then_inc(s["iota_set"], 1)

            def stage1(q, u):
                pool.wait_ge(s["xn_ready"], q + 1)
                wait(pool, s["lo_made"], q)
                pool.sem_inc(s["waits_taken"], 1)
                for v, n in whole(q):
                    ins = pool.tensor_scalar(xs[0:n, v, :], xnb[u][0:n, v, 0:D], XS, None, ALU.mult)
                ins.then_inc(s["xs_made"], 1)
                pool.wait_ge(s["xs_made"], q + 1)
                pool.wait_ge(s["hi_made"], q + 1)
                for v, n in whole(q):
                    ins = pool.tensor_tensor(xp[u][0:n, v, D:2 * D], xs[0:n, v, :], xp[u][0:n, v, 0:D], ALU.subtract)
                ins.then_inc(s["lo_made"], 1)
            over_quads(pool, stage1, LISTS)

            pool.wait_ge(s["xn_stored0"], quad_dmas(NQ, 0))
            pool.wait_ge(s["xn_stored1"], quad_dmas(NQ - 1, 1))
            if_general(pool, general_pool)

            def stage3(b, u):
                if is_int(b, NB):
                    return
                for q in range(NBT):
                    if not batch_tiles(b, q):
                        continue
                    pool.wait_ge(s["idx_ready"], NBT * b + q + 1)
                    wait(pool, s["batch_used"], NBT * (b - 1) + q + 1)
                    pool.sem_inc(s["waits_taken"], 1)
                    for k in batch_tiles(b, q):
                        pool.indirect_dma_start(
                            out=msgs[:, k, :, :].rearrange("p s d -> p (s d)"), out_offset=None, in_=xn_table[:, :],
                            in_offset=bass.IndirectOffsetOnAxis(ap=idxb[:, k:k + 1], axis=0))\
                            .then_inc(s[f"gathered{q}"], 16)
            over_blocks(pool, stage3)

            def stage5(q, u):
                tail = is_int(q, NQ)
                n = len(TAILS) if tail else QT
                pool.wait_ge(s[f"yin_loaded{u}"], 2 * quad_dmas(q, u))
                if is_int(q, 0):
                    pool.wait_ge(s["b2_made"], 1)
                pool.tensor_tensor(y_in[u][:, 0:n, :], y_in[u][:, 0:n, :],
                                   b2m[:, :].unsqueeze(1).to_broadcast([P, n, D]), ALU.add).then_inc(s["yb_made"], 1)
                pool.tensor_tensor(x1_in[u][:, 0:n, :], x1_in[u][:, 0:n, :],
                                   beta_b[:, :].unsqueeze(1).to_broadcast([P, n, D]), ALU.add)\
                    .then_inc(s["xb_made"], 1)
                if not is_int(q, 0):
                    finish(q - 1, 1 - u)

            def finish(q, u):
                n = len(TAILS) if is_int(q, NQ) else QT
                pool.wait_ge(s["zn_made"], q + 1)
                pool.tensor_tensor(z[u][:, 0:n, :], z[u][:, 0:n, :],
                                   gamma_b[:, :].unsqueeze(1).to_broadcast([P, n, D]), ALU.mult)\
                    .then_inc(s["f_scaled"], 1)
                pool.wait_ge(s["f_scaled"], q + 1)
                pool.wait_ge(s["xb_made"], q + 1)
                pool.tensor_tensor(x1_in[u][:, 0:n, :], x1_in[u][:, 0:n, :], z[u][:, 0:n, :], ALU.add)\
                    .then_inc(s["fin_made"], 1)
            over_quads(pool, stage5)
            finish(NQ, 0)

        @block.scalar
        def _(act):
            def exp_keys(q, u):
                for pr in range(1 if is_int(q, NQ) else 2):
                    act.wait_ge(s["kb_made"], 2 * q + pr + 1)
                    nc.scalar.activation(ek[pr], kb1[pr], ACT.Exp, bias=minus1[:, :]).then_inc(s["ek_made"], 1)

            def normalise(q, u):
                tiles = list(enumerate(TAILS)) if is_int(q, NQ) else [(t, P) for t in range(QT)]
                act.wait_ge(s["p1_stats"], q + 1)
                if not (isinstance(q, int) and q < 2):
                    act.wait_ge(s["lo_made"], q - 1)
                    act.wait_ge(s["kx_done"], q - 1)
                for t, n in tiles:
                    col = q * QT + t
                    ins = nc.scalar.activation(xnb[u][0:n, t, 0:D], xin[u][0:n, t, :], ACT.Identity,
                                               bias=nmr_a[0:n, bass.ds(col, 1)], scale=rstd_a[0:n, bass.ds(col, 1)])
                ins.then_inc(s["xn_ready"], 1)

            def first_part(q, u):
                act.wait_ge(s["xn_ready"], q + 1)
                if not (isinstance(q, int) and q < 2):
                    act.wait_ge(s[f"xn_stored{u}"], quad_dmas(q - 2, u))
                for v, n in whole(q):
                    ins = nc.scalar.activation(xp[u][0:n, v, 0:D], xnb[u][0:n, v, 0:D], ACT.Copy, scale=XS)
                ins.then_inc(s["hi_made"], 1)

            def take_turned(q, u):
                act.wait_ge(s["xt_turned"], q + 1)
                w = TAIL if is_int(q, NQ) else QR
                nc.scalar.activation(xTb[u][:, :, 0:w], pd[:, 0:2, 0:w], ACT.Copy).then_inc(s["xt_made"], 1)

            def stage1(q, u):
                exp_keys(q, u)
                if not is_int(q, NQ):
                    take_turned(q + 1, 1 - u)
                if not (is_int(q, 0) or is_int(q, NQ - 1) or is_int(q, NQ)):
                    first_part(q + 1, 1 - u)
                if not (isinstance(q, int) and q + 2 > NQ):
                    normalise(q + 2, u)
                if is_int(q, NQ - 2):
                    first_part(NQ, u)

            def indices(b, q):
                ks = batch_tiles(b, q)
                if not ks:
                    return
                if not is_int(b, 0):
                    act.wait_ge(s[f"gathered{q}"], batch_gathers(b - 1, q))
                nc.scalar.activation(idxb[:, ks[0]:ks[-1] + 1], idx[:, bass.ds(b * TB + ks[0], len(ks))], ACT.Copy)\
                    .then_inc(s["idx_ready"], 1)

            def lists(q):
                if q == NQ - 1:
                    act.wait_ge(s["raw_taken"], 2 * NG)
                    for n in range(NBT):
                        indices(0, n)

            act.dma_start(wk_s[:, :, :], wk.rearrange("(c p) n -> p c n", p=P)).then_inc(s["wk_loaded"], 16)
            act.dma_start(b1k_b[:, :], bk.partition_broadcast(P)).then_inc(s["wk_loaded"], 16)
            act.wait_ge(s["consts_set"], 1)
            nc.scalar.activation(warm, minus1[:, :], ACT.Exp)
            normalise(0, 0)
            first_part(0, 0)
            take_turned(0, 0)
            normalise(1, 1)
            first_part(1, 1)
            over_quads(act, stage1, LISTS, lists)

            if_general(act, None)

            def block_tiles(d):
                return list(enumerate(TAILS)) if is_int(d, NB - 1) else [(0, P), (1, P)]

            def block_xn(b):
                act.wait_ge(s["xr_loaded"], block_dmas(b))
                wait(act, s["r0_made"], b)
                for t, n in block_tiles(b):
                    col = b * 2 + t
                    ins = nc.scalar.activation(xn2[0:n, t * D:(t + 1) * D], xr[0:n, t * D:(t + 1) * D], ACT.Identity,
                                               bias=nmr_a[0:n, bass.ds(col, 1)], scale=rstd_a[0:n, bass.ds(col, 1)])
                ins.then_inc(s["xn2_ready"], 1)

            def block_xnT(b):
                act.wait_ge(s["xt2_turned"], b + 1)
                w = TAIL if is_int(b, NB - 1) else BN
                nc.scalar.activation(pair(xT2)[:, :, 0:w], pair(pd[:, 0, :])[:, :, 0:w], ACT.Copy)\
                    .then_inc(s["xt2_ready"], 1)

            def block_queries(b):
                act.wait_ge(s["q_made"], b + 1)
                wait(act, s["qhat_made"], b)
                wait(act, s["o_made"], b)
                for c in range(C):
                    nc.scalar.activation(pq[:, c * BN:(c + 1) * BN], pd[:, 1, c * BN:(c + 1) * BN], ACT.Exp,
                                         bias=bq_c[:, c:c + 1])
                for c in range(C):
                    ins = nc.scalar.activation(qb[:, c * BN:(c + 1) * BN], pd[:, 1, c * BN:(c + 1) * BN],
                                               ACT.Identity, bias=bq1_c[:, c:c + 1])
                ins.then_inc(s["eq_made"], 1)

            def block_y(d):
                act.wait_ge(s["d_stats"], d + 1)
                wait(act, s["y_stored"], 16 * d)
                wait(act, s["yt_turned"], d)
                for t, n in block_tiles(d):
                    ins = nc.scalar.activation(yr[0:n, t * D:(t + 1) * D], x1[0:n, t * D:(t + 1) * D], ACT.Identity,
                                               bias=nmr2[0:n, t:t + 1], scale=rstd2[0:n, t:t + 1])
                ins.then_inc(s["y_made"], 1)

            def block_yT(d):
                act.wait_ge(s["yt_turned"], d + 1)
                w = TAIL if is_int(d, NB - 1) else BN
                for c in range(C):
                    ins = nc.scalar.activation(yT[:, bass.ds(d * C * BN + c * BN, w)], pd[:, 1, c * BN:c * BN + w],
                                               ACT.Copy, accum_out=ysum[:, c, bass.ds(d, 1)])
                ins.then_inc(s["yt_ready"], 1)

            def stage3(b, u):
                more = not (isinstance(b, int) and b + 1 >= NB)
                if not is_int(b, NB):
                    block_xn(b)
                    for q in range(2 if more else 0):
                        indices(b + 1, q)
                    block_xnT(b)
                    block_queries(b)
                if not is_int(b, 0):
                    block_y(b - 1)
                    for q in range(2, 4 if more else 0):
                        indices(b + 1, q)
                    block_yT(b - 1)
                for q in range(2 if is_int(b, 0) else 4, NBT if more else 0):
                    indices(b + 1, q)
            over_blocks(act, stage3)

            act.wait_ge(s["route_step"], ROUTE_EXP[0])
            nc.scalar.activation(rt[:, R_E1, :], rt[:, R_LG, :], ACT.Exp, bias=rt[:, R_MX1, 0:1],
                                 accum_out=rt[:, R_S1, 0:1]).then_inc(s["route_exp"], 1)
            act.wait_ge(s["route_step"], ROUTE_EXP[1])
            nc.scalar.activation(rt[:, R_E2, :], rt[:, R_RW, :], ACT.Exp, bias=rt[:, R_MX2, 0:1],
                                 accum_out=rt[:, R_S2, 0:1]).then_inc(s["route_exp"], 1)
            act.wait_ge(s["route_step"], ROUTE_EXP[2])
            nc.scalar.activation(rt[:, R_G, 1:2], rt[:, R_M, 2:3], ACT.Exp).then_inc(s["route_exp"], 1)

            def split_y(q, u):
                for out, v in y_quad(y_hi[u], q):
                    ins = nc.scalar.activation(out, v, ACT.Copy)
                ins.then_inc(s["yh_made"], 1)

            def hidden(q, f):
                w = TAIL if is_int(q, NQ) else QR
                act.wait_ge(s["h_made"], NF * q + f + 1)
                wait(act, s["hl_made"], NF * q + f - 1)
                nc.scalar.activation(h_full[f % 2][:, 0:w], hbank(f)[:, 0:w], ACT.Gelu,
                                     bias=b1_c[:, f // FC, f % FC:f % FC + 1]).then_inc(s["h_act"], 1)
                act.wait_ge(s["h_act"], NF * q + f + 1)
                if f == HS - 1:
                    wait(act, s["o5_made"], 2 * q)
                else:
                    wait(act, s["l2_done"], l2_chunks(q, f - HS))
                nc.scalar.activation(h_hi[f % HS][:, 0:w], h_full[f % 2][:, 0:w], ACT.Copy).then_inc(s["hh_made"], 1)

            act.wait_ge(s["logits_made"], 1)
            nc.scalar.activation(mean_c[:, 0:1], minus1[:, :], ACT.Gelu)
            split_y(0, 0)
            for e in range(2):
                act.wait_ge(s[f"w1_loaded{e}"], 32)
                nc.scalar.activation(W1_hi[:, e, :, :], W1_s[:, e, :, :], ACT.Copy).then_inc(s["w1_hi_made"], 1)

            def normalise_z(q, u):
                act.wait_ge(s["f_stats"], q + 1)
                for t, n in (enumerate(TAILS) if is_int(q, NQ) else [(t, P) for t in range(QT)]):
                    ins = nc.scalar.activation(z[u][0:n, t, :], z[u][0:n, t, :], ACT.Identity,
                                               bias=nmr2[0:n, t:t + 1], scale=rstd2[0:n, t:t + 1])
                ins.then_inc(s["zn_made"], 1)

            def stage5(q, u):
                for f in range(NF):
                    hidden(q, f)
                    if f == 1 and not is_int(q, NQ):
                        split_y(q + 1, 1 - u)
                    if f == 5 and not is_int(q, 0):
                        normalise_z(q - 1, 1 - u)
            over_quads(act, stage5)
            normalise_z(NQ, 0)

        @block.tensor
        def _(pe):
            mm = nc.tensor.matmul

            def add_keys(q, u):
                tiles = list(enumerate(TAILS)) if is_int(q, NQ) else [(t, P) for t in range(QT)]
                for t, n in tiles:
                    if t % 2 == 0:
                        pe.wait_ge(s["phi_made"], 2 * q + t // 2 + 1)
                    for c in range(C):
                        ins = mm(pc[:, c, 0:KXW], phi[0:n, t, c * P:(c + 1) * P], xnb[u][0:n, t, :],
                                 start=is_int(q, 0) and t == 0, stop=is_int(q, NQ) and t == len(TAILS) - 1)
                ins.then_inc(s["kx_done"], 1)

            def stage1(q, u):
                tiles = list(enumerate(TAILS)) if is_int(q, NQ) else [(t, P) for t in range(QT)]
                pe.wait_ge(s["xn_ready"], q + 1)
                for t, n in tiles:
                    for c in range(C):
                        ins = nc.tensor.transpose(pd[:, c, t * P:t * P + n], xnb[u][0:n, t, c * P:(c + 1) * P],
                                                  ident[0:n, 0:n])
                ins.then_inc(s["xt_turned"], 1)
                if not is_int(q, 0):
                    add_keys(q - 1, 1 - u)
                else:
                    pe.wait_ge(s["wk_loaded"], 32)
                pe.wait_ge(s["xt_made"], q + 1)
                for pr in range(len(tiles) // 2):
                    for t, n in tiles[2 * pr:2 * pr + 2]:
                        for c in range(C):
                            ins = mm(pd[0:n, 2 + pr, (t % 2) * D:(t % 2 + 1) * D], xTb[u][:, c, t * P:t * P + n],
                                     wk_s[:, c, :], start=c == 0, stop=c == C - 1)
                    ins.then_inc(s["k_made"], 1)

            def turn_list(n, groups):
                pe.wait_ge(s["raw_float"], n + 1)
                for g in groups:
                    wait(pe, s["raw_taken"], NG * n + g - 1)
                    for c in range(4 * g, min(4 * g + 4, NCH)):
                        ins = nc.tensor.transpose(pa[:, g % 2, (c % 4) * P:(c % 4 + 1) * P], rawf[:, c, :],
                                                  ident[:, :])
                    ins.then_inc(s["raw_turned"], 1)

            def lists(q):
                if 1 <= q <= 4:
                    turn_list((q - 1) // 2, range(NG // 2) if q % 2 else range(NG // 2, NG))
                if q == 5:
                    pe.wait_ge(s["raw_taken"], 2 * NG)
                    pe.wait_ge(s["w_loaded"], W_LOADS)
                    pe.wait_ge(s["biases_loaded"], B_LOADS)
                    for n in range(2):
                        for o in range(C):
                            for c in range(C):
                                ins = nc.tensor.transpose(pa[:, n, c * D + o * P:c * D + (o + 1) * P],
                                                          wraw[n][:, o, c * P:(c + 1) * P], ident[:, :])
                    ins.then_inc(s["wlr_turned"], 1)
                if q == NQ - 1:
                    pe.wait_ge(s["flag_sum"], 1)
                    pe.wait_ge(s["wlr_taken"], 1)
                    mm(pa[0:1, 0, 0:1], cntp[:, 0:1], ones[:, 0:1], start=True, stop=True).then_inc(s["flag_added"], 1)

            pe.wait_ge(s["ident_set"], 2)
            pe.wait_ge(s["consts_set"], 1)
            over_quads(pe, stage1, LISTS, lists)
            add_keys(NQ, 0)

            pe.wait_ge(s["kx_taken"], 1)
            for c in range(C):
                for fc in range(C):
                    nc.tensor.transpose(pd[:, 0, fc * D + c * P:fc * D + (c + 1) * P],
                                        kx_s[:, c, fc * P:(fc + 1) * P], ident[:, :])
                ins = nc.tensor.transpose(pd[0:1, 1, c * P:(c + 1) * P], kx_s[:, c, D:D + 1], ident[:, :])
            ins.then_inc(s["kxT_made"], 1)
            pe.wait_ge(s["kxT_taken"], 1)
            for c in range(C):
                o = pd[:, 2, c * P:(c + 1) * P]
                for fc in range(C):
                    mm(o, wv_s[:, fc, c * P:(c + 1) * P], kxT[:, fc, c * P:(c + 1) * P], start=fc == 0, stop=False)
                ins = mm(o, bv_r[0:1, c * P:(c + 1) * P], ks_r[0:1, c * P:(c + 1) * P], start=False, stop=True)
            ins.then_inc(s["kv_made"], 1)
            pe.wait_ge(s["kv_taken"], 1)
            for c in range(C):
                ins = mm(pd[:, 3, c * D:(c + 1) * D], kvT[:, c, :], wo_s[:, c, :], start=True, stop=True)
            ins.then_inc(s["m_made"], 1)
            if_general(pe, general_pe)
            pe.wait_ge(s["m_taken"], 1)

            def turn_xn(d):
                pe.wait_ge(s["xn2_ready"], d + 1)
                wait(pe, s["nrm_eps"], d)
                for h in range(2):
                    n = TAILS[h] if is_int(d, NB - 1) else P
                    for c in range(C):
                        ins = nc.tensor.transpose(pd[:, 0, c * BN + h * P:c * BN + h * P + n],
                                                  xn2[0:n, h * D + c * P:h * D + (c + 1) * P], ident[0:n, 0:n])
                ins.then_inc(s["xt2_turned"], 1)

            def queries(d):
                pe.wait_ge(s["xt2_ready"], d + 1)
                wait(pe, s["yt_ready"], d - 1)
                for o in range(C):
                    for c in range(C):
                        ins = mm(pd[:, 1, o * BN:(o + 1) * BN], wq_s[:, c, o * P:(o + 1) * P],
                                 xT2[:, c * BN:(c + 1) * BN], start=c == 0, stop=c == C - 1)
                ins.then_inc(s["q_made"], 1)

            def normalizers(d):
                pe.wait_ge(s["phq_made"], d + 1)
                for c in range(C):
                    ins = mm(pd[:, 0, c * BN:(c + 1) * BN], KS_s[:, c, :], pq[:, c * BN:(c + 1) * BN],
                             start=True, stop=True)
                ins.then_inc(s["nrm_made"], 1)

            def products(d):
                wait(pe, s["x1_made"], d)
                for a, w, at in ((xT2, wrT, 0), (pq, M_s, D), (aggS, wlT, 0)):
                    if a is pq:
                        pe.wait_ge(s["qhat_made"], d + 1)
                    if a is aggS:
                        pe.wait_ge(s["agg_taken"], d + 1)
                    for h in range(2):
                        for c in range(C):
                            ins = mm(pd[:, 2 + h, at:at + D], a[:, c * BN + h * P:c * BN + (h + 1) * P], w[:, c, :],
                                     start=a is xT2 and c == 0, stop=a is not xT2 and c == C - 1,
                                     skip_group_check=True)
                ins.then_inc(s["o_made"], 1)

            def turn_y(d):
                pe.wait_ge(s["y_made"], d + 1)
                if not is_int(d, NB - 1):
                    pe.wait_ge(s["eq_made"], d + 2)
                for h in range(2):
                    n = TAILS[h] if is_int(d, NB - 1) else P
                    for c in range(C):
                        ins = nc.tensor.transpose(pd[:, 1, c * BN + h * P:c * BN + h * P + n],
                                                  yr[0:n, h * D + c * P:h * D + (c + 1) * P], ident[0:n, 0:n])
                ins.then_inc(s["yt_turned"], 1)

            HOOKS = ((11, products, 1), (11, turn_xn, 0), (13, queries, 0), (22, normalizers, 0), (26, turn_y, 1))

            def stage3(b, u):
                if is_int(b, NB):
                    products(b - 1)
                    turn_y(b - 1)
                    return
                last_block = is_int(b, NB - 1)
                for q in range(NBT):
                    ks = batch_tiles(b, q)
                    for k in ks:
                        for at_tile, work, back in HOOKS:
                            if k == at_tile and not (back and is_int(b, 0)):
                                work(b - back)
                        if k == ks[0]:
                            pe.wait_ge(s["oh_ready"], NBT * b + q + 1)
                            pe.wait_ge(s[f"gathered{q}"], batch_gathers(b, q))
                        slot = k % SLOTS
                        parts = []
                        for db in (-1, 0, 1):
                            c0, c1 = max(LO[k], db * BN), min(LO[k] + WIN, (db + 1) * BN)
                            if c0 < c1 and not (db < 0 and is_int(b, 0)) and not (db > 0 and last_block):
                                parts.append((db, c0 - db * BN, c1 - db * BN, c0 - LO[k]))
                        for db, c0, c1, o0 in parts:
                            v = (u + db) % 2
                            first = (db == 1 and LO[k - 1] + WIN <= BN) or (is_int(b, 0) and k == 0)
                            if db == 1 and first:
                                wait(pe, s["agg_taken"], b)
                            closing = (db == -1 and LO[k + 1] >= 0) or (last_block and k == LAST - 1)
                            o1 = o0 + c1 - c0
                            for c in range(C):
                                for part in range(PARTS):
                                    mm(pa[:, v, c * BN + c0:c * BN + c1], msgs[:, k, part, c * P:(c + 1) * P],
                                       oh[:, slot, o0:o1], start=first and c == 0 and part == 0, stop=closing,
                                       skip_group_check=True)
                            ins = mm(pc[:, v, c0:c1], ones_h[:, :], oh[:, slot, o0:o1], start=first, stop=closing,
                                     skip_group_check=True)
                            if closing:
                                ins.then_inc(s["agg_done"], 1)
                    if ks and not (last_block and ks[-1] == LAST - 1):
                        ins.then_inc(s["batch_used"], 1)
            over_blocks(pe, stage3)

            pe.wait_ge(s["mean_made"], 1)
            for c in range(C):
                ins = mm(pd[0:1, 0, 0:NE], mean_c[:, c:c + 1], Wr_s[:, c, :], start=c == 0, stop=c == C - 1)
            ins.then_inc(s["logits_made"], 1)
            pe.wait_ge(s["gates_made"], 1)
            mm(pd[:, 1, 0:2], ones[0:1, :], gates[0:1, :], start=True, stop=True).then_inc(s["gates_spread"], 1)

            def layer1(q, u, f):
                w = TAIL if is_int(q, NQ) else QR
                e, fc = divmod(f, FC)
                if f == 0:
                    pe.wait_ge(s["yl_made"], q + 1)
                if is_int(q, 0):
                    pe.wait_ge(s["w1_split"], e + 1)
                wait(pe, s["h_act"], NF * q + f - 3)
                for c in range(C):
                    for wp, yp in ((W1_hi, y_hi), (W1_hi, y_lo), (W1_lo, y_hi)):
                        ins = mm(hbank(f)[:, 0:w], wp[:, e, c, fc * P:(fc + 1) * P], yp[u][:, c, 0:w],
                                 start=c == 0 and wp is W1_hi and yp is y_hi, stop=c == C - 1 and wp is W1_lo)
                ins.then_inc(s["h_made"], 1)

            def layer2(q, u, f):
                pe.wait_ge(s["hl_made"], NF * q + f + 1)
                if is_int(q, 0):
                    pe.wait_ge(s["w2_split"], f // FC + 1)
                if f == 0:
                    wait(pe, s["z_made"], 2 * q - 2)
                tiles = list(enumerate(TAILS)) if is_int(q, NQ) else [(t, P) for t in range(QT)]
                hh, hl = h_hi[f % HS], h_lo[f % HS]
                for t, n in tiles:
                    for hp, wp in ((hh, W2_hi), (hh, W2_lo), (hl, W2_hi)):
                        ins = mm(pd[0:n, 2 * u + t // 2, (t % 2) * D:(t % 2 + 1) * D], hp[:, t * P:t * P + n],
                                 wp[:, f, :], start=f == 0 and t % 2 == 0 and hp is hh and wp is W2_hi,
                                 stop=f == NF - 1 and hp is hl, skip_group_check=True)
                    if f == NF - 1 and t % 2:
                        ins.then_inc(s["o5_made"], 1)
                if f < NF - 1:
                    ins.then_inc(s["l2_done"], 1)

            LAG = 2
            pe.wait_ge(s["gates_taken"], 1)

            def stage5(q, u):
                for f in range(NF):
                    layer1(q, u, f)
                    if f >= LAG:
                        layer2(q, u, f - LAG)
                    elif not is_int(q, 0):
                        layer2(q - 1, 1 - u, f - LAG + NF)
            over_quads(pe, stage5)
            for f in range(NF - LAG, NF):
                layer2(NQ, 0, f)

        @block.vector
        def _(dve):
            V = nc.vector

            V.memset(minus1[:, :], -1.0)
            V.memset(ones_h[:, :], 1.0)
            V.memset(zeros[:, :], 0.0)
            V.memset(mv[:, :, :], 1.0)
            V.memset(mask, 0.0)
            V.memset(rel[:, NCH * P:TCOLS], -1.0)
            V.memset(idx[:, NCH * P:TCOLS], 0)
            for u in range(2):
                V.memset(xnb[u][:, :, D:KXW], 1.0)
            V.memset(ones[:, :], 1.0).then_inc(s["mask_step"], 1)
            dve.wait_ge(s["mask_step"], 1)
            for h in range(P // HD):
                ins = V.memset(mask[h * HD:(h + 1) * HD, h * HD:(h + 1) * HD], 1.0)
            ins.then_inc(s["consts_set"], 1)
            V.memset(raw[:, NCH - 1, :], -(1 << 20)).then_inc(s["raw_padded"], 1)

            def row_stats(tiles, bn, m, r, done, value, rs, nm, fill=()):
                wait(dve, s[done], value - 1)
                for t, (v, n) in enumerate(tiles):
                    ins = V.bn_stats(bst[0:n, t, :], v)
                ins.then_inc(s[bn], 1)
                dve.wait_ge(s[bn], value)
                dve.sem_inc(s["waits_taken"], 1)
                for t, (v, n) in enumerate(tiles):
                    ins = V.bn_aggr(mv[0:n, t, :], bst[0:n, t, :])
                ins.then_inc(s[m], 1)
                dve.wait_ge(s[m], value)
                k = len(tiles)
                v, h, ys, yi = nv[:, 0:k], nh[:, 0:k], rs, ny[:, 0:k]
                chain, count = [RSQRT_STEPS * (value - 1)], [0]

                def then(ins):
                    chain[0] = chain[0] + 1
                    count[0] += 1
                    ins.then_inc(s[r], 1)
                    for at_step, work in fill:
                        if at_step == count[0]:
                            work()
                    dve.wait_ge(s[r], chain[0])
                then(V.tensor_scalar(v, mv[:, 0:k, 1], EPS, None, ALU.add))
                then(V.tensor_scalar(h.bitcast(I32), v.bitcast(I32), 1, None, ALU.logical_shift_right))
                then(V.tensor_scalar(yi.bitcast(I32), h.bitcast(I32), -1.0, float(0x5F3759DF), ALU.mult, ALU.add))
                for n in range(NEWTON):
                    then(V.tensor_tensor(h, yi, yi, ALU.mult))
                    then(V.scalar_tensor_tensor(out=h, in0=h, scalar=-0.5, in1=v, op0=ALU.mult, op1=ALU.mult))
                    then(V.scalar_tensor_tensor(out=ys if n == NEWTON - 1 else yi, in0=h, scalar=1.5, in1=yi,
                                                op0=ALU.add, op1=ALU.mult))
                V.scalar_tensor_tensor(out=nm, in0=mv[:, 0:k, 0], scalar=-1.0, in1=rs, op0=ALU.mult, op1=ALU.mult)\
                    .then_inc(s[done], 1)

            def add_bias(q, pr):
                if pr == 0:
                    wait(dve, s["phi_made"], 2 * q)
                dve.wait_ge(s["k_made"], 2 * q + pr + 1)
                V.tensor_tensor(pair(kb1[pr]), pair(pd[:, 2 + pr, :]), bc(b1k_b[:, :], 2), ALU.add)\
                    .then_inc(s["kb_made"], 1)

            def feature(q, pr):
                dve.wait_ge(s["ek_made"], 2 * q + pr + 1)
                V.scalar_tensor_tensor(out=phi[:, 2 * pr:2 * pr + 2, :], in0=pair(ek[pr]), scalar=1.0,
                                       in1=pair(kb1[pr]), op0=ALU.min, op1=ALU.max).then_inc(s["phi_made"], 1)

            def quad_stats(q, u, fill=()):
                tiles = list(enumerate(TAILS)) if is_int(q, NQ) else [(t, P) for t in range(QT)]
                dve.wait_ge(s[f"x_loaded{u}"], quad_dmas(q, u))
                row_stats([(xin[u][0:n, t, :], n) for t, n in tiles], "p1_bn", "p1_mv", "p1_rstd", "p1_stats", q + 1,
                          rstd_a[:, bass.ds(q * QT, len(tiles))], nmr_a[:, bass.ds(q * QT, len(tiles))], fill)

            def stage1(q, u):
                def second_pair():
                    feature(q, 0)
                    add_bias(q, 1)
                if is_int(q, 0):
                    dve.wait_ge(s["bias1_set"], 1)
                if not (isinstance(q, int) and q + 2 > NQ):
                    quad_stats(q + 2, u, [(RSQRT_STEPS - 3, lambda: add_bias(q, 0)), (RSQRT_STEPS, second_pair)])
                    feature(q, 1)
                elif q < NQ:
                    add_bias(q, 0)
                    second_pair()
                    feature(q, 1)
                else:
                    add_bias(q, 0)
                    feature(q, 0)

            def float_list(n):
                dve.wait_ge(s["raw_loaded"], 48 * (n + 1))
                V.tensor_copy(rawf, raw).then_inc(s["raw_float"], 1)
                if n == 0:
                    dve.wait_ge(s["raw_float"], 1)
                    V.memset(raw[:, NCH - 1, :], 0).then_inc(s["raw_padded"], 1)

            def take_list(n, groups):
                if n == 0:
                    dve.wait_ge(s["iota_set"], 2)
                for g in groups:
                    w = min(4, NCH - 4 * g) * P
                    cols = slice(4 * g * P, 4 * g * P + w)
                    dve.wait_ge(s["raw_turned"], NG * n + g + 1)
                    if n == 0:
                        ins = V.tensor_tensor(rel[:, cols], pa[:, g % 2, 0:w], offs[:, cols], ALU.subtract)
                    else:
                        ins = V.tensor_copy(idx[:, cols], pa[:, g % 2, 0:w])
                    ins.then_inc(s["raw_taken"], 1)

            def lists(q):
                if q == 0:
                    float_list(0)
                if 1 <= q <= 4:
                    take_list((q - 1) // 2, range(NG // 2) if q % 2 else range(NG // 2, NG))
                if q == 2:
                    float_list(1)
                if q == 5:
                    dve.wait_ge(s["wlr_turned"], 1)
                    V.tensor_copy(wlT[:, :, :], pair(pa[:, 0, :]))
                    V.tensor_copy(wrT[:, :, :], pair(pa[:, 1, :])).then_inc(s["wlr_taken"], 1)
                    V.tensor_scalar(bq1_c[:, :], bq_c[:, :], 1.0, None, ALU.add)
                    dve.wait_ge(s["raw_taken"], 2 * NG)
                    dve.wait_ge(s["raw_float"], 2)
                    V.tensor_scalar(inside[0], rel, 0.0, None, ALU.is_ge).then_inc(s["flag_a"], 1)
                if q == NQ - 2:
                    dve.wait_ge(s["flag_a"], 1)
                    V.scalar_tensor_tensor(out=inside[1], in0=rel, scalar=WIN - 1.0, in1=inside[0], op0=ALU.is_le,
                                           op1=ALU.mult).then_inc(s["flag_b"], 1)
                    dve.wait_ge(s["flag_b"], 1)
                    V.tensor_reduce(cntp[:, :], inside[1], AX.X, ALU.add).then_inc(s["flag_sum"], 1)
                if q == NQ - 1:
                    dve.wait_ge(s["flag_added"], 1)
                    V.tensor_scalar(flag[:, :], pa[0:1, 0, 0:1], float(E), None, ALU.is_lt).then_inc(s["flag_set"], 1)
            quad_stats(0, 0)
            quad_stats(1, 1)
            dve.wait_ge(s["iota_set"], 1)
            V.tensor_copy(iota_f[:, :], iota_i).then_inc(s["iota_float"], 1)
            dve.wait_ge(s["wk_loaded"], 32)
            V.tensor_scalar(b1k_b[:, :], b1k_b[:, :], 1.0, None, ALU.add).then_inc(s["bias1_set"], 1)
            over_quads(dve, stage1, LISTS, lists)

            dve.wait_ge(s["kx_done"], NQ + 1)
            V.tensor_copy(kx_s, pc[:, :, 0:KXW]).then_inc(s["kx_taken"], 1)
            dve.wait_ge(s["kx_taken"], 1)
            for c in range(C):
                V.tensor_scalar(KS_s[:, c, :], mask, kx_s[:, c, D:D + 1], None, ALU.mult)
            dve.wait_ge(s["kxT_made"], 1)
            V.tensor_copy(kxT, pair(pd[:, 0, :]))
            V.tensor_copy(ks_r, pd[0:1, 1, 0:D]).then_inc(s["kxT_taken"], 1)
            dve.wait_ge(s["kv_made"], 1)
            V.tensor_tensor(kvT, pair(pd[:, 2, 0:C * P]), bc(mask, 2), ALU.mult).then_inc(s["kv_taken"], 1)
            dve.wait_ge(s["m_made"], 1)
            V.tensor_copy(M_s[:, :, :], pair(pd[:, 3, :])).then_inc(s["m_taken"], 1)
            if_general(dve, general_dve)
            dve.wait_ge(s["iota_float"], 1)
            dve.wait_ge(s["raw_taken"], 2 * NG)
            dve.wait_ge(s["p1_stats"], NQ + 1)

            def one_hots(b, q):
                ks = batch_tiles(b, q)
                if not ks:
                    return
                wait(dve, s["batch_used"], NBT * b + q - NBT // 2 + 1)
                m, slot = len(ks), ks[0] % SLOTS
                where = rel[:, bass.ds(b * TB + ks[0], m)].unsqueeze(2).to_broadcast([P, m, WIN])
                V.tensor_tensor(oh[:, slot:slot + m, :], bc(iota_f[:, :], m), where, ALU.is_equal)\
                    .then_inc(s["oh_ready"], 1)

            def neighbours(d, u):
                dve.wait_ge(s["agg_done"], d + 1)
                wait(dve, s["o_made"], d)
                wait(dve, s["x1_made"], d)
                wait(dve, s["agg_taken"], d)
                V.tensor_scalar(rc[:, :], pc[:, u, 0:BN], 1.0, XS, ALU.max, ALU.mult).then_inc(s["cnt_max"], 1)
                dve.wait_ge(s["cnt_max"], d + 1)
                V.reciprocal(rc[:, :], rc[:, :]).then_inc(s["cnt_rec"], 1)
                dve.wait_ge(s["cnt_rec"], d + 1)
                V.tensor_tensor(pair(aggS), pair(pa[:, u, :]), bc(rc[:, :], 2), ALU.mult)\
                    .then_inc(s["agg_taken"], 1)

            def middle(d):
                dve.wait_ge(s["o_made"], d + 1)
                V.tensor_tensor(pair(aggS), pd[:, 2:4, 0:D], bc(bl_b[:, :], 2), ALU.add).then_inc(s["g1_made"], 1)
                dve.wait_ge(s["g1_made"], d + 1)
                dve.wait_ge(s["r0b_made"], d + 1)
                V.scalar_tensor_tensor(out=aggS, in0=aggS, scalar=0.0, in1=r0, op0=ALU.max, op1=ALU.add)\
                    .then_inc(s["x1a_made"], 1)
                dve.wait_ge(s["x1a_made"], d + 1)
                wait(dve, s["x1_stored"], 16 * d)
                wait(dve, s["y_made"], d)
                V.tensor_tensor(pair(x1), pair(aggS), pd[:, 2:4, D:2 * D], ALU.add).then_inc(s["x1_made"], 1)

            def middle_stats(d):
                dve.wait_ge(s["x1_made"], d + 1)
                rows = TAILS if is_int(d, NB - 1) else [P, P]
                row_stats([(x1[0:n, t * D:(t + 1) * D], n) for t, n in enumerate(rows)],
                          "d_bn", "d_mv", "d_rstd", "d_stats", d + 1, rstd2[:, 0:2], nmr2[:, 0:2])

            def residual(b):
                dve.wait_ge(s["xn2_ready"], b + 1)
                wait(dve, s["x1a_made"], b)
                V.tensor_tensor(r0, xr, xn2, ALU.add).then_inc(s["r0_made"], 1)
                dve.wait_ge(s["r0_made"], b + 1)
                V.tensor_tensor(pair(r0), pair(r0), bc(bo_b[:, :], 2), ALU.add).then_inc(s["r0b_made"], 1)

            def query_features(b):
                dve.wait_ge(s["eq_made"], b + 1)
                V.scalar_tensor_tensor(out=pq, in0=pq, scalar=1.0, in1=qb, op0=ALU.min, op1=ALU.max)\
                    .then_inc(s["phq_made"], 1)

            def normalise_queries(b):
                dve.wait_ge(s["nrm_made"], b + 1)
                V.tensor_scalar(qb, pd[:, 0, :], 1e-6, None, ALU.add).then_inc(s["nrm_eps"], 1)
                dve.wait_ge(s["nrm_eps"], b + 1)
                V.reciprocal(qb, qb).then_inc(s["nrm_rec"], 1)
                dve.wait_ge(s["nrm_rec"], b + 1)
                V.tensor_tensor(pq, pq, qb, ALU.mult).then_inc(s["qhat_made"], 1)

            def stage3(b, u):
                d = b - 1
                if is_int(b, NB):
                    neighbours(d, 1 - u)
                    middle(d)
                    middle_stats(d)
                    return
                for q in range(NBT // 2):
                    one_hots(b, q)
                if not is_int(b, 0):
                    neighbours(d, 1 - u)
                one_hots(b, 4)
                one_hots(b, 5)
                if not is_int(b, 0):
                    middle(d)
                residual(b)
                if not is_int(b, 0):
                    middle_stats(d)
                one_hots(b, 6)
                query_features(b)
                one_hots(b, 7)
                normalise_queries(b)
            over_blocks(dve, stage3)

            dve.wait_ge(s["yt_ready"], NB)
            V.tensor_reduce(ysr[:, :], ysum[:, :, :], AX.X, ALU.add).then_inc(s["ysum_made"], 1)
            dve.wait_ge(s["ysum_made"], 1)
            V.tensor_scalar(mean_c[:, :], ysr[:, :], 1.0 / N, None, ALU.mult).then_inc(s["mean_made"], 1)
            V.tensor_copy(rt[:, R_IO, :], iota_f[0:1, 0:NE])
            steps = [0]

            def step(ins):
                steps[0] += 1
                ins.then_inc(s["route_step"], 1)
                dve.wait_ge(s["route_step"], steps[0])

            def row(n, w=NE, at=0):
                return rt[:, n, at:at + w]
            dve.wait_ge(s["logits_made"], 1)
            step(V.tensor_tensor(row(R_LG), pd[0:1, 0, 0:NE], br_r[:, :], ALU.add))
            step(V.tensor_reduce(row(R_MX1, 1), row(R_LG), AX.X, ALU.max))
            step(V.tensor_scalar(row(R_MX1, 1), row(R_MX1, 1), -1.0, None, ALU.mult))
            assert steps[0] == ROUTE_EXP[0]
            dve.wait_ge(s["route_exp"], 1)
            step(V.reciprocal(row(R_S1, 1), row(R_S1, 1)))
            step(V.tensor_scalar(row(R_RW), row(R_E1), row(R_S1, 1), CAP / N, ALU.mult, ALU.min))
            step(V.tensor_reduce(row(R_MX2, 1), row(R_RW), AX.X, ALU.max))
            step(V.tensor_scalar(row(R_MX2, 1), row(R_MX2, 1), -1.0, None, ALU.mult))
            assert steps[0] == ROUTE_EXP[1]
            dve.wait_ge(s["route_exp"], 2)
            step(V.reciprocal(row(R_S2, 1), row(R_S2, 1)))
            step(V.tensor_scalar(row(R_W), row(R_E2), row(R_S2, 1), None, ALU.mult))
            step(V.tensor_reduce(row(R_M, 1), row(R_W), AX.X, ALU.max))

            def first_at(values, largest, n):
                step(V.tensor_scalar(row(R_T), values, largest, float(NE), ALU.is_lt, ALU.mult))
                step(V.tensor_tensor(row(R_U), row(R_T), row(R_IO), ALU.add))
                step(V.tensor_reduce(row(R_I, 1, n), row(R_U), AX.X, ALU.min))
            first_at(row(R_W), row(R_M, 1), 0)
            step(V.tensor_scalar(row(R_T), row(R_IO), row(R_I, 1), -2.0, ALU.is_equal, ALU.mult))
            step(V.tensor_tensor(row(R_W2), row(R_W), row(R_T), ALU.add))
            step(V.tensor_reduce(row(R_M, 1, 1), row(R_W2), AX.X, ALU.max))
            first_at(row(R_W2), row(R_M, 1, 1), 1)
            step(V.tensor_tensor(row(R_M, 1, 2), row(R_M, 1, 1), row(R_M, 1, 0), ALU.subtract))
            V.tensor_copy(pick[:, :], row(R_I, 2)).then_inc(s["picked"], 1)
            step(V.tensor_scalar(row(R_G, 1, 2), row(R_M, 1, 2), 1.0, None, ALU.mult))
            assert steps[0] == ROUTE_EXP[2]
            dve.wait_ge(s["route_exp"], 3)
            step(V.tensor_scalar(row(R_G, 1), row(R_G, 1, 1), 1.0, None, ALU.add))
            step(V.reciprocal(gates[:, 0:1], row(R_G, 1)))
            V.tensor_tensor(gates[:, 1:2], gates[:, 0:1], row(R_G, 1, 1), ALU.mult).then_inc(s["gates_made"], 1)
            dve.wait_ge(s["gates_spread"], 1)
            V.tensor_copy(gate_b[:, :], pd[:, 1, 0:2]).then_inc(s["gates_taken"], 1)
            dve.wait_ge(s["gates_taken"], 1)

            def split_y(q, u):
                dve.wait_ge(s["yh_made"], q + 1)
                for (out, v), (hi, _) in zip(y_quad(y_lo[u], q), y_quad(y_hi[u], q)):
                    ins = V.tensor_tensor(out, v, hi, ALU.subtract)
                ins.then_inc(s["yl_made"], 1)

            split_y(0, 0)

            def split_w1(e):
                dve.wait_ge(s["w1_hi_made"], e + 1)
                V.tensor_tensor(W1_lo[:, e, :, :], W1_s[:, e, :, :], W1_hi[:, e, :, :], ALU.subtract)\
                    .then_inc(s["w1_split"], 1)

            def split_w2(e):
                dve.wait_ge(s[f"w2_loaded{e}"], 16)
                fs = slice(e * FC, (e + 1) * FC)
                V.tensor_scalar(W2_hi[:, fs, :], W2_s[:, fs, :], gate_b[:, e:e + 1], None, ALU.mult)\
                    .then_inc(s["w2_hi_made"], 1)
                dve.wait_ge(s["w2_hi_made"], e + 1)
                V.scalar_tensor_tensor(out=W2_lo[:, fs, :], in0=W2_s[:, fs, :], scalar=gate_b[:, e:e + 1],
                                       in1=W2_hi[:, fs, :], op0=ALU.mult, op1=ALU.subtract).then_inc(s["w2_split"], 1)

            def mix_b2():
                dve.wait_ge(s["b2_loaded"], 32)
                V.tensor_scalar(b2a, b2_b[:, 0, :], gate_b[:, 0:1], None, ALU.mult).then_inc(s["b2_step"], 1)
                dve.wait_ge(s["b2_step"], 1)
                V.scalar_tensor_tensor(out=b2m, in0=b2_b[:, 1, :], scalar=gate_b[:, 1:2], in1=b2a, op0=ALU.mult,
                                       op1=ALU.add).then_inc(s["b2_made"], 1)
            split_w1(0)
            split_w2(0)

            def hidden(q, f):
                w = TAIL if is_int(q, NQ) else QR
                dve.wait_ge(s["hh_made"], NF * q + f + 1)
                V.tensor_tensor(h_lo[f % HS][:, 0:w], h_full[f % 2][:, 0:w], h_hi[f % HS][:, 0:w], ALU.subtract)\
                    .then_inc(s["hl_made"], 1)

            def tiles_of(q):
                return list(enumerate(TAILS)) if is_int(q, NQ) else [(t, P) for t in range(QT)]

            def add_y(q, u):
                dve.wait_ge(s["yb_made"], q + 1)
                wait(dve, s["fin_made"], q - 1)
                pairs = len(tiles_of(q)) // 2
                for pr in range(pairs):
                    dve.wait_ge(s["o5_made"], 2 * q + pr + 1)
                    V.tensor_tensor(z[u][:, 2 * pr:2 * pr + 2, :], pair(pd[:, 2 * u + pr, :]),
                                    y_in[u][:, 2 * pr:2 * pr + 2, :], ALU.add).then_inc(s["z_made"], 1)

            def stats_z(q, u):
                tiles = tiles_of(q)
                dve.wait_ge(s["z_made"], 2 * q + len(tiles) // 2)
                wait(dve, s["zn_made"], q)
                row_stats([(z[u][0:n, t, :], n) for t, n in tiles], "f_bn", "f_mv", "f_rstd", "f_stats", q + 1,
                          rstd2[:, 0:len(tiles)], nmr2[:, 0:len(tiles)])

            def stage5(q, u):
                for f in range(NF):
                    hidden(q, f)
                    if is_int(q, 0) and f < 3:
                        (lambda: split_w1(1), lambda: split_w2(1), mix_b2)[f]()
                    if f == 1 and not is_int(q, 0):
                        add_y(q - 1, 1 - u)
                    if f == 2 and not is_int(q, 0):
                        stats_z(q - 1, 1 - u)
                    if f == 4 and not is_int(q, NQ):
                        split_y(q + 1, 1 - u)
            over_quads(dve, stage5)
            add_y(NQ, 0)
            stats_z(NQ, 0)


_INS = ["x", "src", "dst", "L0_gnn_W_l", "L0_gnn_b_l", "L0_gnn_W_r", "L0_mix_wq", "L0_mix_bq", "L0_mix_wk", "L0_mix_bk",
        "L0_mix_wv", "L0_mix_bv", "L0_mix_wo", "L0_mix_bo", "L0_ffn_Wr", "L0_ffn_br", "L0_ffn_W1", "L0_ffn_b1",
        "L0_ffn_W2", "L0_ffn_b2", "L0_ffn_gamma", "L0_ffn_beta"]


def kernel(**inputs):
    import numpy as np
    import concourse.bacc as bacc
    from concourse.bass_utils import run_bass_kernel_spmd

    nc = bacc.Bacc("TRN2", target_bir_lowering=False, num_devices=1)
    arrays, args = {}, []
    for name in _INS:
        a = np.ascontiguousarray(inputs[name])
        arrays[f"in_{name}"] = a
        args.append(nc.dram_tensor(f"in_{name}", a.shape, mybir.dt.from_np(a.dtype), kind="ExternalInput").ap())
    out = nc.dram_tensor("out", inputs["x"].shape, F32, kind="ExternalOutput").ap()
    build_layer(nc, *args, out)
    r = run_bass_kernel_spmd(nc, [arrays], core_ids=[0])
    return r.results[0]["out"]
```
